# Optimizing a Trainium2 kernel written in Bass

```python
import numpy as np
import jax
import jax.numpy as jnp

def _softmax(x, axis=-1):
    return jax.nn.softmax(x, axis=axis)

def _gelu(x):
    return jax.nn.gelu(x, approximate=True)

def _silu(x):
    return jax.nn.silu(x)

def _sigmoid(x):
    return jax.nn.sigmoid(x)

def _layernorm(x, axis=-1, eps=1e-05):
    m = jnp.mean(x, axis=axis, keepdims=True)
    v = jnp.var(x, axis=axis, keepdims=True)
    return (x - m) / jnp.sqrt(v + eps)

def _scatter_add(tgt, idx, src, axis=0):
    return tgt.at[idx].add(src)

def _segment_sum(src, seg, n):
    return jax.ops.segment_sum(src, seg, n)
kernel_name = 'mk_conv_attn_hybrid_d2_conv_nhwc256_r2_7d3bbb'

def setup_inputs(seed: int=0):
    np.random.seed(seed)
    _w = jnp.asarray

    def _rec_inputs():
        import jax
        import jax.numpy as jnp
        _gk = jax.random.key(seed)
        x = -0.0002928 + 1 * jax.random.normal(jax.random.fold_in(_gk, 1), (4, 32, 32, 128), jnp.float32)
        return x
    x = _rec_inputs()

    def _L0_conv_setup():
        import jax, jax.numpy as jnp
        import numpy as np
        from jax import lax
        N, H, W, C = (4, 32, 32, 128)
        G, K = (8, 3)
        Cg = C // G
        PAD, STRIDE, DIL = (1, 1, 1)
        OFFSET_SCALE = 1.0
        P = K * K

        def _bilinear_sample(img, grid):
            B, Cc, Hi, Wi = img.shape
            x = ((grid[..., 0] + 1.0) * Wi - 1.0) * 0.5
            y = ((grid[..., 1] + 1.0) * Hi - 1.0) * 0.5
            x0 = jnp.floor(x)
            y0 = jnp.floor(y)
            fx = x - x0
            fy = y - y0
            x0i = x0.astype(jnp.int32)
            y0i = y0.astype(jnp.int32)
            flat = img.reshape(B, Cc, Hi * Wi)
            gather = jax.vmap(lambda f, i: f[:, i])

            def corner(xc, yc, w):
                valid = (xc >= 0) & (xc < Wi) & (yc >= 0) & (yc < Hi)
                idx = jnp.clip(yc, 0, Hi - 1) * Wi + jnp.clip(xc, 0, Wi - 1)
                return gather(flat, idx) * (w * valid)[:, None]
            out = corner(x0i, y0i, (1.0 - fx) * (1.0 - fy))
            out = out + corner(x0i + 1, y0i, fx * (1.0 - fy))
            out = out + corner(x0i, y0i + 1, (1.0 - fx) * fy)
            out = out + corner(x0i + 1, y0i + 1, fx * fy)
            return out
        key = jax.random.key(seed)
        ks = jax.random.split(key, 12)
        s = 1.0 / np.sqrt(C)
        return {'x': jax.random.normal(ks[0], (N, H, W, C), jnp.float32), 'in_w': jax.random.normal(ks[1], (C, C), jnp.float32) * s, 'in_b': jnp.zeros((C,), jnp.float32), 'out_w': jax.random.normal(ks[2], (C, C), jnp.float32) * s, 'out_b': jnp.zeros((C,), jnp.float32), 'off_w': jax.random.normal(ks[3], (C, G * P * 2), jnp.float32) * 0.02, 'off_b': jax.random.normal(ks[4], (G * P * 2,), jnp.float32) * 0.1, 'mask_w': jax.random.normal(ks[5], (C, G * P), jnp.float32) * 0.02, 'mask_b': jnp.zeros((G * P,), jnp.float32), 'dw_k': jax.random.normal(ks[6], (C, 1, K, K), jnp.float32) * (1.0 / K), 'bn_g': 1.0 + 0.1 * jax.random.normal(ks[7], (C,), jnp.float32), 'bn_b': 0.1 * jax.random.normal(ks[8], (C,), jnp.float32), 'bn_m': 0.1 * jax.random.normal(ks[9], (C,), jnp.float32), 'bn_v': 1.0 + 0.1 * jax.random.uniform(ks[10], (C,), jnp.float32)}
    _L0_conv_all = _L0_conv_setup()
    _L0_conv_in = {k: v for k, v in _L0_conv_all.items() if k in ('in_w', 'in_b', 'out_w', 'out_b', 'off_w', 'off_b', 'mask_w', 'mask_b', 'dw_k', 'bn_g', 'bn_b', 'bn_m', 'bn_v')}
    del _L0_conv_all

    def _L1_attn_setup():
        import jax, jax.numpy as jnp
        import numpy as np
        key = jax.random.key(seed)
        k1, k2 = jax.random.split(key)
        B, N, F = (4, 2048, 128)
        nodes = jax.random.normal(k1, (B, N, F), dtype=jnp.float32)
        limit = np.sqrt(6.0 / (F + F)).astype(np.float32)
        W = jax.random.uniform(k2, (F, F), dtype=jnp.float32, minval=-limit, maxval=limit)
        return {'nodes': nodes, 'W': W}
    _L1_attn_all = _L1_attn_setup()
    _L1_attn_in = {k: v for k, v in _L1_attn_all.items() if k in ('W',)}
    del _L1_attn_all

    def _L1_ffn_setup():
        import math
        import jax, jax.numpy as jnp
        import numpy as np
        CAPACITY_FACTOR = 1.25
        TOP_K = 2
        LN_EPS = 1e-05

        def _layer_norm(x, gamma, beta):
            mu = jnp.mean(x, axis=-1, keepdims=True)
            var = jnp.var(x, axis=-1, keepdims=True)
            return (x - mu) * jax.lax.rsqrt(var + LN_EPS) * gamma + beta
        key = jax.random.key(seed)
        ks = jax.random.split(key, 4)
        B, S, D, F, E = (8, 2048, 128, 256, 8)
        x = jax.random.normal(ks[0], (B, S, D), dtype=jnp.float32)
        Wr = jax.random.normal(ks[1], (D, E), dtype=jnp.float32) / np.sqrt(D)
        br = jnp.zeros((E,), jnp.float32)
        W1 = jax.random.normal(ks[2], (E, D, F), dtype=jnp.float32) / np.sqrt(D)
        b1 = jnp.zeros((E, F), jnp.float32)
        W2 = jax.random.normal(ks[3], (E, F, D), dtype=jnp.float32) / np.sqrt(F)
        b2 = jnp.zeros((E, D), jnp.float32)
        gamma = jnp.ones((D,), jnp.float32)
        beta = jnp.zeros((D,), jnp.float32)
        return {'x': x, 'Wr': Wr, 'br': br, 'W1': W1, 'b1': b1, 'W2': W2, 'b2': b2, 'gamma': gamma, 'beta': beta}
    _L1_ffn_all = _L1_ffn_setup()
    _L1_ffn_in = {k: v for k, v in _L1_ffn_all.items() if k in ('Wr', 'br', 'W1', 'b1', 'W2', 'b2', 'gamma', 'beta')}
    del _L1_ffn_all
    return {'x': x, 'L0_conv_in_w': _L0_conv_in['in_w'], 'L0_conv_in_b': _L0_conv_in['in_b'], 'L0_conv_out_w': _L0_conv_in['out_w'], 'L0_conv_out_b': _L0_conv_in['out_b'], 'L0_conv_off_w': _L0_conv_in['off_w'], 'L0_conv_off_b': _L0_conv_in['off_b'], 'L0_conv_mask_w': _L0_conv_in['mask_w'], 'L0_conv_mask_b': _L0_conv_in['mask_b'], 'L0_conv_dw_k': _L0_conv_in['dw_k'], 'L0_conv_bn_g': _L0_conv_in['bn_g'], 'L0_conv_bn_b': _L0_conv_in['bn_b'], 'L0_conv_bn_m': _L0_conv_in['bn_m'], 'L0_conv_bn_v': _L0_conv_in['bn_v'], 'L1_attn_W': _L1_attn_in['W'], 'L1_ffn_Wr': _L1_ffn_in['Wr'], 'L1_ffn_br': _L1_ffn_in['br'], 'L1_ffn_W1': _L1_ffn_in['W1'], 'L1_ffn_b1': _L1_ffn_in['b1'], 'L1_ffn_W2': _L1_ffn_in['W2'], 'L1_ffn_b2': _L1_ffn_in['b2'], 'L1_ffn_gamma': _L1_ffn_in['gamma'], 'L1_ffn_beta': _L1_ffn_in['beta']}

def reference(x, L0_conv_in_w, L0_conv_in_b, L0_conv_out_w, L0_conv_out_b, L0_conv_off_w, L0_conv_off_b, L0_conv_mask_w, L0_conv_mask_b, L0_conv_dw_k, L0_conv_bn_g, L0_conv_bn_b, L0_conv_bn_m, L0_conv_bn_v, L1_attn_W, L1_ffn_Wr, L1_ffn_br, L1_ffn_W1, L1_ffn_b1, L1_ffn_W2, L1_ffn_b2, L1_ffn_gamma, L1_ffn_beta):
    import jax
    import jax.numpy as jnp

    def _L0_conv_ref(x, in_w, in_b, out_w, out_b, off_w, off_b, mask_w, mask_b, dw_k, bn_g, bn_b, bn_m, bn_v):
        import jax, jax.numpy as jnp
        import numpy as np
        from jax import lax
        N, H, W, C = (4, 32, 32, 128)
        G, K = (8, 3)
        Cg = C // G
        PAD, STRIDE, DIL = (1, 1, 1)
        OFFSET_SCALE = 1.0
        P = K * K

        def _bilinear_sample(img, grid):
            B, Cc, Hi, Wi = img.shape
            x = ((grid[..., 0] + 1.0) * Wi - 1.0) * 0.5
            y = ((grid[..., 1] + 1.0) * Hi - 1.0) * 0.5
            x0 = jnp.floor(x)
            y0 = jnp.floor(y)
            fx = x - x0
            fy = y - y0
            x0i = x0.astype(jnp.int32)
            y0i = y0.astype(jnp.int32)
            flat = img.reshape(B, Cc, Hi * Wi)
            gather = jax.vmap(lambda f, i: f[:, i])

            def corner(xc, yc, w):
                valid = (xc >= 0) & (xc < Wi) & (yc >= 0) & (yc < Hi)
                idx = jnp.clip(yc, 0, Hi - 1) * Wi + jnp.clip(xc, 0, Wi - 1)
                return gather(flat, idx) * (w * valid)[:, None]
            out = corner(x0i, y0i, (1.0 - fx) * (1.0 - fy))
            out = out + corner(x0i + 1, y0i, fx * (1.0 - fy))
            out = out + corner(x0i, y0i + 1, (1.0 - fx) * fy)
            out = out + corner(x0i + 1, y0i + 1, fx * fy)
            return out
        xp = x @ in_w + in_b
        x1 = jnp.transpose(x, (0, 3, 1, 2))
        x1 = lax.conv_general_dilated(x1, dw_k, (1, 1), [(PAD, PAD), (PAD, PAD)], feature_group_count=C)
        x1 = bn_g[:, None, None] * (x1 - bn_m[:, None, None]) * lax.rsqrt(bn_v + 1e-05)[:, None, None] + bn_b[:, None, None]
        x1 = jax.nn.silu(x1)
        x1 = jnp.transpose(x1, (0, 2, 3, 1))
        offset = x1 @ off_w + off_b
        mask = jax.nn.softmax((x1 @ mask_w + mask_b).reshape(N, H, W, G, P), -1)
        Hi, Wi = (H + 2 * PAD, W + 2 * PAD)
        xpad = jnp.pad(xp, ((0, 0), (PAD, PAD), (PAD, PAD), (0, 0)))
        base = DIL * (K - 1) // 2 + 0.5
        ref_y = (base + jnp.arange(H, dtype=jnp.float32) * STRIDE) / Hi
        ref_x = (base + jnp.arange(W, dtype=jnp.float32) * STRIDE) / Wi
        ref = jnp.stack(jnp.meshgrid(ref_x, ref_y, indexing='xy'), -1)
        g1 = jnp.arange(K, dtype=jnp.float32) * DIL - DIL * (K - 1) // 2
        gx = jnp.repeat(g1 / Wi, K)
        gy = jnp.tile(g1 / Hi, K)
        grid = jnp.stack([gx, gy], -1)
        norm = jnp.array([Wi, Hi], jnp.float32)
        loc = ref[None, :, :, None, None, :] + grid[None, None, None, None, :, :] * OFFSET_SCALE + offset.reshape(N, H, W, G, P, 2) * (OFFSET_SCALE / norm)
        sgrid = 2.0 * loc - 1.0
        img = xpad.reshape(N, Hi * Wi, G, Cg).transpose(0, 2, 3, 1).reshape(N * G, Cg, Hi, Wi)
        sg = sgrid.reshape(N, H * W, G, P, 2).transpose(0, 2, 1, 3, 4).reshape(N * G, H * W, P, 2)
        samples = _bilinear_sample(img, sg)
        m = mask.reshape(N, H * W, G, P).transpose(0, 2, 1, 3).reshape(N * G, 1, H * W, P)
        out = (samples * m).sum(-1)
        out = out.reshape(N, C, H * W).transpose(0, 2, 1).reshape(N, H, W, C)
        return out @ out_w + out_b

    def _L1_attn_ref(nodes, W):
        import jax, jax.numpy as jnp
        import numpy as np
        F = nodes.shape[-1]
        norm_const = 1.0 / jnp.sqrt(jnp.asarray(F, dtype=nodes.dtype))
        x = jnp.einsum('bnf,fg->bng', nodes, W)
        prods = jnp.einsum('bnf,bmf->bnm', x, nodes)
        att_scores = jax.nn.softmax(prods * norm_const, axis=-1)
        messgs = jnp.einsum('bnm,bmf->bnf', att_scores, nodes)
        return messgs

    def _L1_ffn_ref(x, Wr, br, W1, b1, W2, b2, gamma, beta):
        import math
        import jax, jax.numpy as jnp
        import numpy as np
        CAPACITY_FACTOR = 1.25
        TOP_K = 2
        LN_EPS = 1e-05

        def _layer_norm(x, gamma, beta):
            mu = jnp.mean(x, axis=-1, keepdims=True)
            var = jnp.var(x, axis=-1, keepdims=True)
            return (x - mu) * jax.lax.rsqrt(var + LN_EPS) * gamma + beta
        B, S, D = x.shape
        E = Wr.shape[1]
        N = B * S
        K = TOP_K
        logits = jnp.mean(x, axis=1) @ Wr + br
        routing_weights = jax.nn.softmax(logits, axis=-1)
        capacity = float(math.ceil(N * CAPACITY_FACTOR / E))
        expected_loads = routing_weights.sum(axis=0) * (N / B)
        scale = jnp.where(expected_loads > capacity, capacity / expected_loads, 1.0)
        routing_weights = jax.nn.softmax(routing_weights * scale, axis=-1)
        rw_tok = jnp.broadcast_to(routing_weights[:, None, :], (B, S, E)).reshape(N, E)
        top_w, top_i = jax.lax.top_k(rw_tok, K)
        top_w = jax.nn.softmax(top_w, axis=-1)
        xf = x.reshape(N, D)
        h = jax.nn.gelu(jnp.einsum('nd,edf->enf', xf, W1) + b1[:, None, :], approximate=False)
        y = jnp.einsum('enf,efd->end', h, W2) + b2[:, None, :]
        w_dense = jnp.zeros((N, E), x.dtype).at[jnp.arange(N)[:, None], top_i].add(top_w)
        out = jnp.einsum('ne,end->nd', w_dense, y).reshape(B, S, D)
        out = _layer_norm(out + x, gamma, beta)
        return out

    def _gn(v, G=32, eps=1e-05):
        B_, H_, W_, C_ = v.shape
        g = v.reshape(B_, H_, W_, G, C_ // G)
        m = jnp.mean(g, axis=(1, 2, 4), keepdims=True)
        s = jnp.var(g, axis=(1, 2, 4), keepdims=True)
        return ((g - m) / jnp.sqrt(s + eps)).reshape(v.shape)

    def _ln_c(v, eps=1e-06):
        m = jnp.mean(v, axis=-1, keepdims=True)
        s = jnp.var(v, axis=-1, keepdims=True)
        return (v - m) / jnp.sqrt(s + eps)

    def _ln_t(v, eps=1e-05):
        m = jnp.mean(v, axis=-1, keepdims=True)
        s = jnp.var(v, axis=-1, keepdims=True)
        return (v - m) / jnp.sqrt(s + eps)

    def _to_tokens(v):
        B_, H_, W_, C_ = v.shape
        return v.reshape(B_, H_ * W_, C_)

    def _from_tokens(t, like):
        return t.reshape(like.shape)
    x = x + _L0_conv_ref(_gn(x), L0_conv_in_w, L0_conv_in_b, L0_conv_out_w, L0_conv_out_b, L0_conv_off_w, L0_conv_off_b, L0_conv_mask_w, L0_conv_mask_b, L0_conv_dw_k, L0_conv_bn_g, L0_conv_bn_b, L0_conv_bn_m, L0_conv_bn_v)
    t = _to_tokens(x)
    t = t + _L1_attn_ref(_ln_t(t), L1_attn_W)
    t = t + _L1_ffn_ref(_ln_t(t), L1_ffn_Wr, L1_ffn_br, L1_ffn_W1, L1_ffn_b1, L1_ffn_W2, L1_ffn_b2, L1_ffn_gamma, L1_ffn_beta)
    x = _from_tokens(t, x)
    return x

_drawn_inputs = setup_inputs


def setup_inputs(seed=0):
    import zlib

    import numpy as np

    out = dict(_drawn_inputs(seed))
    spreads = {'L0_conv_in_b': (0.0, 0.1),
     'L0_conv_out_b': (0.0, 0.1),
     'L1_ffn_br': (0.0, 0.1),
     'L1_ffn_b1': (0.0, 0.359),
     'L1_ffn_b2': (0.0, 0.1),
     'L1_ffn_gamma': (1.0, 0.2),
     'L1_ffn_beta': (0.0, 0.1)}
    factors = {'L0_conv_bn_g': 5.856, 'L0_conv_bn_b': 6.427, 'L0_conv_bn_m': 6.304, 'L0_conv_bn_v': 8.0}
    for name, (base, spread) in spreads.items():
        noise = np.random.default_rng([zlib.crc32(name.encode()), seed]).standard_normal(out[name].shape)
        drawn = base * np.exp(spread * noise) if base else spread * noise
        out[name] = jnp.asarray(drawn.astype(out[name].dtype))
    for name, factor in factors.items():
        out[name] = (out[name] * factor).astype(out[name].dtype)
    return out
```

```python
from contextlib import ExitStack

import concourse.bass as bass
from concourse import mybir

ALU = mybir.AluOpType
ACT = mybir.ActivationFunctionType
AX = mybir.AxisListType
F32 = mybir.dt.float32
I32 = mybir.dt.int32
U32 = mybir.dt.uint32

B, H, W, C = 4, 32, 32, 128
P = 128
G, PTS = 8, 9
CG = C // G
GP = G * PTS
REACH = 2
TAPS = 2 * REACH + 1
WIN = TAPS + 2
PAD = WIN // 2
HP, WP = H + 2 * PAD, W + 2 * PAD
ROWS = 4
CHUNKS = H // ROWS
CT = ROWS * P
TOK = H * W
TILES = TOK // P
HALF = CHUNKS // 2
SLOTS = ROWS * (HALF - 1) + ROWS + WIN - 1
STENCIL = WIN * WIN
PROD = 7
E = 8
FF = 256
FH = FF // P
CAPACITY = -(-B * TOK * 5 // (4 * E))
GN_EPS = BN_EPS = LN_EPS = 1e-5
GN_C = 4
SEGS = [0, 10, 20, 30, 40, STENCIL]
BIG_SHIFT = 4.0


class Own:

    def __init__(self, eng, sem):
        self.eng, self.sem, self.base, self.n, self.alone = eng, sem, 0, 0, None

    def __call__(self, ins):
        ins.then_inc(self.sem, 1)
        self.n += 1
        return ins

    def wait(self):
        self.eng.wait_ge(self.sem, self.base + self.n)
        if self.alone is not None:
            self.eng.sem_inc(self.alone, 1)

    def link(self, ins):
        self(ins)
        self.wait()

    def enter(self, i, per, at=None):
        self.saved = self.n if at is None else at
        self.base, self.n, self.per = i * per + self.saved, 0, per

    def leave(self, turns):
        assert self.n == self.per, (self.n, self.per)
        self.base, self.n = 0, self.saved + turns * self.per


def hybrid_block_kernel(nc, x, in_w, in_b, out_w, out_b, off_w, off_b, mask_w, mask_b, dw_k, bn_g, bn_b,
                        bn_m, bn_v, attn_w, wr, br, w1, b1, w2, b2, gamma, beta, out):
    padded = nc.dram_tensor("padded", (B, WP, HP, C), F32, kind="Internal").ap()
    with ExitStack() as ctx:
        def sb(name, shape, dt=F32):
            return ctx.enter_context(nc.sbuf_tensor(name, shape, dt))

        def sem(name):
            return ctx.enter_context(nc.semaphore(name))

        bank = [ctx.enter_context(nc.psum_tensor(f"bank{i}", [P, 512], F32)) for i in range(4)]
        pair = [ctx.enter_context(nc.psum_tensor(f"pair{i}", [P, 1024], F32)) for i in range(2)]

        res = sb("res", [P, B * TILES, C])
        stage = sb("stage", [P, H, C])
        shifted = sb("shifted", [P, WIN, SLOTS * G, CG])
        xg = sb("xg", [P, HP - 4, B, W + 2])
        xg_rows = xg[:, :, :, :].rearrange("c y n w -> c (y n) w")

        ident = sb("ident", [P, P])
        ones = sb("ones", [P, P])
        group_mean = sb("group_mean", [P, P])
        in_w_sb = sb("in_w_sb", [P, C])
        out_w_sb = sb("out_w_sb", [P, C])
        off_raw = sb("off_raw", [P, 2 * GP])
        offmask_w = sb("offmask_w", [P, 3 * GP])
        attn_w_sb = sb("attn_w_sb", [P, C])
        wr_sb = sb("wr_sb", [P, E])
        b2_sb = sb("b2_sb", [E, C])
        bias_rows = sb("bias_rows", [1, 4, C])
        bias_all = sb("bias_all", [P, 4, C])
        off_b_raw = sb("off_b_raw", [1, 2 * GP])
        offmask_b = sb("offmask_b", [1, 3 * GP])
        br_sb = sb("br_sb", [1, E])
        dw_sb = sb("dw_sb", [P, 9])
        bn_sb = sb("bn_sb", [P, 4])
        bn_fold = sb("bn_fold", [P, 4])
        neg_half = sb("neg_half", [P, 32])
        tap_bias = sb("tap_bias", [P, TAPS + 1])
        cols4 = sb("cols4", [4, 4, P])
        zero_rows = sb("zero_rows", [P, 3 * C])

        gn_stats = sb("gn_stats", [P, B, 2, 6])
        gn_mv = sb("gn_mv", [P, B, 2])
        gn_v = sb("gn_v", [P, 4, B])

        conv = sb("conv", [P, ROWS * B, W])
        gate = sb("gate", [P, CT])
        x1 = gate
        off = sb("off", [P, ROWS, 3 * GP])
        far = sb("far", [P, ROWS * GP])
        row_max = sb("row_max", [P, ROWS * G])
        row_sum = sb("row_sum", [P, ROWS * G])
        mask = sb("mask", [P, ROWS * G, PTS])
        mask_near = sb("mask_near", [P, ROWS * GP])
        mask_far = sb("mask_far", [P, ROWS * GP])
        hats = sb("hats", [P, 2, ROWS * GP, TAPS])
        outer = sb("outer", [P, ROWS * G, TAPS, TAPS])
        far_xy = outer[:, :, :, :].rearrange("p g a b -> p (g a b)")[:, 0:ROWS * 2 * GP] \
            .rearrange("p (r o) -> p r o", r=ROWS)
        stencil = sb("stencil", [P, ROWS * G, WIN, WIN])
        prod = sb("prod", [P, PROD, ROWS * G, CG])
        samp = sb("samp", [P, CT])
        samp_t = sb("samp_t", [P, B, ROWS, W])
        far_count = sb("far_count", [1, ROWS * GP], I32)
        far_rows_f = sb("far_rows_f", [1, ROWS])
        far_rows = sb("far_rows", [1, ROWS], I32)

        grid = sb("grid", [P, 2 * GP])
        grid_i = sb("grid_i", [P, 2 * GP], I32)
        part_i = sb("part_i", [P, 1], I32)
        part_f = sb("part_f", [P, 1])
        cell0 = sb("cell0", [P, GP])
        pos = sb("pos", [P, 2 * GP])
        low = sb("low", [P, 2 * GP])
        low_i = sb("low_i", [P, 2 * GP], I32)
        over = sb("over", [P, 2 * GP])
        frac = sb("frac", [P, 2, 2 * GP])
        corner = sb("corner", [P, 2, 2 * GP])
        inside = sb("inside", [P, 2, 2 * GP])
        far_m = sb("far_m", [P, GP])
        cell_f = sb("cell_f", [P, GP])
        cells = sb("cells", [P, GP, 4])
        cell_w = sb("cell_w", [P, GP, 4])
        cell_t = sb("cell_t", [P, GP])
        cell_now = sb("cell_now", [P, 4], U32)
        w_now = sb("w_now", [P, 4])
        got = sb("got", [P, 4, CG])
        fix = sb("fix", [P, ROWS * G, CG])

        over_shifted = shifted[:, :, :, :].rearrange("p d s c -> p (d s c)")
        at = [0]

        def reuse(n):
            at[0] += n
            assert at[0] <= WIN * SLOTS * C
            return over_shifted[:, at[0] - n:at[0]]

        normed = reuse(B * TOK).rearrange("p (t c) -> p t c", c=C)
        normed_t = reuse(B * TOK).rearrange("p (n t) -> p n t", n=B)
        keyed = reuse(B * TOK).rearrange("p (n t) -> p n t", n=B)
        probs = reuse(2 * TOK).rearrange("p (s t) -> p s t", s=2)
        probs_t = reuse(TOK)
        hidden = reuse(2 * 4 * 512).rearrange("p (s f t) -> p s f t", s=2, f=4)
        w1_sel = stage[:, 0:16, :].rearrange("p (s f) c -> p s (f c)", s=8)
        w2_sel = stage[:, 16:32, :].rearrange("p (s f) c -> p s f c", s=8)
        b1_sel = sb("b1_sel", [P, 2 * B, FH])
        stats = sb("stats", [P, TILES, 6])
        mv = sb("mv", [P, B * TILES, 2])
        rstd = sb("rstd", [P, B * TILES])
        neg_max = sb("neg_max", [P, 2])
        den = sb("den", [P, 2])
        rden = sb("rden", [P, 2])
        tok_sum = sb("tok_sum", [P, 2 * B])
        tok_mean = sb("tok_mean", [P, B])
        route = sb("route", [B, 16, E])
        route_s = sb("route_s", [B, 16])
        route_i = sb("route_i", [B, 2], I32)
        rank = sb("rank", [B, E])
        pick_w = sb("pick_w", [B, B, 2])
        weight_all = sb("weight_all", [P, B, 2])
        over_prod = prod[:, :, :, :].rearrange("p s g c -> p s (g c)")
        y_new = over_prod[:, 0, :].rearrange("p (t c) -> p t c", c=C)
        dense_t = over_prod[0:E, 1, :].rearrange("e (n t) -> e n t", n=B)

        def flat_rows(q):
            return over_prod[:, q, :] if q < PROD else samp[:, :]

        x_in = [sem(f"x_in{n}") for n in range(B)]
        w_in = sem("w_in")
        zeros_set = sem("zeros_set")
        pads_out = sem("pads_out")
        consts = sem("consts")
        dve = sem("dve")
        pool = sem("pool")
        act = sem("act")
        xt_done = sem("xt_done")
        xt_copied = sem("xt_copied")
        gn_mm = sem("gn_mm")
        gn_in = sem("gn_in")
        gn_var = sem("gn_var")
        gn_rstd = sem("gn_rstd")
        xg_ready = sem("xg_ready")
        bias_mm = sem("bias_mm")
        bn_var = sem("bn_var")
        bn_rstd = sem("bn_rstd")
        fold_done = sem("fold_done")
        flat_done = sem("flat_done")
        proj_mm = sem("proj_mm")
        proj_out = sem("proj_out")
        padded_out = [sem(f"padded_out{q}") for q in range(H // 8)]
        copies_in = sem("copies_in")
        rows_ready = sem("rows_ready")
        conv_done = sem("conv_done")
        gate_done = sem("gate_done")
        x1_done = sem("x1_done")
        off_mm = sem("off_mm")
        off_done = sem("off_done")
        logits_done = sem("logits_done")
        exp_done = sem("exp_done")
        hats_done = sem("hats_done")
        masks_done = sem("masks_done")
        far_mm = sem("far_mm")
        far_done = sem("far_done")
        hats_used = sem("hats_used")
        prod_free = sem("prod_free")
        prod_done = sem("prod_done")
        fix_done = sem("fix_done")
        gathered = sem("gathered")
        waited = sem("waited")
        samp_done = sem("samp_done")
        samp_tp = sem("samp_tp")
        samp_t_done = sem("samp_t_done")
        conv_out = sem("conv_out")
        res1_done = sem("res1_done")
        rows_used = sem("rows_used")
        var1 = sem("var1")
        rstd1 = sem("rstd1")
        normed1 = sem("normed1")
        tp1 = sem("tp1")
        normed_t1 = sem("normed_t1")
        key_mm = sem("key_mm")
        keyed_done = sem("keyed_done")
        score_mm = sem("score_mm")
        max_done = sem("max_done")
        prob_done = sem("prob_done")
        probs_tp = sem("probs_tp")
        probs_t_a = sem("probs_t_a")
        probs_t_v = sem("probs_t_v")
        mix_mm = sem("mix_mm")
        res2_done = sem("res2_done")
        var2 = sem("var2")
        rstd2 = sem("rstd2")
        normed2 = sem("normed2")
        tp2 = sem("tp2")
        normed_t2 = sem("normed_t2")
        mean_done = sem("mean_done")
        logit_mm = sem("logit_mm")
        shifted_logits = sem("shifted_logits")
        scaled_logits = sem("scaled_logits")
        gap_done = sem("gap_done")
        routing_done = sem("routing_done")
        r_exp = sem("r_exp")
        load_mm = sem("load_mm")
        picked = sem("picked")
        spread_mm = sem("spread_mm")
        spread_done = sem("spread_done")
        experts_in = [sem(f"experts_in{n}") for n in range(B)]
        w2_scaled = sem("w2_scaled")
        up_mm = sem("up_mm")
        gelu_done = sem("gelu_done")
        down_mm = sem("down_mm")
        y_done = sem("y_done")
        var3 = sem("var3")
        rstd3 = sem("rstd3")
        res3_done = sem("res3_done")
        stored = sem("stored")

        N_W = 19
        x_tiles = x.rearrange("n (k r) w c -> n (r w) k c", r=ROWS)
        out_tiles = out.rearrange("n (k r) w c -> n (r w) k c", r=ROWS)
        PIECE = 2 * ROWS
        PCS = H // PIECE
        N_PADS = B * (2 * PAD + 2)
        FIRST = ROWS + WIN - 1
        PIECES = [(0, FIRST)] + [(FIRST + ROWS * k, FIRST + ROWS * (k + 1)) for k in range(HALF - 1)]

        block = ctx.enter_context(nc.Block())

        @block.sync
        def _(sp):
            for n in range(B):
                sp.dma_start(res[:, n * TILES:(n + 1) * TILES, :], x_tiles[n]).then_inc(x_in[n], 16)
            sp.wait_ge(zeros_set, 1)
            for n in range(B):
                for w0 in (0, WP - PAD):
                    for p0 in range(PAD):
                        sp.dma_start(padded[n, w0 + p0, :, :].rearrange("(a b) c -> a (b c)", a=19),
                                     zero_rows[0:19, 0:2 * C]).then_inc(pads_out, 16)
                for y0 in (0, HP - PAD):
                    sp.dma_start(padded[n, PAD:PAD + W, y0:y0 + PAD, :].rearrange("w y c -> w (y c)"),
                                 zero_rows[32 * n:32 * n + W, :]).then_inc(pads_out, 16)
            for q in range(PCS):
                sp.wait_ge(proj_out, 2 * (q + 1))
                sp.dma_start(padded[:, PAD:PAD + W, PAD + PIECE * q:PAD + PIECE * (q + 1), :]
                             .rearrange("n w y c -> n w (y c)"),
                             stage[:, PIECE * q:PIECE * (q + 1), :].rearrange("p y c -> p (y c)")
                             ).then_inc(padded_out[q], 16)

            def copies(i, r0, r1, s0):
                for d in range(WIN):
                    sp.dma_start(shifted[:, d, s0 * G:(s0 + r1 - r0) * G, :]
                                 .rearrange("p s c -> p (s c)"),
                                 padded[:, d:d + W, r0:r1, :].rearrange("n w y c -> n w (y c)")
                                 ).then_inc(copies_in, 16)
                sp.wait_ge(copies_in, 16 * WIN * (i + 1))

            sp.wait_ge(pads_out, 16 * N_PADS)
            for i, (r0, r1) in enumerate(PIECES):
                for q in range(-(-(r1 - PAD) // PIECE)):
                    sp.wait_ge(padded_out[q], 16)
                copies(i, r0, r1, r0)
                sp.sem_inc(rows_ready, 1)
            for q in range(PCS):
                sp.wait_ge(padded_out[q], 16)
            for k in range(HALF):
                s0, s1 = ROWS * k, (ROWS * (k + 1) if k < HALF - 1 else SLOTS)
                sp.wait_ge(rows_used, k + 1)
                copies(HALF + k, ROWS * HALF + s0, ROWS * HALF + s1, s0)
                sp.sem_inc(rows_ready, (0, 0, 1, HALF - 1)[k]) if k >= 2 else None

            for n in range(B):
                sp.wait_ge(picked, 1)
                for j in range(2):
                    e = sp.value_load(route_i[n:n + 1, j:j + 1], min_val=0, max_val=E - 1)
                    s = 2 * n + j
                    sp.dma_start(w1_sel[:, s, :], w1[bass.ds(e, 1), :, :].rearrange("e d f -> d (e f)")
                                 ).then_inc(experts_in[n], 16)
                    sp.dma_start(w2_sel[:, s, :, :],
                                 w2[bass.ds(e, 1), :, :].rearrange("e (h f) d -> f (e h) d", h=FH)
                                 ).then_inc(experts_in[n], 16)
                    sp.dma_start(b1_sel[:, s, :],
                                 b1[bass.ds(e, 1), :].rearrange("e (h f) -> f (e h)", h=FH),
                                 allow_slow_non_contiguous=True).then_inc(experts_in[n], 16)
            for q in range(2 * B):
                sp.wait_ge(res3_done, q + 1)
                sp.dma_start(out_tiles[q // 2][:, 4 * (q % 2):4 * (q % 2) + 4, :],
                             res[:, 4 * q:4 * q + 4, :]).then_inc(stored, 16)
            sp.wait_ge(stored, 16 * 2 * B)

        @block.scalar
        def _(sc):
            own = Own(sc, act)
            loads = [(in_w_sb[:, :], in_w), (out_w_sb[:, :], out_w), (off_raw[:, :], off_w),
                     (offmask_w[:, 2 * GP:], mask_w), (attn_w_sb[:, :], attn_w), (wr_sb[:, :], wr),
                     (b2_sb[:, :], b2), (dw_sb[:, :], dw_k.rearrange("c a y x -> c (a y x)")),
                     (off_b_raw[:, :], off_b.rearrange("(a n) -> a n", a=1)),
                     (offmask_b[:, 2 * GP:], mask_b.rearrange("(a n) -> a n", a=1)),
                     (br_sb[:, :], br.rearrange("(a n) -> a n", a=1))]
            for i, v in enumerate((in_b, out_b, gamma, beta)):
                loads.append((bias_rows[:, i, :], v.rearrange("(a n) -> a n", a=1)))
            for i, v in enumerate((bn_g, bn_b, bn_m, bn_v)):
                loads.append((bn_sb[:, i:i + 1], v.rearrange("(n a) -> n a", a=1)))
            for dst, src in loads:
                sc.dma_start(dst, src, allow_slow_non_contiguous=True).then_inc(w_in, 16)
            assert len(loads) == N_W
            for i in range(2 * B):
                sc.wait_ge(gn_in, i + 1)
                if i == 0:
                    sc.wait_ge(zeros_set, 2)
                n, h = i // 2, i % 2
                sc.activation(xg[:, 1 + 16 * h:17 + 16 * h, n, 1:W + 1],
                              bank[i % 4][:, :].rearrange("c (y w) -> c y w", w=W),
                              ACT.Copy).then_inc(xt_copied, 1)

            sc.wait_ge(xg_ready, B)
            for q in range(CHUNKS):
                sc.activation(flat_rows(q).rearrange("c (y n w) -> c y n w", y=ROWS, n=B),
                              xg[:, 1 + ROWS * q:1 + ROWS * (q + 1), :, 1:W + 1], ACT.Copy).then_inc(flat_done, 1)

            def prepare(k):
                sc.wait_ge(conv_done, k + 1)
                cf = conv[:, :, :].rearrange("c a w -> c (a w)")
                sc.activation(gate[:, :], cf, ACT.Tanh, bias=bn_fold[:, 1:2], scale=bn_fold[:, 0:1])
                sc.activation(cf, cf, ACT.Identity, bias=bn_fold[:, 1:2], scale=bn_fold[:, 0:1]
                              ).then_inc(gate_done, 1)
                sc.wait_ge(off_mm, k + 1)
                sc.wait_ge(fix_done, k + 1)
                sc.activation(off[:, :, :], pair[0][:, :].rearrange("p (r o) -> p r o", r=ROWS)[:, :, 0:3 * GP],
                              ACT.Copy).then_inc(off_done, 1)
                sc.wait_ge(off_done, k + 1)
                sc.wait_ge(hats_used, k + 1)
                for t in range(TAPS):
                    own(sc.activation(
                        hats[:, :, :, t].rearrange("p a (r g) -> p a r g", r=ROWS),
                        off[:, :, 0:2 * GP].rearrange("p r (a g) -> p a r g", a=2),
                        ACT.Abs, bias=tap_bias[:, t:t + 1]))
                own.wait()
                hf = hats[:, :, :, :].rearrange("p a g t -> p (a g t)")
                sc.activation(hf, hf, ACT.Relu, bias=tap_bias[:, TAPS:TAPS + 1], scale=-1.0).then_inc(hats_done, 1)
                sc.wait_ge(logits_done, k + 1)
                mf = mask[:, :, :].rearrange("p g q -> p (g q)")
                sc.activation(mf, mf, ACT.Exp).then_inc(exp_done, 1)

            def copy_out(k):
                sc.wait_ge(samp_tp, k + 1)
                sc.activation(samp_t[:, :, :, :].rearrange("c n r w -> c r n w"),
                              bank[2][:, :].rearrange("c (r n w) -> c r n w", r=ROWS, n=B),
                              ACT.Copy).then_inc(samp_t_done, 1)

            sc.wait_ge(fold_done, 1)
            sc.wait_ge(consts, 1)
            prepare(0)
            with sc.Fori(0, CHUNKS - 1) as k:
                own.enter(k, TAPS)
                prepare(k + 1)
                copy_out(k)
                own.leave(CHUNKS - 1)
            copy_out(CHUNKS - 1)

            def copy_t(i, done, out_sem, sums):
                sc.wait_ge(done, i + 1)
                n, h = i // 2, i % 2
                kw = {"accum_out": tok_sum[:, i:i + 1]} if sums else {}
                sc.activation(normed_t[:, n, h * 512:(h + 1) * 512], bank[i % 2][:, :], ACT.Copy, **kw
                              ).then_inc(out_sem, 1)

            for i in range(2 * B):
                copy_t(i, tp1, normed_t1, False)
            for i in range(2 * B):
                sc.wait_ge(key_mm, i + 1)
                sc.activation(keyed[:, i // 2, (i % 2) * 512:(i % 2 + 1) * 512], bank[2 + i % 2][:, :],
                              ACT.Copy, scale=float(C) ** -0.5).then_inc(keyed_done, 1)

            def exps(i, s):
                sc.wait_ge(max_done, i + 1)
                sc.activation(probs[:, s, :], pair[s][:, :], ACT.Exp, bias=neg_max[:, s:s + 1],
                              accum_out=den[:, s:s + 1]).then_inc(prob_done, 1)

            def half_probs(i):
                sc.wait_ge(probs_tp, 2 * i + 1)
                sc.activation(probs_t[:, 0:512], bank[0][:, :], ACT.Copy).then_inc(probs_t_a, 1)

            with sc.Fori(0, B * TILES // 2) as j:
                for s in range(2):
                    exps(j * 2 + s, s)
                    half_probs(j * 2 + s)

            for i in range(2 * B):
                copy_t(i, tp2, normed_t2, True)
            sc.wait_ge(normed_t2, 2 * B)
            sc.wait_ge(shifted_logits, 1)
            sc.activation(route[:, 1, :], route[:, 0, :], ACT.Exp).then_inc(r_exp, 1)
            sc.wait_ge(scaled_logits, 1)
            sc.activation(route[:, 5, :], route[:, 4, :], ACT.Exp).then_inc(r_exp, 1)
            sc.wait_ge(gap_done, 1)
            sc.activation(route_s[:, 9:10], route_s[:, 8:9], ACT.Exp).then_inc(r_exp, 1)
            for q in range(2 * B):
                sc.wait_ge(experts_in[q // 2], 96)
                if q >= 2:
                    sc.wait_ge(down_mm, 4 * (q - 1))
                for f in range(4):
                    sc.wait_ge(up_mm, 4 * q + f + 1)
                    s = 2 * (q // 2) + f // 2
                    sc.activation(hidden[:, q % 2, f, :], bank[f % 2][:, :], ACT.Gelu,
                                  bias=b1_sel[:, s, f % 2:f % 2 + 1]).then_inc(gelu_done, 1)

        @block.tensor
        def _(pe):
            pe.wait_ge(consts, 1)
            for i in range(2 * B):
                if i % 2 == 0:
                    pe.wait_ge(x_in[i // 2], 16)
                if i >= 4:
                    pe.wait_ge(xt_copied, i - 3)
                    pe.wait_ge(gn_in, i - 3)
                for t in range(4):
                    mm = pe.transpose(bank[i % 4][:, t * P:(t + 1) * P], res[:, 4 * i + t, :], ident[:, :])
                mm.then_inc(xt_done, 1)
            pe.wait_ge(w_in, 16 * N_W)
            pe.matmul(pair[0][:, 0:4 * C], ones[0:1, :], bias_rows[:, :, :].rearrange("a v c -> a (v c)"),
                      start=True, stop=True).then_inc(bias_mm, 1)
            pe.wait_ge(gn_in, 2 * B + 1)
            pe.matmul(pair[1][:, 0:B], group_mean[:, :], gn_mv[:, :, 0], start=True, stop=True).then_inc(gn_mm, 1)
            pe.wait_ge(gn_in, 2 * B + 2)
            pe.matmul(pair[1][:, 512:512 + B], group_mean[:, :], gn_v[:, 1, :], start=True, stop=True
                      ).then_inc(gn_mm, 1)
            for q in range(CHUNKS):
                pe.wait_ge(flat_done, q + 1)
                if q >= 2:
                    pe.wait_ge(proj_out, q - 1)
                for r in range(ROWS):
                    mm = pe.matmul(bank[q % 2][:, r * P:(r + 1) * P], flat_rows(q)[:, r * P:(r + 1) * P],
                                   in_w_sb[:, :], start=True, stop=True)
                mm.then_inc(proj_mm, 1)
            pe.sem_inc(prod_free, PROD)

            def offsets(k):
                pe.wait_ge(x1_done, k + 1)
                pe.wait_ge(fold_done, 1)
                if not isinstance(k, int) or k > 0:
                    pe.wait_ge(off_done, k)
                for r in range(ROWS):
                    o = pair[0][:, r * 256:r * 256 + 3 * GP]
                    pe.matmul(o, x1[:, r * P:(r + 1) * P], offmask_w[:, :], start=True, stop=False)
                    mm = pe.matmul(o, ones[0:1, :], offmask_b[:, :], start=False, stop=True)
                mm.then_inc(off_mm, 1)

            def count_far(k):
                pe.wait_ge(masks_done, k + 1)
                if not isinstance(k, int) or k > 0:
                    pe.wait_ge(far_done, k)
                pe.matmul(pair[1][:, 0:ROWS * GP], ones[:, :], far[:, :], start=True, stop=True).then_inc(far_mm, 1)

            def add_up(k, s):
                for d in range(SEGS[s], SEGS[s + 1]):
                    pe.wait_ge(prod_done, k * STENCIL + d + 1)
                    pe.matmul(bank[3][:, :], ident[:, :], prod[:, d % PROD, :, :].rearrange("p g c -> p (g c)"),
                              start=(d == 0), stop=(d == STENCIL - 1)).then_inc(prod_free, 1)

            def project(k):
                pe.wait_ge(samp_done, k + 1)
                for r in range(ROWS):
                    mm = pe.transpose(bank[2][:, r * P:(r + 1) * P], samp[:, r * P:(r + 1) * P], ident[:, :])
                mm.then_inc(samp_tp, 1)
                pe.wait_ge(samp_t_done, k + 1)
                for n in range(B):
                    mm = pe.matmul(bank[0][:, n * P:(n + 1) * P], samp_t[:, n, :, :].rearrange("c r w -> c (r w)"),
                                   out_w_sb[:, :], start=True, stop=True)
                mm.then_inc(conv_out, 1)

            pe.wait_ge(proj_out, CHUNKS)
            offsets(0)
            count_far(0)
            with pe.Fori(0, CHUNKS - 1) as k:
                add_up(k, 0)
                add_up(k, 1)
                offsets(k + 1)
                add_up(k, 2)
                add_up(k, 3)
                count_far(k + 1)
                add_up(k, 4)
                project(k)
            for s in range(5):
                add_up(CHUNKS - 1, s)
            project(CHUNKS - 1)

            def transposes(i, normed_sem, tp_sem, copied):
                pe.wait_ge(normed_sem, i // 2 + 1)
                if i >= 2:
                    pe.wait_ge(copied, i - 1)
                for t in range(4):
                    mm = pe.transpose(bank[i % 2][:, t * P:(t + 1) * P], normed[:, 4 * i + t, :], ident[:, :])
                mm.then_inc(tp_sem, 1)

            for i in range(2 * B):
                transposes(i, normed1, tp1, normed_t1)
            for i in range(2 * B):
                pe.wait_ge(normed_t1, i + 1)
                if i >= 2:
                    pe.wait_ge(keyed_done, i - 1)
                pe.matmul(bank[2 + i % 2][:, :], attn_w_sb[:, :],
                          normed_t[:, i // 2, (i % 2) * 512:(i % 2 + 1) * 512], start=True, stop=True
                          ).then_inc(key_mm, 1)

            def scores(i):
                n, t = divmod(i, TILES)
                if i == 0:
                    pe.wait_ge(keyed_done, 2 * B)
                if i >= 2:
                    pe.wait_ge(prob_done, i - 1)
                for h in range(2):
                    mm = pe.matmul(pair[i % 2][:, h * 512:(h + 1) * 512], keyed[:, n, t * P:(t + 1) * P],
                                   normed_t[:, n, h * 512:(h + 1) * 512], start=True, stop=True)
                mm.then_inc(score_mm, 1)

            def mix(i):
                n = i // TILES
                pe.wait_ge(prob_done, i + 1)
                for h in range(2):
                    if i >= 1:
                        pe.wait_ge((probs_t_a, probs_t_v)[h], i)
                    for m in range(4):
                        mm = pe.transpose(bank[h][:, m * P:(m + 1) * P],
                                          probs[:, i % 2, (4 * h + m) * P:(4 * h + m + 1) * P], ident[:, :])
                    mm.then_inc(probs_tp, 1)
                pe.wait_ge(probs_t_a, i + 1)
                pe.wait_ge(probs_t_v, i + 1)
                if i >= 1:
                    pe.wait_ge(res2_done, i)
                for m in range(TILES):
                    mm = pe.matmul(bank[2][:, 0:C], probs_t[:, m * P:(m + 1) * P], normed[:, n * TILES + m, :],
                                   start=(m == 0), stop=(m == TILES - 1))
                mm.then_inc(mix_mm, 1)

            for i in range(B * TILES + 1):
                if i < B * TILES:
                    scores(i)
                if i >= 1:
                    mix(i - 1)

            for i in range(2 * B):
                transposes(i, normed2, tp2, normed_t2)
            pe.wait_ge(mean_done, 1)
            pe.matmul(bank[2][0:B, 0:E], tok_mean[:, :], wr_sb[:, :], start=True, stop=False)
            pe.matmul(bank[2][0:B, 0:E], ones[0:1, 0:B], br_sb[:, :], start=False, stop=True).then_inc(logit_mm, 1)
            pe.wait_ge(routing_done, 1)
            pe.matmul(bank[2][0:B, 0:E], ones[0:B, 0:B], route[:, 2, :], start=True, stop=True).then_inc(load_mm, 1)
            pe.wait_ge(picked, 1)
            pe.matmul(bank[2][:, 0:2 * B], ones[0:B, :], pick_w[:, :, :].rearrange("k n j -> k (n j)"),
                      start=True, stop=True).then_inc(spread_mm, 1)
            pe.matmul(bank[3][0:E, :], route[:, 12, :], cols4[:, :, :].rearrange("k n t -> k (n t)"),
                      start=True, stop=True).then_inc(spread_mm, 1)

            def up(q):
                n = q // 2
                if q % 2 == 0:
                    pe.wait_ge(experts_in[n], 96)
                for f in range(4):
                    i = 4 * q + f
                    if i >= 2:
                        pe.wait_ge(gelu_done, i - 1)
                    pe.matmul(bank[f % 2][:, :], w1_sel[:, 2 * n + f // 2, (f % 2) * P:(f % 2 + 1) * P],
                              normed_t[:, n, (q % 2) * 512:(q % 2 + 1) * 512], start=True, stop=True
                              ).then_inc(up_mm, 1)

            def down(q):
                n = q // 2
                pe.wait_ge(gelu_done, 4 * (q + 1))
                pe.wait_ge(w2_scaled, n + 1)
                for t in range(4):
                    i = 4 * q + t
                    if i >= 2:
                        pe.wait_ge(y_done, i - 1)
                    o = bank[2 + t % 2][:, 0:C]
                    pe.matmul(o, dense_t[:, n, :], b2_sb[:, :], start=True, stop=False)
                    for f in range(4):
                        mm = pe.matmul(o, hidden[:, q % 2, f, t * P:(t + 1) * P],
                                       w2_sel[:, 2 * n + f // 2, f % 2, :], start=False, stop=(f == 3))
                    mm.then_inc(down_mm, 1)

            for q in range(2 * B + 1):
                if q == 1:
                    pe.wait_ge(spread_done, 1)
                if q < 2 * B:
                    up(q)
                if q >= 1:
                    down(q - 1)

        @block.gpsimd
        def _(gp):
            own = Own(gp, pool)
            gp.memset(zero_rows[:, :], 0.0).then_inc(zeros_set, 1)
            gp.memset(xg[:, :, :, :], 0.0).then_inc(zeros_set, 1)
            own(gp.memset(ident[:, :], 0.0))
            own(gp.memset(ones[:, :], 1.0))
            own(gp.memset(group_mean[:, :], 1.0 / GN_C))
            own.wait()
            own(gp.affine_select(out=ident[:, :], in_=ident[:, :], compare_op=ALU.not_equal, fill=1.0, base=0,
                                 pattern=[[-1, P]], channel_multiplier=1))
            gm = group_mean[:, :].rearrange("p (g j) -> p g j", j=GN_C)
            own.link(gp.affine_select(out=gm, in_=gm, compare_op=ALU.is_ge, fill=0.0, base=0,
                                      pattern=[[-GN_C, P // GN_C], [0, GN_C]], channel_multiplier=1))
            own.link(gp.affine_select(out=gm, in_=gm, compare_op=ALU.is_ge, fill=0.0, base=GN_C - 1,
                                      pattern=[[GN_C, P // GN_C], [0, GN_C]], channel_multiplier=-1))
            for t in range(TAPS):
                gp.memset(tap_bias[:, t:t + 1], float(REACH - t))
            gp.memset(tap_bias[:, TAPS:TAPS + 1], 1.0)
            own.link(gp.memset(neg_half[:, :], -0.5))
            own.link(gp.iota(rank[:, :], pattern=[[-1, E]], base=E, channel_multiplier=0,
                             allow_small_or_imprecise_dtypes=True))
            for n in range(B):
                own.link(gp.tensor_copy(cols4[:, n, :], ones[0:B, :])) if n == 0 else \
                    own.link(gp.tensor_copy(cols4[:, n, :], ones[0:B, :]))
            gp.affine_select(out=cols4[:, :, :], in_=cols4[:, :, :], compare_op=ALU.is_equal, fill=0.0, base=0,
                             pattern=[[-1, B], [0, P]], channel_multiplier=1).then_inc(consts, 1)

            for n in range(B):
                own.link(gp.iota(grid_i[32 * n:32 * n + 32, 0:GP].rearrange("p (g a b) -> p g a b", g=G, a=3),
                            pattern=[[0, G], [1, 3], [0, 3]], base=-1, channel_multiplier=1))
                own.link(gp.iota(part_i[32 * n:32 * n + 32, :], pattern=[[0, 1]],
                            base=(n * WP + PAD) * HP * G + PAD * G, channel_multiplier=0))
            own.link(gp.iota(grid_i[:, GP:2 * GP].rearrange("p (g a b) -> p g a b", g=G, a=3),
                        pattern=[[0, G], [0, 3], [1, 3]], base=-1, channel_multiplier=0))
            own.link(gp.iota(low_i[:, 0:GP].rearrange("p (g a) -> p g a", g=G),
                        pattern=[[1, G], [0, PTS]], base=0, channel_multiplier=0))
            own.link(gp.tensor_copy(grid[:, :], grid_i[:, :]))
            own.link(gp.tensor_copy(part_f[:, :], part_i[:, :]))
            own.link(gp.tensor_copy(cell0[:, :], low_i[:, 0:GP]))
            own.link(gp.tensor_scalar(cell0[:, :], cell0[:, :], part_f[:, 0:1], None, ALU.add))

            gp.wait_ge(bn_var, 1)
            gp.tensor_tensor(bn_fold[:, 3:4], bn_fold[:, 2:3], neg_half[:, 0:1], ALU.pow).then_inc(bn_rstd, 1)
            gp.wait_ge(gn_var, 1)
            gp.tensor_tensor(gn_v[:, 3, :], gn_v[:, 2, :], neg_half[:, 0:B], ALU.pow).then_inc(gn_rstd, 1)

            def wait(what, count):
                gp.wait_ge(what, count)
                gp.sem_inc(waited, 1)

            own.alone = waited
            gp.sem_inc(fix_done, 1)
            ROW_STEPS, POINT_STEPS = 32, 7
            for q in range(PCS):
                wait(padded_out[q], 16)
            wait(pads_out, 16 * N_PADS)
            own(gp.memset(fix[:, :, :], 0.0))
            start = own.n
            per_row = 1 + ROW_STEPS + GP * POINT_STEPS
            per_chunk = ROWS * per_row + 1
            table = padded.rearrange("n w y (g c) -> (n w y g) c", g=G)
            with gp.Fori(0, CHUNKS) as k:
                wait(off_done, k + 1)
                wait(masks_done, k + 1)
                wait(far_done, k + 1)
                with gp.Fori(0, ROWS) as r:
                    row0 = k * per_chunk + start + r * per_row
                    any_far = gp.value_load(far_rows[0:1, bass.ds(r, 1)], min_val=0, max_val=P * GP)
                    with gp.If(any_far > 0):
                        own.base, own.n = row0, 0
                        own(gp.tensor_copy(pos[:, :], off[:, bass.ds(r, 1), 0:2 * GP].rearrange("p r o -> p (r o)")))
                        own(gp.tensor_copy(far_m[:, :], mask_far[:, bass.ds(r * GP, GP)]))
                        own.wait()
                        own.link(gp.tensor_tensor(pos[:, :], pos[:, :], grid[:, :], ALU.add))
                        own.link(gp.tensor_scalar(pos[:, :], pos[:, :], 33.0, -2.0, ALU.min, ALU.max))
                        own.link(gp.tensor_copy(low_i[:, :], pos[:, :]))
                        own.link(gp.tensor_copy(low[:, :], low_i[:, :]))
                        own.link(gp.tensor_tensor(over[:, :], low[:, :], pos[:, :], ALU.subtract))
                        own.link(gp.tensor_scalar(over[:, :], over[:, :], 0.0, None, ALU.is_gt))
                        own.link(gp.tensor_tensor(low[:, :], low[:, :], over[:, :], ALU.subtract))
                        own.link(gp.tensor_tensor(frac[:, 1, :], pos[:, :], low[:, :], ALU.subtract))
                        own.link(gp.tensor_scalar(frac[:, 0, :], frac[:, 1, :], -1.0, 1.0, ALU.mult, ALU.add))
                        own(gp.tensor_scalar(over[:, :], low[:, :], 1.0, 1.0, ALU.add, ALU.mult))
                        own.wait()
                        for a in range(2):
                            own(gp.tensor_scalar(corner[:, a, :], (low, over)[a][:, :], float(W - 1), 0.0,
                                                 ALU.min, ALU.max))
                        own.wait()
                        for a in range(2):
                            own(gp.tensor_tensor(inside[:, a, :], corner[:, a, :], (low, over)[a][:, :],
                                                 ALU.subtract))
                        own.wait()
                        own.link(gp.tensor_scalar(inside[:, :, :], inside[:, :, :], 0.0, None, ALU.is_equal))
                        own.link(gp.tensor_tensor(frac[:, :, :], frac[:, :, :], inside[:, :, :], ALU.mult))
                        own(gp.tensor_scalar(corner[:, :, 0:GP], corner[:, :, 0:GP], float(HP * G), 0.0,
                                             ALU.mult, ALU.add))
                        own(gp.tensor_scalar(corner[:, :, GP:], corner[:, :, GP:], float(G), 0.0, ALU.mult, ALU.add))
                        own.wait()
                        for a in range(2):
                            own.link(gp.tensor_tensor(cell_f[:, :], corner[:, a, 0:GP], cell0[:, :], ALU.add))
                            own.link(gp.tensor_tensor(cell_t[:, :], far_m[:, :], frac[:, a, 0:GP], ALU.mult))
                            for b in range(2):
                                own(gp.tensor_tensor(cells[:, :, 2 * a + b], cell_f[:, :], corner[:, b, GP:], ALU.add))
                                own(gp.tensor_tensor(cell_w[:, :, 2 * a + b], cell_t[:, :], frac[:, b, GP:], ALU.mult))
                            own.wait()
                        assert own.n == ROW_STEPS, own.n
                        with gp.Fori(0, G) as g:
                            with gp.Fori(0, PTS) as q:
                                point = g * PTS + q
                                count = gp.value_load(far_count[0:1, bass.ds(r * GP + point, 1)], min_val=0, max_val=P)
                                own.base, own.n = row0 + (ROW_STEPS + point * POINT_STEPS), 0
                                with gp.If(count > 0):
                                    own(gp.tensor_copy(cell_now[:, :], cells[:, bass.ds(point, 1), :]
                                                       .rearrange("p a b -> p (a b)")))
                                    own(gp.tensor_copy(w_now[:, :], cell_w[:, bass.ds(point, 1), :]
                                                       .rearrange("p a b -> p (a b)")))
                                    own.wait()
                                    for a in range(4):
                                        gp.indirect_dma_start(
                                            out=got[:, a, :], out_offset=None, in_=table,
                                            in_offset=bass.IndirectOffsetOnAxis(ap=cell_now[:, a:a + 1], axis=0)
                                        ).then_inc(gathered, 16)
                                    gp.wait_ge(gathered, 64)
                                    gp.inc_swdge_sem([gathered], [64], mode="sub")
                                    own.link(gp.tensor_tensor(got[:, :, :], got[:, :, :],
                                                              w_now[:, :].unsqueeze(2).to_broadcast([P, 4, CG]), ALU.mult))
                                    to = fix[:, bass.ds(r * G + g, 1), :].rearrange("p a c -> p (a c)")
                                    for a in range(4):
                                        own.link(gp.tensor_tensor(to, to, got[:, a, :], ALU.add))
                                    assert own.n == POINT_STEPS
                                with gp.Else():
                                    gp.sem_inc(pool, POINT_STEPS)
                        gp.nop()
                    with gp.Else():
                        gp.sem_inc(pool, per_row - 1)
                    own.base, own.n = row0 + (per_row - 1), 0
                    own.link(gp.tensor_scalar(grid[:, GP:], grid[:, GP:], 1.0, 0.0, ALU.add, ALU.add))
                own.base, own.n = k * per_chunk + (start + ROWS * per_row), 0
                own.wait()
                gp.sem_inc(fix_done, 1)
                wait(samp_done, k + 1)
                own.link(gp.memset(fix[:, :, :], 0.0))
            own.base, own.n, own.alone = 0, start + CHUNKS * per_chunk, None

            for done, out_sem in ((var1, rstd1), (var2, rstd2)):
                for n in range(B):
                    gp.wait_ge(done, n + 1)
                    gp.tensor_tensor(rstd[:, n * TILES:(n + 1) * TILES], mv[:, n * TILES:(n + 1) * TILES, 1],
                                     neg_half[:, 0:TILES], ALU.pow).then_inc(out_sem, 1)
            for q in range(2 * B):
                gp.wait_ge(var3, q + 1)
                gp.tensor_tensor(rstd[:, 4 * q:4 * q + 4], mv[:, 4 * q:4 * q + 4, 1], neg_half[:, 0:4], ALU.pow
                                 ).then_inc(rstd3, 1)

        @block.vector
        def _(ve):
            own = Own(ve, dve)
            for i in range(2 * B):
                ve.wait_ge(xt_done, i + 1)
                ve.bn_stats(gn_stats[:, i // 2, i % 2, :], bank[i % 4][:, :]).then_inc(gn_in, 1)
            ve.wait_ge(gn_in, 2 * B)
            for n in range(B):
                last = ve.bn_aggr(gn_mv[:, n, :], gn_stats[:, n, :, :].rearrange("p a b -> p (a b)"))
            last.then_inc(gn_in, 1)
            ve.wait_ge(w_in, 16 * N_W)
            for src, dst in ((off_raw, offmask_w), (off_b_raw, offmask_b)):
                own(ve.tensor_copy(dst[:, 0:2 * GP].rearrange("p (a g) -> p a g", a=2),
                                   src[:, :].rearrange("p (g a) -> p a g", a=2)))
            ve.tensor_scalar(bn_fold[:, 2:3], bn_sb[:, 3:4], BN_EPS, None, ALU.add).then_inc(bn_var, 1)
            ve.wait_ge(bias_mm, 1)
            own(ve.tensor_copy(bias_all[:, :, :].rearrange("p v c -> p (v c)"), pair[0][:, 0:4 * C]))
            ve.wait_ge(gn_mm, 1)
            own.link(ve.tensor_copy(gn_v[:, 0, :], pair[1][:, 0:B]))
            own.link(ve.tensor_tensor(gn_v[:, 2, :], gn_mv[:, :, 0], gn_v[:, 0, :], ALU.subtract))
            own.link(ve.tensor_tensor(gn_v[:, 2, :], gn_v[:, 2, :], gn_v[:, 2, :], ALU.mult))
            ve.tensor_tensor(gn_v[:, 1, :], gn_v[:, 2, :], gn_mv[:, :, 1], ALU.add).then_inc(gn_in, 1)
            ve.wait_ge(gn_mm, 2)
            ve.tensor_scalar(gn_v[:, 2, :], pair[1][:, 512:512 + B], GN_EPS, None, ALU.add).then_inc(gn_var, 1)
            ve.wait_ge(bn_rstd, 1)
            own.link(ve.tensor_tensor(bn_fold[:, 0:1], bn_sb[:, 0:1], bn_fold[:, 3:4], ALU.mult))
            own.link(ve.tensor_tensor(bn_fold[:, 1:2], bn_sb[:, 2:3], bn_fold[:, 0:1], ALU.mult))
            own.link(ve.tensor_tensor(bn_fold[:, 1:2], bn_sb[:, 1:2], bn_fold[:, 1:2], ALU.subtract))
            ve.tensor_scalar(bn_fold[:, 0:2], bn_fold[:, 0:2], 0.5, None, ALU.mult).then_inc(fold_done, 1)
            ve.wait_ge(gn_rstd, 1)
            ve.wait_ge(xt_copied, 2 * B)
            for n in range(B):
                v = xg[:, 1:H + 1, n, 1:W + 1]
                ve.tensor_scalar(v, v, gn_v[:, 0, n:n + 1], gn_v[:, 3, n:n + 1], ALU.subtract, ALU.mult
                                 ).then_inc(xg_ready, 1)
            for q in range(CHUNKS):
                ve.wait_ge(proj_mm, q + 1)
                ve.tensor_tensor(stage[:, ROWS * q:ROWS * (q + 1), :],
                                 bank[q % 2][:, :].rearrange("p (r c) -> p r c", r=ROWS),
                                 bias_all[:, 0:1, :].to_broadcast([P, ROWS, C]), ALU.add).then_inc(proj_out, 1)

            def convolve(k):
                for t in range(9):
                    src = xg_rows[:, bass.ds((k * ROWS + t // 3) * B, ROWS * B), t % 3:t % 3 + W]
                    if t == 0:
                        own.link(ve.tensor_scalar(conv[:, :, :], src, dw_sb[:, 0:1], None, ALU.mult))
                    elif t < 8:
                        own.link(ve.scalar_tensor_tensor(conv[:, :, :], src, dw_sb[:, t:t + 1], conv[:, :, :],
                                                         ALU.mult, ALU.add))
                    else:
                        ve.scalar_tensor_tensor(conv[:, :, :], src, dw_sb[:, t:t + 1], conv[:, :, :],
                                                ALU.mult, ALU.add).then_inc(conv_done, 1)

            def finish_silu(k):
                ve.wait_ge(gate_done, k + 1)
                ve.scalar_tensor_tensor(x1[:, :], gate[:, :], 1.0, conv[:, :, :].rearrange("c a w -> c (a w)"),
                                        ALU.add, ALU.mult).then_inc(x1_done, 1)

            def mask_logits(k):
                ve.wait_ge(off_done, k + 1)
                own(ve.tensor_tensor(far_xy[:, :, :], off[:, :, 0:2 * GP], off[:, :, 0:2 * GP], ALU.mult))
                lg = off[:, :, 2 * GP:].rearrange("p r (g q) -> p r g q", g=G)
                own(ve.tensor_reduce(row_max[:, :].rearrange("p (r g) -> p r g", r=ROWS), lg, AX.X, ALU.max))
                own.wait()
                own(ve.tensor_tensor(far[:, :].rearrange("p (r g) -> p r g", r=ROWS), far_xy[:, :, 0:GP],
                                     far_xy[:, :, GP:], ALU.max))
                for r in range(ROWS):
                    last = ve.tensor_tensor(mask[:, r * G:(r + 1) * G, :], lg[:, r],
                                            row_max[:, r * G:(r + 1) * G].unsqueeze(2).to_broadcast([P, G, PTS]),
                                            ALU.subtract)
                last.then_inc(logits_done, 1)
                own.wait()
                own.link(ve.tensor_scalar(far[:, :], far[:, :], float(REACH) ** 2, None, ALU.is_gt))

            def masks(k):
                mf = mask[:, :, :].rearrange("p g q -> p (g q)")
                ve.wait_ge(exp_done, k + 1)
                own.link(ve.tensor_reduce(row_sum[:, :], mask[:, :, :], AX.X, ALU.add))
                own.link(ve.reciprocal(row_sum[:, :], row_sum[:, :]))
                own.link(ve.tensor_tensor(mask[:, :, :], mask[:, :, :],
                                          row_sum[:, :].unsqueeze(2).to_broadcast([P, ROWS * G, PTS]), ALU.mult))
                own(ve.scalar_tensor_tensor(mask_near[:, :], far[:, :], 0.5, mf, ALU.is_lt, ALU.mult))
                ve.tensor_tensor(mask_far[:, :], far[:, :], mf, ALU.mult).then_inc(masks_done, 1)
                ve.wait_ge(hats_done, k + 1)
                own.wait()
                own(ve.tensor_tensor(hats[:, 1, :, :], hats[:, 1, :, :],
                                     mask_near[:, :].unsqueeze(2).to_broadcast([P, ROWS * GP, TAPS]), ALU.mult))
                ve.wait_ge(far_mm, k + 1)
                own(ve.tensor_copy(far_count[:, :], pair[1][0:1, 0:ROWS * GP]))
                own.link(ve.tensor_reduce(far_rows_f[:, :],
                                          pair[1][0:1, 0:ROWS * GP].rearrange("p (r o) -> p r o", r=ROWS),
                                          AX.X, ALU.add))
                ve.tensor_copy(far_rows[:, :], far_rows_f[:, :]).then_inc(far_done, 1)

            def stencils(k):
                if not isinstance(k, int) or k > 0:
                    ve.wait_ge(prod_done, k * STENCIL)
                own.link(ve.memset(stencil[:, :, :, :], 0.0))
                hx = hats[:, 0, :, :].rearrange("p (g q) t -> p g q t", q=PTS)
                hy = hats[:, 1, :, :].rearrange("p (g q) t -> p g q t", q=PTS)
                for q in range(PTS):
                    kx, ky = q // 3, q % 3
                    full = [P, ROWS * G, TAPS, TAPS]
                    own(ve.tensor_tensor(outer[:, :, :, :], hy[:, :, q, :].unsqueeze(3).to_broadcast(full),
                                         hx[:, :, q, :].unsqueeze(2).to_broadcast(full), ALU.mult))
                    own.wait()
                    to = stencil[:, :, ky:ky + TAPS, kx:kx + TAPS]
                    own.link(ve.tensor_tensor(to, to, outer[:, :, :, :], ALU.add))
                ve.sem_inc(hats_used, 1)

            def products(k, s):
                if s == 0:
                    ve.wait_ge(rows_ready, k + 1)
                for d in range(SEGS[s], SEGS[s + 1]):
                    dy, dx = divmod(d, WIN)
                    ve.wait_ge(prod_free, k * STENCIL + d + 1)
                    ins = ve.tensor_tensor(prod[:, d % PROD, :, :],
                                           shifted[:, dx, bass.ds(((k % HALF) * ROWS + dy) * G, ROWS * G), :],
                                           stencil[:, :, dy, dx].unsqueeze(2).to_broadcast([P, ROWS * G, CG]), ALU.mult)
                    ins.then_inc(prod_done, 1)

            def collect(k):
                ve.wait_ge(prod_free, k * STENCIL + STENCIL + PROD)
                ve.sem_inc(rows_used, 1)
                ve.wait_ge(fix_done, k + 2)
                ve.tensor_tensor(samp[:, :], bank[3][:, :], fix[:, :, :].rearrange("p g c -> p (g c)"), ALU.add
                                 ).then_inc(samp_done, 1)

            def residual(k):
                ve.wait_ge(conv_out, k + 1)
                to = res[:, :, :].rearrange("p (n k) c -> p n k c", n=B)[:, :, bass.ds(k, 1), :] \
                    .rearrange("p n k c -> p n (k c)")
                ve.tensor_tensor(to, bank[0][:, :].rearrange("p (n c) -> p n c", n=B), to, ALU.add
                                 ).then_inc(res1_done, 1)
                ve.wait_ge(res1_done, k + 1)
                own.link(ve.tensor_tensor(to, to, bias_all[:, 1:2, :].to_broadcast([P, B, C]), ALU.add))

            own.wait()
            ve.sem_inc(hats_used, 1)
            n0 = own.n
            convolve(0)
            finish_silu(0)
            mask_logits(0)
            masks(0)
            stencils(0)
            per = own.n - n0
            with ve.Fori(0, CHUNKS - 1) as k:
                own.enter(k, per + 1)
                products(k, 0)
                convolve(k + 1)
                products(k, 1)
                finish_silu(k + 1)
                products(k, 2)
                mask_logits(k + 1)
                products(k, 3)
                masks(k + 1)
                products(k, 4)
                stencils(k + 1)
                collect(k)
                residual(k)
                own.leave(CHUNKS - 1)
            for s in range(5):
                products(CHUNKS - 1, s)
            collect(CHUNKS - 1)
            residual(CHUNKS - 1)

            def normalise(n, src, done, rstd_sem, normed_sem):
                for t in range(TILES):
                    own(ve.bn_stats(stats[:, t, :], src[:, n * TILES + t, :]))
                own.wait()
                for t in range(TILES):
                    own(ve.bn_aggr(mv[:, n * TILES + t, :], stats[:, t, :]))
                own.wait()
                v = mv[:, n * TILES:(n + 1) * TILES, 1]
                ve.tensor_scalar(v, v, LN_EPS, None, ALU.add).then_inc(done, 1)
                ve.wait_ge(rstd_sem, n + 1)
                for t in range(n * TILES, (n + 1) * TILES):
                    last = ve.tensor_scalar(normed[:, t, :], src[:, t, :], mv[:, t, 0:1], rstd[:, t:t + 1],
                                            ALU.subtract, ALU.mult)
                last.then_inc(normed_sem, 1)

            for n in range(B):
                normalise(n, res, var1, rstd1, normed1)

            def maxima(i, s):
                ve.wait_ge(score_mm, i + 1)
                ve.tensor_reduce(neg_max[:, s:s + 1], pair[s][:, :], AX.X, ALU.max, negate=True).then_inc(max_done, 1)

            def half_probs(i):
                ve.wait_ge(probs_tp, 2 * i + 2)
                ve.tensor_copy(probs_t[:, 512:1024], bank[1][:, :]).then_inc(probs_t_v, 1)

            def add_mix(i, s):
                ve.wait_ge(prob_done, i + 1)
                own(ve.reciprocal(rden[:, s:s + 1], den[:, s:s + 1]))
                ve.wait_ge(mix_mm, i + 1)
                own.wait()
                to = res[:, bass.ds(i, 1), :].rearrange("p a c -> p (a c)")
                ve.scalar_tensor_tensor(to, bank[2][:, 0:C], rden[:, s:s + 1], to, ALU.mult, ALU.add
                                        ).then_inc(res2_done, 1)

            maxima(0, 0)
            with ve.Fori(0, B * TILES // 2 - 1) as j:
                own.enter(j, 2)
                for s in range(2):
                    maxima(j * 2 + s + 1, 1 - s)
                    half_probs(j * 2 + s)
                    add_mix(j * 2 + s, s)
                own.leave(B * TILES // 2 - 1)
            maxima(B * TILES - 1, 1)
            for s in range(2):
                half_probs(B * TILES - 2 + s)
                add_mix(B * TILES - 2 + s, s)
            ve.wait_ge(res2_done, B * TILES)

            for n in range(B):
                normalise(n, res, var2, rstd2, normed2)

            ve.wait_ge(normed_t2, 2 * B)
            own.link(ve.tensor_reduce(tok_mean[:, :], tok_sum[:, :].rearrange("p (n h) -> p n h", h=2), AX.X, ALU.add))
            ve.tensor_scalar(tok_mean[:, :], tok_mean[:, :], 1.0 / TOK, None, ALU.mult).then_inc(mean_done, 1)
            ve.wait_ge(logit_mm, 1)
            own.link(ve.tensor_copy(route[:, 3, :], bank[2][0:B, 0:E]))
            own.link(ve.tensor_reduce(route_s[:, 0:1], route[:, 3, :], AX.X, ALU.max))
            ve.tensor_scalar(route[:, 0, :], route[:, 3, :], route_s[:, 0:1], None, ALU.subtract
                             ).then_inc(shifted_logits, 1)
            ve.wait_ge(r_exp, 1)
            own.link(ve.tensor_reduce(route_s[:, 1:2], route[:, 1, :], AX.X, ALU.add))
            own.link(ve.reciprocal(route_s[:, 2:3], route_s[:, 1:2]))
            ve.tensor_scalar(route[:, 2, :], route[:, 1, :], route_s[:, 2:3], None, ALU.mult).then_inc(routing_done, 1)
            ve.wait_ge(load_mm, 1)
            own.link(ve.tensor_scalar(route[:, 6, :], bank[2][0:B, 0:E], float(TOK), float(CAPACITY), ALU.mult, ALU.max))
            own.link(ve.reciprocal(route[:, 7, :], route[:, 6, :]))
            own.link(ve.scalar_tensor_tensor(route[:, 8, :], route[:, 7, :], float(CAPACITY), route[:, 2, :],
                                             ALU.mult, ALU.mult))
            own.link(ve.tensor_reduce(route_s[:, 3:4], route[:, 8, :], AX.X, ALU.max))
            ve.tensor_scalar(route[:, 4, :], route[:, 8, :], route_s[:, 3:4], None, ALU.subtract
                             ).then_inc(scaled_logits, 1)
            ve.wait_ge(r_exp, 2)
            own.link(ve.tensor_reduce(route_s[:, 4:5], route[:, 5, :], AX.X, ALU.add))
            own.link(ve.reciprocal(route_s[:, 5:6], route_s[:, 4:5]))
            own.link(ve.tensor_scalar(route[:, 9, :], route[:, 5, :], route_s[:, 5:6], None, ALU.mult))
            for j in range(2):
                w = route[:, 9, :]
                own.link(ve.tensor_reduce(route_s[:, 6 + j:7 + j], w, AX.X, ALU.max))
                own.link(ve.scalar_tensor_tensor(route[:, 13, :], w, route_s[:, 6 + j:7 + j], rank[:, :],
                                                 ALU.is_equal, ALU.mult))
                own.link(ve.tensor_reduce(route_s[:, 12 + j:13 + j], route[:, 13, :], AX.X, ALU.max))
                own.link(ve.tensor_scalar(route[:, 10 + j, :], rank[:, :], route_s[:, 12 + j:13 + j], None, ALU.is_equal))
                own.link(ve.tensor_scalar(route_i[:, j:j + 1], route_s[:, 12 + j:13 + j], -1.0, float(E),
                                          ALU.mult, ALU.add))
                if j == 0:
                    own.link(ve.scalar_tensor_tensor(w, route[:, 10, :], -BIG_SHIFT, w, ALU.mult, ALU.add))
            ve.tensor_tensor(route_s[:, 8:9], route_s[:, 7:8], route_s[:, 6:7], ALU.subtract).then_inc(gap_done, 1)
            ve.wait_ge(r_exp, 3)
            own.link(ve.tensor_scalar(route_s[:, 10:11], route_s[:, 9:10], 1.0, None, ALU.add))
            own.link(ve.reciprocal(route_s[:, 10:11], route_s[:, 10:11]))
            own.link(ve.tensor_tensor(route_s[:, 11:12], route_s[:, 9:10], route_s[:, 10:11], ALU.mult))
            own.link(ve.tensor_scalar(route[:, 14, :], route[:, 11, :], route_s[:, 11:12], None, ALU.mult))
            own.link(ve.scalar_tensor_tensor(route[:, 12, :], route[:, 10, :], route_s[:, 10:11], route[:, 14, :],
                                             ALU.mult, ALU.add))
            own.link(ve.tensor_copy(pick_w[:, :, :], route_s[:, 10:12].unsqueeze(1).to_broadcast([B, B, 2])))
            ve.tensor_tensor(pick_w[:, :, :], pick_w[:, :, :], ident[0:B, 0:B].unsqueeze(2).to_broadcast([B, B, 2]),
                             ALU.mult).then_inc(picked, 1)
            ve.wait_ge(spread_mm, 2)
            own.link(ve.tensor_copy(weight_all[:, :, :].rearrange("p n j -> p (n j)"), bank[2][:, 0:2 * B]))
            ve.tensor_copy(dense_t[:, :, :].rearrange("e n t -> e (n t)"), bank[3][0:E, :]).then_inc(spread_done, 1)

            for q in range(2 * B):
                if q % 2 == 0:
                    n = q // 2
                    ve.wait_ge(experts_in[n], 96)
                    for j in range(2):
                        last = ve.tensor_scalar(w2_sel[:, 2 * n + j, :, :], w2_sel[:, 2 * n + j, :, :],
                                                weight_all[:, n, j:j + 1], None, ALU.mult)
                    last.then_inc(w2_scaled, 1)
                if q >= 1:
                    ve.wait_ge(res3_done, q)
                for t in range(4):
                    ve.wait_ge(down_mm, 4 * q + t + 1)
                    ve.tensor_tensor(y_new[:, t, :], bank[2 + t % 2][:, 0:C], normed[:, 4 * q + t, :], ALU.add
                                     ).then_inc(y_done, 1)
                    ve.wait_ge(y_done, 4 * q + t + 1)
                    own(ve.bn_stats(stats[:, t, :], y_new[:, t, :]))
                own.wait()
                for t in range(4):
                    own(ve.bn_aggr(mv[:, 4 * q + t, :], stats[:, t, :]))
                own.wait()
                v = mv[:, 4 * q:4 * q + 4, 1]
                ve.tensor_scalar(v, v, LN_EPS, None, ALU.add).then_inc(var3, 1)
                ve.wait_ge(rstd3, q + 1)
                for t in range(4):
                    own(ve.tensor_scalar(y_new[:, t, :], y_new[:, t, :], mv[:, 4 * q + t, 0:1],
                                         rstd[:, 4 * q + t:4 * q + t + 1], ALU.subtract, ALU.mult))
                own.wait()
                to = res[:, 4 * q:4 * q + 4, :]
                own.link(ve.tensor_tensor(y_new[:, :, :], y_new[:, :, :],
                                          bias_all[:, 2:3, :].to_broadcast([P, 4, C]), ALU.mult))
                own(ve.tensor_tensor(to, to, bias_all[:, 3:4, :].to_broadcast([P, 4, C]), ALU.add))
                own.wait()
                ve.tensor_tensor(to, to, y_new[:, :, :], ALU.add).then_inc(res3_done, 1)


_INS = ['x', 'L0_conv_in_w', 'L0_conv_in_b', 'L0_conv_out_w', 'L0_conv_out_b', 'L0_conv_off_w', 'L0_conv_off_b',
        'L0_conv_mask_w', 'L0_conv_mask_b', 'L0_conv_dw_k', 'L0_conv_bn_g', 'L0_conv_bn_b', 'L0_conv_bn_m',
        'L0_conv_bn_v', 'L1_attn_W', 'L1_ffn_Wr', 'L1_ffn_br', 'L1_ffn_W1', 'L1_ffn_b1', 'L1_ffn_W2', 'L1_ffn_b2',
        'L1_ffn_gamma', 'L1_ffn_beta']
_OUTS = [((B, H, W, C), 'float32')]


def kernel(**inputs):
    import numpy as _np
    import concourse.bacc as _bacc
    from concourse import mybir as _mybir
    from concourse.bass_utils import run_bass_kernel_spmd as _run

    nc = _bacc.Bacc("TRN2", target_bir_lowering=False, num_devices=1)
    arrays, args = {}, []
    for name in _INS:
        a = _np.ascontiguousarray(inputs[name])
        arrays[f"in_{name}_dram"] = a
        args.append(nc.dram_tensor(f"in_{name}_dram", a.shape, _mybir.dt.from_np(a.dtype), kind="ExternalInput").ap())
    for i, (shape, dtype) in enumerate(_OUTS):
        dt = _mybir.dt.from_np(_np.dtype(dtype))
        args.append(nc.dram_tensor(f"out_{i}_dram", shape, dt, kind="ExternalOutput").ap())
    hybrid_block_kernel(nc, *args)
    r = _run(nc, [arrays], core_ids=[0])
    got = tuple(r.results[0][f"out_{i}_dram"] for i in range(len(_OUTS)))
    return got[0]
```

```python
from contextlib import ExitStack

import concourse.bass as bass
from concourse import mybir

ALU = mybir.AluOpType
ACT = mybir.ActivationFunctionType
AX = mybir.AxisListType
F32 = mybir.dt.float32
I32 = mybir.dt.int32
U32 = mybir.dt.uint32

B, H, W, C = 4, 32, 32, 128
P = 128
G, PTS = 8, 9
CG = C // G
GP = G * PTS
REACH = 2
TAPS = 2 * REACH + 1
WIN = TAPS + 2
PAD = WIN // 2
HP, WP = H + 2 * PAD, W + 2 * PAD
ROWS = 4
CHUNKS = H // ROWS
CT = ROWS * P
TOK = H * W
TILES = TOK // P
HALF = CHUNKS // 2
SLOTS = ROWS * (HALF - 1) + ROWS + WIN - 1
STENCIL = WIN * WIN
PROD = 7
E = 8
FF = 256
FH = FF // P
CAPACITY = -(-B * TOK * 5 // (4 * E))
GN_EPS = BN_EPS = LN_EPS = 1e-5
GN_C = 4
AHEAD, AT_OFFSETS, AT_FAR, AT_COLLECT = 8, 18, 32, 3
BIG_SHIFT = 4.0


class Own:

    def __init__(self, eng, sem):
        self.eng, self.sem, self.base, self.n, self.alone = eng, sem, 0, 0, None

    def __call__(self, ins):
        ins.then_inc(self.sem, 1)
        self.n += 1
        return ins

    def wait(self):
        self.eng.wait_ge(self.sem, self.base + self.n)
        if self.alone is not None:
            self.eng.sem_inc(self.alone, 1)

    def link(self, ins):
        self(ins)
        self.wait()

    def enter(self, i, per, at=None):
        self.saved = self.n if at is None else at
        self.base, self.n, self.per = i * per + self.saved, 0, per

    def leave(self, turns):
        assert self.n == self.per, (self.n, self.per)
        self.base, self.n = 0, self.saved + turns * self.per


def hybrid_block_kernel(nc, x, in_w, in_b, out_w, out_b, off_w, off_b, mask_w, mask_b, dw_k, bn_g, bn_b,
                        bn_m, bn_v, attn_w, wr, br, w1, b1, w2, b2, gamma, beta, out):
    padded = nc.dram_tensor("padded", (B, WP, HP, C), F32, kind="Internal").ap()
    with ExitStack() as ctx:
        def sb(name, shape, dt=F32):
            return ctx.enter_context(nc.sbuf_tensor(name, shape, dt))

        def sem(name):
            return ctx.enter_context(nc.semaphore(name))

        banks = ctx.enter_context(nc.psum_tensor("banks", [P, 4 * 512], F32))
        bank = [banks[:, i * 512:(i + 1) * 512] for i in range(4)]
        pair = [ctx.enter_context(nc.psum_tensor(f"pair{i}", [P, 1024], F32)) for i in range(2)]

        res = sb("res", [P, B * TILES, C])
        stage = sb("stage", [P, H, C])
        shifted = sb("shifted", [P, WIN, SLOTS * G, CG])
        xg = sb("xg", [P, HP - 4, B, W + 2])
        xg_rows = xg[:, :, :, :].rearrange("c y n w -> c (y n) w")

        ident = sb("ident", [P, P])
        ones = sb("ones", [P, P])
        group_mean = sb("group_mean", [P, P])
        in_w_sb = sb("in_w_sb", [P, C])
        out_w_sb = sb("out_w_sb", [P, C])
        offmask_w = sb("offmask_w", [P, 3 * GP])
        attn_w_sb = sb("attn_w_sb", [P, C])
        wr_sb = sb("wr_sb", [P, E])
        b2_sb = sb("b2_sb", [E, C])
        bias_all = sb("bias_all", [P, 4, C])
        offmask_b = sb("offmask_b", [1, 3 * GP])
        br_sb = sb("br_sb", [1, E])
        dw_sb = sb("dw_sb", [P, 9])
        bn_sb = sb("bn_sb", [P, 4])
        bn_fold = sb("bn_fold", [P, 4])
        neg_half = sb("neg_half", [P, 32])
        tap_bias = sb("tap_bias", [P, TAPS + 1])
        zero_col = sb("zero_col", [P, 1])
        cols4 = sb("cols4", [4, 4, P])

        gn_stats = sb("gn_stats", [P, B, 2, 6])
        gn_mv = sb("gn_mv", [P, B, 2])
        gn_v = sb("gn_v", [P, 4, B])

        conv = sb("conv", [P, ROWS * B, W])
        gate = sb("gate", [P, CT])
        x1 = gate
        off = sb("off", [P, 2, ROWS, 3 * GP])
        far = sb("far", [P, ROWS * GP])
        row_max = sb("row_max", [P, ROWS * G])
        row_sum = sb("row_sum", [P, ROWS * G])
        mask = sb("mask", [P, ROWS * G, PTS])
        mask_far = sb("mask_far", [P, 2, ROWS * GP])
        hats = sb("hats", [P, 2, ROWS * GP, TAPS])
        outer = sb("outer", [P, ROWS * G, TAPS, TAPS])
        far_xy = outer[:, :, :, :].rearrange("p g a b -> p (g a b)")[:, 0:ROWS * 2 * GP] \
            .rearrange("p (r o) -> p r o", r=ROWS)
        stencil = sb("stencil", [P, 2, ROWS * G * STENCIL])
        stencil_of = stencil[:, :, :].rearrange("p s (g a b) -> p s g a b", a=WIN, b=WIN)
        prod = sb("prod", [P, PROD, ROWS * G, CG])
        samp = sb("samp", [P, CT])
        samp_t = sb("samp_t", [P, B, ROWS, W])
        far_sums = sb("far_sums", [1, ROWS * G + ROWS])
        far_points = sb("far_points", [1, 2, ROWS * GP], I32)
        far_groups = sb("far_groups", [1, 2, ROWS * G + ROWS], I32)

        zero_rows = stencil[:, 1, 0:3 * C]
        hats_flat = hats[:, :, :, :].rearrange("p a g t -> p (a g t)")
        off_raw = hats_flat[:, 0:2 * GP]
        off_b_raw = hats_flat[0:1, 2 * GP:4 * GP]
        bias_rows = hats_flat[0:1, 4 * GP:4 * GP + 4 * C].rearrange("a (v c) -> a v c", c=C)

        grid = sb("grid", [P, 2 * GP])
        grid_i = sb("grid_i", [P, 2 * GP], I32)
        part_i = sb("part_i", [P, 1], I32)
        part_f = sb("part_f", [P, 1])
        cell0 = sb("cell0", [P, GP])
        low_i = sb("low_i", [P, 2 * GP], I32)
        cell_now = sb("cell_now", [P, 4], U32)
        w_now = sb("w_now", [P, 4])
        over_stage = stage[:, :, :].rearrange("p y c -> p (y c)")
        at = [0]

        def staged(n):
            at[0] += n
            assert at[0] <= H * C
            return over_stage[:, at[0] - n:at[0]]

        pos = staged(2 * GP)
        low = staged(2 * GP)
        over = staged(2 * GP)
        frac = staged(4 * GP).rearrange("p (a o) -> p a o", a=2)
        corner = staged(4 * GP).rearrange("p (a o) -> p a o", a=2)
        inside = staged(4 * GP).rearrange("p (a o) -> p a o", a=2)
        far_m = staged(GP)
        cell_f = staged(GP)
        cell_t = staged(GP)
        cells = staged(4 * GP).rearrange("p (o a) -> p o a", a=4)
        cell_w = staged(4 * GP).rearrange("p (o a) -> p o a", a=4)
        got = staged(4 * CG).rearrange("p (a c) -> p a c", a=4)
        fix = staged(CT).rearrange("p (g c) -> p g c", c=CG)

        over_shifted = shifted[:, :, :, :].rearrange("p d s c -> p (d s c)")
        at_shifted = [0]

        def reuse(n):
            at_shifted[0] += n
            assert at_shifted[0] <= WIN * SLOTS * C
            return over_shifted[:, at_shifted[0] - n:at_shifted[0]]

        normed = reuse(B * TOK).rearrange("p (t c) -> p t c", c=C)
        normed_t = reuse(B * TOK).rearrange("p (n t) -> p n t", n=B)
        keyed = reuse(B * TOK).rearrange("p (n t) -> p n t", n=B)
        probs = reuse(2 * TOK).rearrange("p (s t) -> p s t", s=2)
        probs_t = reuse(TOK)
        hidden = reuse(2 * 4 * 512).rearrange("p (s f t) -> p s f t", s=2, f=4)
        w1_sel = stage[:, 0:16, :].rearrange("p (s f) c -> p s (f c)", s=8)
        w2_sel = stage[:, 16:32, :].rearrange("p (s f) c -> p s f c", s=8)
        b1_sel = sb("b1_sel", [P, 2 * B, FH])
        stats = sb("stats", [P, TILES, 6])
        mv = sb("mv", [P, B * TILES, 2])
        rstd = sb("rstd", [P, B * TILES])
        neg_max = sb("neg_max", [P, 2])
        den = sb("den", [P, 2])
        rden = sb("rden", [P, 2])
        tok_sum = sb("tok_sum", [P, 2 * B])
        tok_mean = sb("tok_mean", [P, B])
        route = sb("route", [B, 16, E])
        route_s = sb("route_s", [B, 16])
        route_i = sb("route_i", [B, 2], I32)
        rank = sb("rank", [B, E])
        pick_w = sb("pick_w", [B, B, 2])
        weight_all = sb("weight_all", [P, B, 2])
        over_prod = prod[:, :, :, :].rearrange("p s g c -> p s (g c)")
        y_new = over_prod[:, 0, :].rearrange("p (t c) -> p t c", c=C)
        dense_t = over_prod[0:E, 1, :].rearrange("e (n t) -> e n t", n=B)

        def flat_rows(q):
            return over_prod[:, q, :] if q < PROD else samp[:, :]

        x_in = [sem(f"x_in{n}") for n in range(B)]
        w_in = sem("w_in")
        zeros_set = sem("zeros_set")
        pads_out = sem("pads_out")
        consts = sem("consts")
        dve = sem("dve")
        pool = sem("pool")
        act = sem("act")
        xt_done = sem("xt_done")
        xt_copied = sem("xt_copied")
        gn_mm = sem("gn_mm")
        gn_in = sem("gn_in")
        gn_var = sem("gn_var")
        gn_rstd = sem("gn_rstd")
        xg_ready = sem("xg_ready")
        bias_mm = sem("bias_mm")
        bn_var = sem("bn_var")
        bn_rstd = sem("bn_rstd")
        fold_done = sem("fold_done")
        res_biased = sem("res_biased")
        stencil_clear = sem("stencil_clear")
        flat_done = sem("flat_done")
        proj_mm = sem("proj_mm")
        proj_out = sem("proj_out")
        padded_out = [sem(f"padded_out{q}") for q in range(H // 8)]
        copies_in = sem("copies_in")
        rows_ready = sem("rows_ready")
        conv_done = sem("conv_done")
        gate_done = sem("gate_done")
        x1_done = sem("x1_done")
        off_mm = sem("off_mm")
        off_done = sem("off_done")
        logits_done = sem("logits_done")
        exp_done = sem("exp_done")
        hats_done = sem("hats_done")
        masks_done = sem("masks_done")
        far_mm = sem("far_mm")
        far_done = sem("far_done")
        hats_used = sem("hats_used")
        prod_free = sem("prod_free")
        prod_done = sem("prod_done")
        fix_done = sem("fix_done")
        gathered = sem("gathered")
        waited = sem("waited")
        act_waited = sem("act_waited")
        samp_done = sem("samp_done")
        samp_tp = sem("samp_tp")
        samp_t_done = sem("samp_t_done")
        conv_out = sem("conv_out")
        res1_done = sem("res1_done")
        rows_used = sem("rows_used")
        var1 = sem("var1")
        rstd1 = sem("rstd1")
        normed1 = sem("normed1")
        tp1 = sem("tp1")
        normed_t1 = sem("normed_t1")
        key_mm = sem("key_mm")
        keyed_done = sem("keyed_done")
        score_mm = sem("score_mm")
        max_done = sem("max_done")
        prob_done = sem("prob_done")
        probs_tp = sem("probs_tp")
        probs_t_a = sem("probs_t_a")
        probs_t_v = sem("probs_t_v")
        mix_mm = sem("mix_mm")
        res2_done = sem("res2_done")
        var2 = sem("var2")
        rstd2 = sem("rstd2")
        normed2 = sem("normed2")
        tp2 = sem("tp2")
        normed_t2 = sem("normed_t2")
        mean_done = sem("mean_done")
        logit_mm = sem("logit_mm")
        shifted_logits = sem("shifted_logits")
        scaled_logits = sem("scaled_logits")
        gap_done = sem("gap_done")
        routing_done = sem("routing_done")
        r_exp = sem("r_exp")
        load_mm = sem("load_mm")
        picked = sem("picked")
        spread_mm = sem("spread_mm")
        spread_done = sem("spread_done")
        experts_in = [sem(f"experts_in{n}") for n in range(B)]
        w2_scaled = sem("w2_scaled")
        up_mm = sem("up_mm")
        gelu_done = sem("gelu_done")
        down_mm = sem("down_mm")
        y_done = sem("y_done")
        var3 = sem("var3")
        rstd3 = sem("rstd3")
        res3_done = sem("res3_done")
        stored = sem("stored")

        N_W = 19
        x_tiles = x.rearrange("n (k r) w c -> n (r w) k c", r=ROWS)
        out_tiles = out.rearrange("n (k r) w c -> n (r w) k c", r=ROWS)
        PIECE = 2 * ROWS
        PCS = H // PIECE
        N_PADS = B * (2 * PAD + 2)
        FIRST = ROWS + WIN - 1
        PIECES = [(0, FIRST)] + [(FIRST + ROWS * k, FIRST + ROWS * (k + 1)) for k in range(HALF - 1)]

        block = ctx.enter_context(nc.Block())

        @block.sync
        def _(sp):
            for n in range(B):
                sp.dma_start(res[:, n * TILES:(n + 1) * TILES, :], x_tiles[n]).then_inc(x_in[n], 16)
            sp.wait_ge(zeros_set, 1)
            for n in range(B):
                for w0 in (0, WP - PAD):
                    for p0 in range(PAD):
                        sp.dma_start(padded[n, w0 + p0, :, :].rearrange("(a b) c -> a (b c)", a=19),
                                     zero_rows[0:19, 0:2 * C]).then_inc(pads_out, 16)
                for y0 in (0, HP - PAD):
                    sp.dma_start(padded[n, PAD:PAD + W, y0:y0 + PAD, :].rearrange("w y c -> w (y c)"),
                                 zero_rows[32 * n:32 * n + W, :]).then_inc(pads_out, 16)
            for q in range(PCS):
                sp.wait_ge(proj_out, 2 * (q + 1))
                sp.dma_start(padded[:, PAD:PAD + W, PAD + PIECE * q:PAD + PIECE * (q + 1), :]
                             .rearrange("n w y c -> n w (y c)"),
                             stage[:, PIECE * q:PIECE * (q + 1), :].rearrange("p y c -> p (y c)")
                             ).then_inc(padded_out[q], 16)

            def copies(i, r0, r1, s0):
                for d in range(WIN):
                    sp.dma_start(shifted[:, d, s0 * G:(s0 + r1 - r0) * G, :]
                                 .rearrange("p s c -> p (s c)"),
                                 padded[:, d:d + W, r0:r1, :].rearrange("n w y c -> n w (y c)")
                                 ).then_inc(copies_in, 16)
                sp.wait_ge(copies_in, 16 * WIN * (i + 1))

            sp.wait_ge(pads_out, 16 * N_PADS)
            for i, (r0, r1) in enumerate(PIECES):
                for q in range(-(-(r1 - PAD) // PIECE)):
                    sp.wait_ge(padded_out[q], 16)
                copies(i, r0, r1, r0)
                sp.sem_inc(rows_ready, 1)
            for q in range(PCS):
                sp.wait_ge(padded_out[q], 16)
            for k in range(HALF):
                s0, s1 = ROWS * k, (ROWS * (k + 1) if k < HALF - 1 else SLOTS)
                sp.wait_ge(rows_used, k + 1)
                copies(HALF + k, ROWS * HALF + s0, ROWS * HALF + s1, s0)
                if k >= 2:
                    sp.sem_inc(rows_ready, 1 if k == 2 else HALF - 1)

            for n in range(B):
                sp.wait_ge(picked, 1)
                for j in range(2):
                    e = sp.value_load(route_i[n:n + 1, j:j + 1], min_val=0, max_val=E - 1)
                    s = 2 * n + j
                    sp.dma_start(w1_sel[:, s, :], w1[bass.ds(e, 1), :, :].rearrange("e d f -> d (e f)")
                                 ).then_inc(experts_in[n], 16)
                    sp.dma_start(w2_sel[:, s, :, :],
                                 w2[bass.ds(e, 1), :, :].rearrange("e (h f) d -> f (e h) d", h=FH)
                                 ).then_inc(experts_in[n], 16)
                    sp.dma_start(b1_sel[:, s, :],
                                 b1[bass.ds(e, 1), :].rearrange("e (h f) -> f (e h)", h=FH),
                                 allow_slow_non_contiguous=True).then_inc(experts_in[n], 16)
            for q in range(2 * B):
                sp.wait_ge(res3_done, q + 1)
                sp.dma_start(out_tiles[q // 2][:, 4 * (q % 2):4 * (q % 2) + 4, :],
                             res[:, 4 * q:4 * q + 4, :]).then_inc(stored, 16)
            sp.wait_ge(stored, 16 * 2 * B)

        @block.scalar
        def _(sc):
            own = Own(sc, act)
            loads = [(in_w_sb[:, :], in_w), (out_w_sb[:, :], out_w), (off_raw[:, :], off_w),
                     (offmask_w[:, 2 * GP:], mask_w), (attn_w_sb[:, :], attn_w), (wr_sb[:, :], wr),
                     (b2_sb[:, :], b2), (dw_sb[:, :], dw_k.rearrange("c a y x -> c (a y x)")),
                     (off_b_raw[:, :], off_b.rearrange("(a n) -> a n", a=1)),
                     (offmask_b[:, 2 * GP:], mask_b.rearrange("(a n) -> a n", a=1)),
                     (br_sb[:, :], br.rearrange("(a n) -> a n", a=1))]
            for i, v in enumerate((in_b, out_b, gamma, beta)):
                loads.append((bias_rows[:, i, :], v.rearrange("(a n) -> a n", a=1)))
            for i, v in enumerate((bn_g, bn_b, bn_m, bn_v)):
                loads.append((bn_sb[:, i:i + 1], v.rearrange("(n a) -> n a", a=1)))
            for dst, src in loads:
                sc.dma_start(dst, src, allow_slow_non_contiguous=True).then_inc(w_in, 16)
            assert len(loads) == N_W
            for i in range(2 * B):
                sc.wait_ge(gn_in, i + 1)
                if i == 0:
                    sc.wait_ge(zeros_set, 2)
                n, h = i // 2, i % 2
                sc.activation(xg[:, 1 + 16 * h:17 + 16 * h, n, 1:W + 1],
                              bank[i % 4][:, :].rearrange("c (y w) -> c y w", w=W),
                              ACT.Copy).then_inc(xt_copied, 1)

            sc.wait_ge(xg_ready, B)
            for q in range(CHUNKS):
                sc.activation(flat_rows(q).rearrange("c (y n w) -> c y n w", y=ROWS, n=B),
                              xg[:, 1 + ROWS * q:1 + ROWS * (q + 1), :, 1:W + 1], ACT.Copy).then_inc(flat_done, 1)

            def prepare(k):
                sc.wait_ge(conv_done, k + 1)
                cf = conv[:, :, :].rearrange("c a w -> c (a w)")
                sc.activation(gate[:, :], cf, ACT.Tanh, bias=bn_fold[:, 1:2], scale=bn_fold[:, 0:1])
                sc.activation(cf, cf, ACT.Identity, bias=bn_fold[:, 1:2], scale=bn_fold[:, 0:1]
                              ).then_inc(gate_done, 1)
                sc.wait_ge(off_mm, k + 1)
                sc.wait_ge(fix_done, k + 1)
                sc.sem_inc(act_waited, 1)
                sc.activation(off[:, bass.ds(k % 2, 1), :, :].rearrange("p s r o -> p (s r) o"), pair[0][:, :].rearrange("p (r o) -> p r o", r=ROWS)[:, :, 0:3 * GP],
                              ACT.Copy).then_inc(off_done, 1)
                sc.wait_ge(off_done, k + 1)
                sc.wait_ge(hats_used, k + 1)
                sc.sem_inc(act_waited, 1)
                for t in range(TAPS):
                    own(sc.activation(
                        hats[:, :, :, t].rearrange("p a (r g) -> p a r g", r=ROWS),
                        off[:, bass.ds(k % 2, 1), :, 0:2 * GP].rearrange("p s r (a g) -> p a (s r) g", a=2),
                        ACT.Abs, bias=tap_bias[:, t:t + 1]))
                own.wait()
                hf = hats[:, :, :, :].rearrange("p a g t -> p (a g t)")
                sc.activation(hf, hf, ACT.Relu, bias=tap_bias[:, TAPS:TAPS + 1], scale=-1.0).then_inc(hats_done, 1)
                sc.wait_ge(logits_done, k + 1)
                mf = mask[:, :, :].rearrange("p g q -> p (g q)")
                sc.activation(mf, mf, ACT.Exp).then_inc(exp_done, 1)

            def copy_out(k):
                sc.wait_ge(samp_tp, k + 1)
                sc.activation(samp_t[:, :, :, :].rearrange("c n r w -> c r n w"),
                              bank[2][:, :].rearrange("c (r n w) -> c r n w", r=ROWS, n=B),
                              ACT.Copy).then_inc(samp_t_done, 1)

            sc.wait_ge(fold_done, 1)
            sc.wait_ge(consts, 1)
            prepare(0)
            with sc.Fori(0, CHUNKS - 1) as k:
                own.enter(k, TAPS)
                prepare(k + 1)
                copy_out(k)
                own.leave(CHUNKS - 1)
            copy_out(CHUNKS - 1)

            def copy_t(i, done, out_sem, sums):
                sc.wait_ge(done, i + 1)
                n, h = i // 2, i % 2
                kw = {"accum_out": tok_sum[:, i:i + 1]} if sums else {}
                sc.activation(normed_t[:, n, h * 512:(h + 1) * 512], bank[i % 2][:, :], ACT.Copy, **kw
                              ).then_inc(out_sem, 1)

            for i in range(2 * B):
                copy_t(i, tp1, normed_t1, False)
            for i in range(2 * B):
                sc.wait_ge(key_mm, i + 1)
                sc.activation(keyed[:, i // 2, (i % 2) * 512:(i % 2 + 1) * 512], bank[2 + i % 2][:, :],
                              ACT.Copy, scale=float(C) ** -0.5).then_inc(keyed_done, 1)

            def exps(i, s):
                sc.wait_ge(max_done, i + 1)
                sc.activation(probs[:, s, :], pair[s][:, :], ACT.Exp, bias=neg_max[:, s:s + 1],
                              accum_out=den[:, s:s + 1]).then_inc(prob_done, 1)

            def half_probs(i):
                sc.wait_ge(probs_tp, 2 * i + 1)
                sc.activation(probs_t[:, 0:512], bank[0][:, :], ACT.Copy).then_inc(probs_t_a, 1)

            with sc.Fori(0, B * TILES // 2) as j:
                for s in range(2):
                    exps(j * 2 + s, s)
                    half_probs(j * 2 + s)

            for i in range(2 * B):
                copy_t(i, tp2, normed_t2, True)
            sc.wait_ge(normed_t2, 2 * B)
            sc.wait_ge(shifted_logits, 1)
            sc.activation(route[:, 1, :], route[:, 0, :], ACT.Exp).then_inc(r_exp, 1)
            sc.wait_ge(scaled_logits, 1)
            sc.activation(route[:, 5, :], route[:, 4, :], ACT.Exp).then_inc(r_exp, 1)
            sc.wait_ge(gap_done, 1)
            sc.activation(route_s[:, 9:10], route_s[:, 8:9], ACT.Exp).then_inc(r_exp, 1)
            for q in range(2 * B):
                sc.wait_ge(experts_in[q // 2], 96)
                if q >= 2:
                    sc.wait_ge(down_mm, 4 * (q - 1))
                for f in range(4):
                    sc.wait_ge(up_mm, 4 * q + f + 1)
                    s = 2 * (q // 2) + f // 2
                    sc.activation(hidden[:, q % 2, f, :], bank[f % 2][:, :], ACT.Gelu,
                                  bias=b1_sel[:, s, f % 2:f % 2 + 1]).then_inc(gelu_done, 1)

        @block.tensor
        def _(pe):
            pe.wait_ge(consts, 1)
            for i in range(2 * B):
                if i % 2 == 0:
                    pe.wait_ge(x_in[i // 2], 16)
                if i >= 4:
                    pe.wait_ge(xt_copied, i - 3)
                    pe.wait_ge(gn_in, i - 3)
                for t in range(4):
                    mm = pe.transpose(bank[i % 4][:, t * P:(t + 1) * P], res[:, 4 * i + t, :], ident[:, :])
                mm.then_inc(xt_done, 1)
            pe.wait_ge(w_in, 16 * N_W)
            pe.matmul(pair[0][:, 0:4 * C], ones[0:1, :], bias_rows[:, :, :].rearrange("a v c -> a (v c)"),
                      start=True, stop=True).then_inc(bias_mm, 1)
            pe.wait_ge(gn_in, 2 * B + 1)
            pe.matmul(pair[1][:, 0:B], group_mean[:, :], gn_mv[:, :, 0], start=True, stop=True).then_inc(gn_mm, 1)
            pe.wait_ge(gn_in, 2 * B + 2)
            pe.matmul(pair[1][:, 512:512 + B], group_mean[:, :], gn_v[:, 1, :], start=True, stop=True
                      ).then_inc(gn_mm, 1)
            for q in range(CHUNKS):
                pe.wait_ge(flat_done, q + 1)
                if q >= 2:
                    pe.wait_ge(proj_out, q - 1)
                for r in range(ROWS):
                    mm = pe.matmul(bank[q % 2][:, r * P:(r + 1) * P], flat_rows(q)[:, r * P:(r + 1) * P],
                                   in_w_sb[:, :], start=True, stop=True)
                mm.then_inc(proj_mm, 1)
            pe.sem_inc(prod_free, PROD)

            def offsets(k):
                pe.wait_ge(x1_done, k + 1)
                pe.wait_ge(fold_done, 1)
                if not isinstance(k, int) or k > 0:
                    pe.wait_ge(off_done, k)
                for r in range(ROWS):
                    o = pair[0][:, r * 256:r * 256 + 3 * GP]
                    pe.matmul(o, x1[:, r * P:(r + 1) * P], offmask_w[:, :], start=True, stop=False)
                    mm = pe.matmul(o, ones[0:1, :], offmask_b[:, :], start=False, stop=True)
                mm.then_inc(off_mm, 1)

            def count_far(k):
                pe.wait_ge(masks_done, k + 1)
                if not isinstance(k, int) or k > 0:
                    pe.wait_ge(far_done, k)
                pe.matmul(pair[1][:, 0:ROWS * GP], ones[:, :], far[:, :], start=True, stop=True).then_inc(far_mm, 1)

            def add_up(k, first, last):
                for i in range(first, last):
                    c, d = k + i // STENCIL, i % STENCIL
                    acc = banks[:, bass.ds(512 + (c % 2) * 1024, 512)]
                    pe.wait_ge(prod_done, c * STENCIL + d + 1)
                    pe.matmul(acc, ident[:, :], prod[:, d % PROD, :, :].rearrange("p g c -> p (g c)"),
                              start=(d == 0), stop=(d == STENCIL - 1)).then_inc(prod_free, 1)

            def samples_t(k):
                pe.wait_ge(samp_done, k + 1)
                for r in range(ROWS):
                    mm = pe.transpose(bank[2][:, r * P:(r + 1) * P], samp[:, r * P:(r + 1) * P], ident[:, :])
                mm.then_inc(samp_tp, 1)

            def project(k):
                pe.wait_ge(samp_t_done, k + 1)
                pe.wait_ge(res1_done, k + 1)
                for n in range(B):
                    mm = pe.matmul(bank[0][:, n * P:(n + 1) * P], samp_t[:, n, :, :].rearrange("c r w -> c (r w)"),
                                   out_w_sb[:, :], start=True, stop=True)
                mm.then_inc(conv_out, 1)

            pe.wait_ge(proj_out, CHUNKS)
            offsets(0)
            count_far(0)
            add_up(0, 0, AHEAD)
            with pe.Fori(0, CHUNKS - 1) as k:
                add_up(k, AHEAD, AT_OFFSETS)
                offsets(k + 1)
                add_up(k, AT_OFFSETS, AT_FAR)
                count_far(k + 1)
                add_up(k, AT_FAR, STENCIL + AT_COLLECT)
                samples_t(k)
                add_up(k, STENCIL + AT_COLLECT, STENCIL + AT_COLLECT + 3)
                project(k)
                add_up(k, STENCIL + AT_COLLECT + 3, STENCIL + AHEAD)
            add_up(CHUNKS - 1, AHEAD, STENCIL)
            samples_t(CHUNKS - 1)
            project(CHUNKS - 1)

            def transposes(i, normed_sem, tp_sem, copied):
                pe.wait_ge(normed_sem, i // 2 + 1)
                if i >= 2:
                    pe.wait_ge(copied, i - 1)
                for t in range(4):
                    mm = pe.transpose(bank[i % 2][:, t * P:(t + 1) * P], normed[:, 4 * i + t, :], ident[:, :])
                mm.then_inc(tp_sem, 1)

            for i in range(2 * B):
                transposes(i, normed1, tp1, normed_t1)
            for i in range(2 * B):
                pe.wait_ge(normed_t1, i + 1)
                if i >= 2:
                    pe.wait_ge(keyed_done, i - 1)
                pe.matmul(bank[2 + i % 2][:, :], attn_w_sb[:, :],
                          normed_t[:, i // 2, (i % 2) * 512:(i % 2 + 1) * 512], start=True, stop=True
                          ).then_inc(key_mm, 1)

            def scores(i):
                n, t = divmod(i, TILES)
                if i == 0:
                    pe.wait_ge(keyed_done, 2 * B)
                if i >= 2:
                    pe.wait_ge(prob_done, i - 1)
                for h in range(2):
                    mm = pe.matmul(pair[i % 2][:, h * 512:(h + 1) * 512], keyed[:, n, t * P:(t + 1) * P],
                                   normed_t[:, n, h * 512:(h + 1) * 512], start=True, stop=True)
                mm.then_inc(score_mm, 1)

            def mix(i):
                n = i // TILES
                pe.wait_ge(prob_done, i + 1)
                for h in range(2):
                    if i >= 1:
                        pe.wait_ge((probs_t_a, probs_t_v)[h], i)
                    for m in range(4):
                        mm = pe.transpose(bank[h][:, m * P:(m + 1) * P],
                                          probs[:, i % 2, (4 * h + m) * P:(4 * h + m + 1) * P], ident[:, :])
                    mm.then_inc(probs_tp, 1)
                pe.wait_ge(probs_t_a, i + 1)
                pe.wait_ge(probs_t_v, i + 1)
                if i >= 1:
                    pe.wait_ge(res2_done, i)
                for m in range(TILES):
                    mm = pe.matmul(bank[2][:, 0:C], probs_t[:, m * P:(m + 1) * P], normed[:, n * TILES + m, :],
                                   start=(m == 0), stop=(m == TILES - 1))
                mm.then_inc(mix_mm, 1)

            for i in range(B * TILES + 1):
                if i < B * TILES:
                    scores(i)
                if i >= 1:
                    mix(i - 1)

            for i in range(2 * B):
                transposes(i, normed2, tp2, normed_t2)
            pe.wait_ge(mean_done, 1)
            pe.matmul(bank[2][0:B, 0:E], tok_mean[:, :], wr_sb[:, :], start=True, stop=False)
            pe.matmul(bank[2][0:B, 0:E], ones[0:1, 0:B], br_sb[:, :], start=False, stop=True).then_inc(logit_mm, 1)
            pe.wait_ge(routing_done, 1)
            pe.matmul(bank[2][0:B, 0:E], ones[0:B, 0:B], route[:, 2, :], start=True, stop=True).then_inc(load_mm, 1)
            pe.wait_ge(picked, 1)
            pe.matmul(bank[2][:, 0:2 * B], ones[0:B, :], pick_w[:, :, :].rearrange("k n j -> k (n j)"),
                      start=True, stop=True).then_inc(spread_mm, 1)
            pe.matmul(bank[3][0:E, :], route[:, 12, :], cols4[:, :, :].rearrange("k n t -> k (n t)"),
                      start=True, stop=True).then_inc(spread_mm, 1)

            def up(q):
                n = q // 2
                if q % 2 == 0:
                    pe.wait_ge(experts_in[n], 96)
                for f in range(4):
                    i = 4 * q + f
                    if i >= 2:
                        pe.wait_ge(gelu_done, i - 1)
                    pe.matmul(bank[f % 2][:, :], w1_sel[:, 2 * n + f // 2, (f % 2) * P:(f % 2 + 1) * P],
                              normed_t[:, n, (q % 2) * 512:(q % 2 + 1) * 512], start=True, stop=True
                              ).then_inc(up_mm, 1)

            def down(q):
                n = q // 2
                pe.wait_ge(gelu_done, 4 * (q + 1))
                pe.wait_ge(w2_scaled, n + 1)
                for t in range(4):
                    i = 4 * q + t
                    if i >= 2:
                        pe.wait_ge(y_done, i - 1)
                    o = bank[2 + t % 2][:, 0:C]
                    pe.matmul(o, dense_t[:, n, :], b2_sb[:, :], start=True, stop=False)
                    for f in range(4):
                        mm = pe.matmul(o, hidden[:, q % 2, f, t * P:(t + 1) * P],
                                       w2_sel[:, 2 * n + f // 2, f % 2, :], start=False, stop=(f == 3))
                    mm.then_inc(down_mm, 1)

            for q in range(2 * B + 1):
                if q == 1:
                    pe.wait_ge(spread_done, 1)
                if q < 2 * B:
                    up(q)
                if q >= 1:
                    down(q - 1)

        @block.gpsimd
        def _(gp):
            own = Own(gp, pool)
            gp.memset(zero_rows, 0.0).then_inc(zeros_set, 1)
            gp.memset(xg[:, :, :, :], 0.0).then_inc(zeros_set, 1)
            own(gp.memset(ident[:, :], 0.0))
            own(gp.memset(ones[:, :], 1.0))
            own(gp.memset(group_mean[:, :], 1.0 / GN_C))
            own.wait()
            own(gp.affine_select(out=ident[:, :], in_=ident[:, :], compare_op=ALU.not_equal, fill=1.0, base=0,
                                 pattern=[[-1, P]], channel_multiplier=1))
            gm = group_mean[:, :].rearrange("p (g j) -> p g j", j=GN_C)
            own.link(gp.affine_select(out=gm, in_=gm, compare_op=ALU.is_ge, fill=0.0, base=0,
                                      pattern=[[-GN_C, P // GN_C], [0, GN_C]], channel_multiplier=1))
            own.link(gp.affine_select(out=gm, in_=gm, compare_op=ALU.is_ge, fill=0.0, base=GN_C - 1,
                                      pattern=[[GN_C, P // GN_C], [0, GN_C]], channel_multiplier=-1))
            for t in range(TAPS):
                gp.memset(tap_bias[:, t:t + 1], float(REACH - t))
            gp.memset(tap_bias[:, TAPS:TAPS + 1], 1.0)
            own(gp.memset(zero_col[:, :], 0.0))
            own.link(gp.memset(neg_half[:, :], -0.5))
            own.link(gp.iota(rank[:, :], pattern=[[-1, E]], base=E, channel_multiplier=0,
                             allow_small_or_imprecise_dtypes=True))
            own.link(gp.tensor_copy(cols4[:, :, :], ones[0:B, :].unsqueeze(1).to_broadcast([B, B, P])))
            gp.affine_select(out=cols4[:, :, :], in_=cols4[:, :, :], compare_op=ALU.is_equal, fill=0.0, base=0,
                             pattern=[[-1, B], [0, P]], channel_multiplier=1).then_inc(consts, 1)

            for n in range(B):
                own.link(gp.iota(grid_i[32 * n:32 * n + 32, 0:GP].rearrange("p (g a b) -> p g a b", g=G, a=3),
                            pattern=[[0, G], [1, 3], [0, 3]], base=-1, channel_multiplier=1))
                own.link(gp.iota(part_i[32 * n:32 * n + 32, :], pattern=[[0, 1]],
                            base=(n * WP + PAD) * HP * G + PAD * G, channel_multiplier=0))
            own.link(gp.iota(grid_i[:, GP:2 * GP].rearrange("p (g a b) -> p g a b", g=G, a=3),
                        pattern=[[0, G], [0, 3], [1, 3]], base=-1, channel_multiplier=0))
            own.link(gp.iota(low_i[:, 0:GP].rearrange("p (g a) -> p g a", g=G),
                        pattern=[[1, G], [0, PTS]], base=0, channel_multiplier=0))
            own.link(gp.tensor_copy(grid[:, :], grid_i[:, :]))
            own.link(gp.tensor_copy(part_f[:, :], part_i[:, :]))
            own.link(gp.tensor_copy(cell0[:, :], low_i[:, 0:GP]))
            own.link(gp.tensor_scalar(cell0[:, :], cell0[:, :], part_f[:, 0:1], None, ALU.add))

            gp.wait_ge(bn_var, 1)
            gp.tensor_tensor(bn_fold[:, 3:4], bn_fold[:, 2:3], neg_half[:, 0:1], ALU.pow).then_inc(bn_rstd, 1)
            gp.wait_ge(gn_var, 1)
            gp.tensor_tensor(gn_v[:, 3, :], gn_v[:, 2, :], neg_half[:, 0:B], ALU.pow).then_inc(gn_rstd, 1)

            gp.memset(stencil[:, 0, :], 0.0).then_inc(stencil_clear, 1)
            gp.wait_ge(xt_done, 2 * B)
            gp.tensor_tensor(res[:, :, :], res[:, :, :], bias_all[:, 1:2, :].to_broadcast([P, B * TILES, C]), ALU.add
                             ).then_inc(res_biased, 1)

            def wait(what, count):
                gp.wait_ge(what, count)
                gp.sem_inc(waited, 1)

            own.alone = waited
            gp.sem_inc(fix_done, 2)
            ROW_STEPS, POINT_STEPS = 32, 7
            for q in range(PCS):
                wait(padded_out[q], 16)
            wait(pads_out, 16 * N_PADS)
            gp.memset(stencil[:, 1, :], 0.0).then_inc(stencil_clear, 1)
            own(gp.memset(fix[:, :, :], 0.0))
            start = own.n
            per_row = 1 + ROW_STEPS + GP * POINT_STEPS
            per_chunk = ROWS * per_row + 1
            table = padded.rearrange("n w y (g c) -> (n w y g) c", g=G)
            with gp.Fori(0, CHUNKS) as k:
                wait(off_done, k + 1)
                wait(masks_done, k + 1)
                wait(far_done, k + 1)
                with gp.Fori(0, ROWS) as r:
                    row0 = k * per_chunk + start + r * per_row
                    any_far = gp.value_load(far_groups[0:1, bass.ds(k % 2, 1), bass.ds(r + ROWS * G, 1)]
                                            .rearrange("a s g -> a (s g)"), min_val=0, max_val=P * GP)
                    with gp.If(any_far > 0):
                        own.base, own.n = row0, 0
                        own(gp.tensor_copy(pos[:, :], off[:, bass.ds(k % 2, 1), bass.ds(r, 1), 0:2 * GP]
                                           .rearrange("p s r o -> p (s r o)")))
                        own(gp.tensor_copy(far_m[:, :], mask_far[:, bass.ds(k % 2, 1), bass.ds(r * GP, GP)]
                                           .rearrange("p s o -> p (s o)")))
                        own.wait()
                        own.link(gp.tensor_tensor(pos[:, :], pos[:, :], grid[:, :], ALU.add))
                        own.link(gp.tensor_scalar(pos[:, :], pos[:, :], 33.0, -2.0, ALU.min, ALU.max))
                        own.link(gp.tensor_copy(low_i[:, :], pos[:, :]))
                        own.link(gp.tensor_copy(low[:, :], low_i[:, :]))
                        own.link(gp.tensor_tensor(over[:, :], low[:, :], pos[:, :], ALU.subtract))
                        own.link(gp.tensor_scalar(over[:, :], over[:, :], 0.0, None, ALU.is_gt))
                        own.link(gp.tensor_tensor(low[:, :], low[:, :], over[:, :], ALU.subtract))
                        own.link(gp.tensor_tensor(frac[:, 1, :], pos[:, :], low[:, :], ALU.subtract))
                        own.link(gp.tensor_scalar(frac[:, 0, :], frac[:, 1, :], -1.0, 1.0, ALU.mult, ALU.add))
                        own(gp.tensor_scalar(over[:, :], low[:, :], 1.0, 1.0, ALU.add, ALU.mult))
                        own.wait()
                        for a in range(2):
                            own(gp.tensor_scalar(corner[:, a, :], (low, over)[a][:, :], float(W - 1), 0.0,
                                                 ALU.min, ALU.max))
                        own.wait()
                        for a in range(2):
                            own(gp.tensor_tensor(inside[:, a, :], corner[:, a, :], (low, over)[a][:, :],
                                                 ALU.subtract))
                        own.wait()
                        own.link(gp.tensor_scalar(inside[:, :, :], inside[:, :, :], 0.0, None, ALU.is_equal))
                        own.link(gp.tensor_tensor(frac[:, :, :], frac[:, :, :], inside[:, :, :], ALU.mult))
                        own(gp.tensor_scalar(corner[:, :, 0:GP], corner[:, :, 0:GP], float(HP * G), 0.0,
                                             ALU.mult, ALU.add))
                        own(gp.tensor_scalar(corner[:, :, GP:], corner[:, :, GP:], float(G), 0.0, ALU.mult, ALU.add))
                        own.wait()
                        for a in range(2):
                            own.link(gp.tensor_tensor(cell_f[:, :], corner[:, a, 0:GP], cell0[:, :], ALU.add))
                            own.link(gp.tensor_tensor(cell_t[:, :], far_m[:, :], frac[:, a, 0:GP], ALU.mult))
                            for b in range(2):
                                own(gp.tensor_tensor(cells[:, :, 2 * a + b], cell_f[:, :], corner[:, b, GP:], ALU.add))
                                own(gp.tensor_tensor(cell_w[:, :, 2 * a + b], cell_t[:, :], frac[:, b, GP:], ALU.mult))
                            own.wait()
                        assert own.n == ROW_STEPS, own.n
                        with gp.Fori(0, G) as g:
                            in_group = gp.value_load(far_groups[0:1, bass.ds(k % 2, 1), bass.ds(r * G + g, 1)]
                                                     .rearrange("a s g -> a (s g)"), min_val=0, max_val=P * PTS)
                            with gp.If(in_group > 0):
                                with gp.Fori(0, PTS) as q:
                                    point = g * PTS + q
                                    count = gp.value_load(far_points[0:1, bass.ds(k % 2, 1), bass.ds(r * GP + point, 1)]
                                                          .rearrange("a s g -> a (s g)"), min_val=0, max_val=P)
                                    own.base, own.n = row0 + (ROW_STEPS + point * POINT_STEPS), 0
                                    with gp.If(count > 0):
                                        own(gp.tensor_copy(cell_now[:, :], cells[:, bass.ds(point, 1), :]
                                                           .rearrange("p a b -> p (a b)")))
                                        own(gp.tensor_copy(w_now[:, :], cell_w[:, bass.ds(point, 1), :]
                                                           .rearrange("p a b -> p (a b)")))
                                        own.wait()
                                        for a in range(4):
                                            gp.indirect_dma_start(
                                                out=got[:, a, :], out_offset=None, in_=table,
                                                in_offset=bass.IndirectOffsetOnAxis(ap=cell_now[:, a:a + 1], axis=0)
                                            ).then_inc(gathered, 16)
                                        gp.wait_ge(gathered, 64)
                                        gp.inc_swdge_sem([gathered], [64], mode="sub")
                                        own.link(gp.tensor_tensor(got[:, :, :], got[:, :, :],
                                                                  w_now[:, :].unsqueeze(2).to_broadcast([P, 4, CG]), ALU.mult))
                                        to = fix[:, bass.ds(r * G + g, 1), :].rearrange("p a c -> p (a c)")
                                        for a in range(4):
                                            own.link(gp.tensor_tensor(to, to, got[:, a, :], ALU.add))
                                        assert own.n == POINT_STEPS
                                    with gp.Else():
                                        gp.sem_inc(pool, POINT_STEPS)
                                gp.nop()
                            with gp.Else():
                                gp.sem_inc(pool, PTS * POINT_STEPS)
                        gp.nop()
                    with gp.Else():
                        gp.sem_inc(pool, per_row - 1)
                    own.base, own.n = row0 + (per_row - 1), 0
                    own.link(gp.tensor_scalar(grid[:, GP:], grid[:, GP:], 1.0, 0.0, ALU.add, ALU.add))
                own.base, own.n = k * per_chunk + (start + ROWS * per_row), 0
                own.wait()
                gp.sem_inc(fix_done, 1)
                wait(samp_done, k + 1)
                own.link(gp.memset(fix[:, :, :], 0.0))
                gp.tensor_copy(stencil[:, bass.ds(k % 2, 1), :].rearrange("p s g -> p (s g)"),
                               zero_col[:, 0:1].to_broadcast([P, ROWS * G * STENCIL])).then_inc(stencil_clear, 1)
            own.base, own.n, own.alone = 0, start + CHUNKS * per_chunk, None

            for done, out_sem in ((var1, rstd1), (var2, rstd2)):
                for n in range(B):
                    gp.wait_ge(done, n + 1)
                    gp.tensor_tensor(rstd[:, n * TILES:(n + 1) * TILES], mv[:, n * TILES:(n + 1) * TILES, 1],
                                     neg_half[:, 0:TILES], ALU.pow).then_inc(out_sem, 1)
            for q in range(2 * B):
                gp.wait_ge(var3, q + 1)
                gp.tensor_tensor(rstd[:, 4 * q:4 * q + 4], mv[:, 4 * q:4 * q + 4, 1], neg_half[:, 0:4], ALU.pow
                                 ).then_inc(rstd3, 1)

        @block.vector
        def _(ve):
            own = Own(ve, dve)
            for i in range(2 * B):
                ve.wait_ge(xt_done, i + 1)
                ve.bn_stats(gn_stats[:, i // 2, i % 2, :], bank[i % 4][:, :]).then_inc(gn_in, 1)
            ve.wait_ge(gn_in, 2 * B)
            for n in range(B):
                last = ve.bn_aggr(gn_mv[:, n, :], gn_stats[:, n, :, :].rearrange("p a b -> p (a b)"))
            last.then_inc(gn_in, 1)
            ve.wait_ge(w_in, 16 * N_W)
            for src, dst in ((off_raw, offmask_w), (off_b_raw, offmask_b)):
                own(ve.tensor_copy(dst[:, 0:2 * GP].rearrange("p (a g) -> p a g", a=2),
                                   src[:, :].rearrange("p (g a) -> p a g", a=2)))
            ve.tensor_scalar(bn_fold[:, 2:3], bn_sb[:, 3:4], BN_EPS, None, ALU.add).then_inc(bn_var, 1)
            ve.wait_ge(bias_mm, 1)
            own(ve.tensor_copy(bias_all[:, :, :].rearrange("p v c -> p (v c)"), pair[0][:, 0:4 * C]))
            ve.wait_ge(gn_mm, 1)
            own.link(ve.tensor_copy(gn_v[:, 0, :], pair[1][:, 0:B]))
            own.link(ve.tensor_tensor(gn_v[:, 2, :], gn_mv[:, :, 0], gn_v[:, 0, :], ALU.subtract))
            own.link(ve.tensor_tensor(gn_v[:, 2, :], gn_v[:, 2, :], gn_v[:, 2, :], ALU.mult))
            ve.tensor_tensor(gn_v[:, 1, :], gn_v[:, 2, :], gn_mv[:, :, 1], ALU.add).then_inc(gn_in, 1)
            ve.wait_ge(gn_mm, 2)
            ve.tensor_scalar(gn_v[:, 2, :], pair[1][:, 512:512 + B], GN_EPS, None, ALU.add).then_inc(gn_var, 1)
            ve.wait_ge(bn_rstd, 1)
            own.link(ve.tensor_tensor(bn_fold[:, 0:1], bn_sb[:, 0:1], bn_fold[:, 3:4], ALU.mult))
            own.link(ve.tensor_tensor(bn_fold[:, 1:2], bn_sb[:, 2:3], bn_fold[:, 0:1], ALU.mult))
            own.link(ve.tensor_tensor(bn_fold[:, 1:2], bn_sb[:, 1:2], bn_fold[:, 1:2], ALU.subtract))
            ve.tensor_scalar(bn_fold[:, 0:2], bn_fold[:, 0:2], 0.5, None, ALU.mult).then_inc(fold_done, 1)
            ve.wait_ge(gn_rstd, 1)
            ve.wait_ge(xt_copied, 2 * B)
            for n in range(B):
                v = xg[:, 1:H + 1, n, 1:W + 1]
                ve.tensor_scalar(v, v, gn_v[:, 0, n:n + 1], gn_v[:, 3, n:n + 1], ALU.subtract, ALU.mult
                                 ).then_inc(xg_ready, 1)
            for q in range(CHUNKS):
                ve.wait_ge(proj_mm, q + 1)
                ve.tensor_tensor(stage[:, ROWS * q:ROWS * (q + 1), :],
                                 bank[q % 2][:, :].rearrange("p (r c) -> p r c", r=ROWS),
                                 bias_all[:, 0:1, :].to_broadcast([P, ROWS, C]), ALU.add).then_inc(proj_out, 1)

            def nothing(n):
                pass

            def convolve(k, fill):
                for t in range(9):
                    src = xg_rows[:, bass.ds((k * ROWS + t // 3) * B, ROWS * B), t % 3:t % 3 + W]
                    if t == 0:
                        own(ve.tensor_scalar(conv[:, :, :], src, dw_sb[:, 0:1], None, ALU.mult))
                    elif t < 8:
                        own(ve.scalar_tensor_tensor(conv[:, :, :], src, dw_sb[:, t:t + 1], conv[:, :, :],
                                                    ALU.mult, ALU.add))
                    else:
                        ve.scalar_tensor_tensor(conv[:, :, :], src, dw_sb[:, t:t + 1], conv[:, :, :],
                                                ALU.mult, ALU.add).then_inc(conv_done, 1)
                    if t < 8:
                        fill(1)
                        own.wait()

            def finish_silu(k):
                ve.wait_ge(gate_done, k + 1)
                ve.scalar_tensor_tensor(x1[:, :], gate[:, :], 1.0, conv[:, :, :].rearrange("c a w -> c (a w)"),
                                        ALU.add, ALU.mult).then_inc(x1_done, 1)

            def mask_logits(k, fill):
                ve.wait_ge(off_done, k + 1)
                now = off[:, bass.ds(k % 2, 1), :, :].rearrange("p s r o -> p (s r) o")
                own(ve.tensor_tensor(far_xy[:, :, :], now[:, :, 0:2 * GP], now[:, :, 0:2 * GP], ALU.mult))
                lg = now[:, :, 2 * GP:].rearrange("p r (g q) -> p r g q", g=G)
                own(ve.tensor_reduce(row_max[:, :].rearrange("p (r g) -> p r g", r=ROWS), lg, AX.X, ALU.max))
                fill(1)
                own.wait()
                own(ve.tensor_tensor(far[:, :].rearrange("p (r g) -> p r g", r=ROWS), far_xy[:, :, 0:GP],
                                     far_xy[:, :, GP:], ALU.max))
                for r in range(ROWS):
                    last = ve.tensor_tensor(mask[:, r * G:(r + 1) * G, :], lg[:, r],
                                            row_max[:, r * G:(r + 1) * G].unsqueeze(2).to_broadcast([P, G, PTS]),
                                            ALU.subtract)
                last.then_inc(logits_done, 1)
                own.wait()
                own(ve.tensor_scalar(far[:, :], far[:, :], float(REACH) ** 2, None, ALU.is_gt))

            def masks(k, fill):
                mf = mask[:, :, :].rearrange("p g q -> p (g q)")
                ve.wait_ge(exp_done, k + 1)
                own(ve.tensor_reduce(row_sum[:, :], mask[:, :, :], AX.X, ALU.add))
                fill(1)
                own.wait()
                own.link(ve.reciprocal(row_sum[:, :], row_sum[:, :]))
                own(ve.tensor_tensor(mask[:, :, :], mask[:, :, :],
                                     row_sum[:, :].unsqueeze(2).to_broadcast([P, ROWS * G, PTS]), ALU.mult))
                fill(1)
                own.wait()
                far_part = mask_far[:, bass.ds(k % 2, 1), :].rearrange("p s o -> p (s o)")
                own.link(ve.tensor_tensor(far_part, far[:, :], mf, ALU.mult))
                own.link(ve.tensor_tensor(mf, mf, far_part, ALU.subtract))
                ve.sem_inc(masks_done, 1)
                ve.wait_ge(hats_done, k + 1)
                own(ve.tensor_tensor(hats[:, 1, :, :], hats[:, 1, :, :],
                                     mf.unsqueeze(2).to_broadcast([P, ROWS * GP, TAPS]), ALU.mult))

            def far_counts(k, fill):
                now = bass.ds(k % 2, 1)
                ve.wait_ge(far_mm, k + 1)
                own(ve.tensor_copy(far_points[:, now, :].rearrange("a s o -> a (s o)"), pair[1][0:1, 0:ROWS * GP]))
                own(ve.tensor_reduce(far_sums[:, 0:ROWS * G],
                                     pair[1][0:1, 0:ROWS * GP].rearrange("p (g q) -> p g q", q=PTS), AX.X, ALU.add))
                own(ve.tensor_reduce(far_sums[:, ROWS * G:],
                                     pair[1][0:1, 0:ROWS * GP].rearrange("p (r o) -> p r o", r=ROWS), AX.X, ALU.add))
                fill(1)
                own.wait()
                ve.tensor_copy(far_groups[:, now, :].rearrange("a s o -> a (s o)"), far_sums[:, :]).then_inc(far_done, 1)

            def stencils(k, fill):
                ve.wait_ge(stencil_clear, k + 1)
                hx = hats[:, 0, :, :].rearrange("p (g q) t -> p g q t", q=PTS)
                hy = hats[:, 1, :, :].rearrange("p (g q) t -> p g q t", q=PTS)
                now = stencil_of[:, bass.ds(k % 2, 1), :, :, :].rearrange("p s g a b -> p (s g) a b")
                for q in range(PTS):
                    kx, ky = q // 3, q % 3
                    full = [P, ROWS * G, TAPS, TAPS]
                    own.wait()
                    own(ve.tensor_tensor(outer[:, :, :, :], hy[:, :, q, :].unsqueeze(3).to_broadcast(full),
                                         hx[:, :, q, :].unsqueeze(2).to_broadcast(full), ALU.mult))
                    fill(1)
                    own.wait()
                    to = now[:, :, ky:ky + TAPS, kx:kx + TAPS]
                    own(ve.tensor_tensor(to, to, outer[:, :, :, :], ALU.add))
                    fill(1 if q < PTS - 1 else 0)
                own.wait()
                ve.sem_inc(hats_used, 1)

            def products(k, first, last):
                for i in range(first, last):
                    c, d = k + i // STENCIL, i % STENCIL
                    dy, dx = divmod(d, WIN)
                    if d == 0:
                        ve.wait_ge(rows_ready, c + 1)
                    ve.wait_ge(prod_free, c * STENCIL + d + 1)
                    ve.tensor_tensor(prod[:, d % PROD, :, :],
                                     shifted[:, dx, bass.ds(((c % HALF) * ROWS + dy) * G, ROWS * G), :],
                                     stencil_of[:, bass.ds(c % 2, 1), :, dy, dx].rearrange("p s g -> p (s g)")
                                     .unsqueeze(2).to_broadcast([P, ROWS * G, CG]), ALU.mult).then_inc(prod_done, 1)

            def collect(k):
                ve.wait_ge(prod_free, k * STENCIL + STENCIL + PROD)
                ve.sem_inc(rows_used, 1)
                ve.wait_ge(fix_done, k + 3)
                ve.tensor_tensor(samp[:, :], banks[:, bass.ds(512 + (k % 2) * 1024, 512)],
                                 fix[:, :, :].rearrange("p g c -> p (g c)"), ALU.add).then_inc(samp_done, 1)

            def residual(k):
                ve.wait_ge(conv_out, k + 1)
                to = res[:, :, :].rearrange("p (n k) c -> p n k c", n=B)[:, :, bass.ds(k, 1), :] \
                    .rearrange("p n k c -> p n (k c)")
                ve.tensor_tensor(to, bank[0][:, :].rearrange("p (n c) -> p n c", n=B), to, ALU.add
                                 ).then_inc(res1_done, 1)

            own.wait()
            ve.sem_inc(hats_used, 1)
            ve.sem_inc(res1_done, 1)
            n0 = own.n
            convolve(0, nothing)
            finish_silu(0)
            mask_logits(0, nothing)
            masks(0, nothing)
            far_counts(0, nothing)
            stencils(0, nothing)
            per = own.n - n0
            products(0, 0, AHEAD)
            ve.wait_ge(res_biased, 1)
            with ve.Fori(0, CHUNKS - 1) as k:
                own.enter(k, per)
                place = [AHEAD]

                def fill(n):
                    products(k, place[0], place[0] + n)
                    place[0] += n

                convolve(k + 1, fill)
                fill(2)
                finish_silu(k + 1)
                fill(6)
                mask_logits(k + 1, fill)
                fill(5)
                masks(k + 1, fill)
                stencils(k + 1, fill)
                far_counts(k + 1, fill)
                fill(STENCIL + AT_COLLECT - place[0])
                collect(k)
                fill(STENCIL + AHEAD - place[0])
                residual(k)
                own.leave(CHUNKS - 1)
            products(CHUNKS - 1, AHEAD, STENCIL)
            collect(CHUNKS - 1)
            residual(CHUNKS - 1)
            ve.wait_ge(res1_done, CHUNKS + 1)

            def normalise(n, src, done, rstd_sem, normed_sem):
                for t in range(TILES):
                    own(ve.bn_stats(stats[:, t, :], src[:, n * TILES + t, :]))
                own.wait()
                for t in range(TILES):
                    own(ve.bn_aggr(mv[:, n * TILES + t, :], stats[:, t, :]))
                own.wait()
                v = mv[:, n * TILES:(n + 1) * TILES, 1]
                ve.tensor_scalar(v, v, LN_EPS, None, ALU.add).then_inc(done, 1)
                ve.wait_ge(rstd_sem, n + 1)
                for t in range(n * TILES, (n + 1) * TILES):
                    last = ve.tensor_scalar(normed[:, t, :], src[:, t, :], mv[:, t, 0:1], rstd[:, t:t + 1],
                                            ALU.subtract, ALU.mult)
                last.then_inc(normed_sem, 1)

            for n in range(B):
                normalise(n, res, var1, rstd1, normed1)

            def maxima(i, s):
                ve.wait_ge(score_mm, i + 1)
                ve.tensor_reduce(neg_max[:, s:s + 1], pair[s][:, :], AX.X, ALU.max, negate=True).then_inc(max_done, 1)

            def half_probs(i):
                ve.wait_ge(probs_tp, 2 * i + 2)
                ve.tensor_copy(probs_t[:, 512:1024], bank[1][:, :]).then_inc(probs_t_v, 1)

            def add_mix(i, s):
                ve.wait_ge(prob_done, i + 1)
                own(ve.reciprocal(rden[:, s:s + 1], den[:, s:s + 1]))
                ve.wait_ge(mix_mm, i + 1)
                own.wait()
                to = res[:, bass.ds(i, 1), :].rearrange("p a c -> p (a c)")
                ve.scalar_tensor_tensor(to, bank[2][:, 0:C], rden[:, s:s + 1], to, ALU.mult, ALU.add
                                        ).then_inc(res2_done, 1)

            maxima(0, 0)
            with ve.Fori(0, B * TILES // 2 - 1) as j:
                own.enter(j, 2)
                for s in range(2):
                    maxima(j * 2 + s + 1, 1 - s)
                    half_probs(j * 2 + s)
                    add_mix(j * 2 + s, s)
                own.leave(B * TILES // 2 - 1)
            maxima(B * TILES - 1, 1)
            for s in range(2):
                half_probs(B * TILES - 2 + s)
                add_mix(B * TILES - 2 + s, s)
            ve.wait_ge(res2_done, B * TILES)

            for n in range(B):
                normalise(n, res, var2, rstd2, normed2)

            ve.wait_ge(normed_t2, 2 * B)
            own.link(ve.tensor_reduce(tok_mean[:, :], tok_sum[:, :].rearrange("p (n h) -> p n h", h=2), AX.X, ALU.add))
            ve.tensor_scalar(tok_mean[:, :], tok_mean[:, :], 1.0 / TOK, None, ALU.mult).then_inc(mean_done, 1)
            ve.wait_ge(logit_mm, 1)
            own.link(ve.tensor_copy(route[:, 3, :], bank[2][0:B, 0:E]))
            own.link(ve.tensor_reduce(route_s[:, 0:1], route[:, 3, :], AX.X, ALU.max))
            ve.tensor_scalar(route[:, 0, :], route[:, 3, :], route_s[:, 0:1], None, ALU.subtract
                             ).then_inc(shifted_logits, 1)
            ve.wait_ge(r_exp, 1)
            own.link(ve.tensor_reduce(route_s[:, 1:2], route[:, 1, :], AX.X, ALU.add))
            own.link(ve.reciprocal(route_s[:, 2:3], route_s[:, 1:2]))
            ve.tensor_scalar(route[:, 2, :], route[:, 1, :], route_s[:, 2:3], None, ALU.mult).then_inc(routing_done, 1)
            ve.wait_ge(load_mm, 1)
            own.link(ve.tensor_scalar(route[:, 6, :], bank[2][0:B, 0:E], float(TOK), float(CAPACITY), ALU.mult, ALU.max))
            own.link(ve.reciprocal(route[:, 7, :], route[:, 6, :]))
            own.link(ve.scalar_tensor_tensor(route[:, 8, :], route[:, 7, :], float(CAPACITY), route[:, 2, :],
                                             ALU.mult, ALU.mult))
            own.link(ve.tensor_reduce(route_s[:, 3:4], route[:, 8, :], AX.X, ALU.max))
            ve.tensor_scalar(route[:, 4, :], route[:, 8, :], route_s[:, 3:4], None, ALU.subtract
                             ).then_inc(scaled_logits, 1)
            ve.wait_ge(r_exp, 2)
            own.link(ve.tensor_reduce(route_s[:, 4:5], route[:, 5, :], AX.X, ALU.add))
            own.link(ve.reciprocal(route_s[:, 5:6], route_s[:, 4:5]))
            own.link(ve.tensor_scalar(route[:, 9, :], route[:, 5, :], route_s[:, 5:6], None, ALU.mult))
            for j in range(2):
                w = route[:, 9, :]
                own.link(ve.tensor_reduce(route_s[:, 6 + j:7 + j], w, AX.X, ALU.max))
                own.link(ve.scalar_tensor_tensor(route[:, 13, :], w, route_s[:, 6 + j:7 + j], rank[:, :],
                                                 ALU.is_equal, ALU.mult))
                own.link(ve.tensor_reduce(route_s[:, 12 + j:13 + j], route[:, 13, :], AX.X, ALU.max))
                own.link(ve.tensor_scalar(route[:, 10 + j, :], rank[:, :], route_s[:, 12 + j:13 + j], None, ALU.is_equal))
                own.link(ve.tensor_scalar(route_i[:, j:j + 1], route_s[:, 12 + j:13 + j], -1.0, float(E),
                                          ALU.mult, ALU.add))
                if j == 0:
                    own.link(ve.scalar_tensor_tensor(w, route[:, 10, :], -BIG_SHIFT, w, ALU.mult, ALU.add))
            ve.tensor_tensor(route_s[:, 8:9], route_s[:, 7:8], route_s[:, 6:7], ALU.subtract).then_inc(gap_done, 1)
            ve.wait_ge(r_exp, 3)
            own.link(ve.tensor_scalar(route_s[:, 10:11], route_s[:, 9:10], 1.0, None, ALU.add))
            own.link(ve.reciprocal(route_s[:, 10:11], route_s[:, 10:11]))
            own.link(ve.tensor_tensor(route_s[:, 11:12], route_s[:, 9:10], route_s[:, 10:11], ALU.mult))
            own.link(ve.tensor_scalar(route[:, 14, :], route[:, 11, :], route_s[:, 11:12], None, ALU.mult))
            own.link(ve.scalar_tensor_tensor(route[:, 12, :], route[:, 10, :], route_s[:, 10:11], route[:, 14, :],
                                             ALU.mult, ALU.add))
            own.link(ve.tensor_copy(pick_w[:, :, :], route_s[:, 10:12].unsqueeze(1).to_broadcast([B, B, 2])))
            ve.tensor_tensor(pick_w[:, :, :], pick_w[:, :, :], ident[0:B, 0:B].unsqueeze(2).to_broadcast([B, B, 2]),
                             ALU.mult).then_inc(picked, 1)
            ve.wait_ge(spread_mm, 2)
            own.link(ve.tensor_copy(weight_all[:, :, :].rearrange("p n j -> p (n j)"), bank[2][:, 0:2 * B]))
            ve.tensor_copy(dense_t[:, :, :].rearrange("e n t -> e (n t)"), bank[3][0:E, :]).then_inc(spread_done, 1)

            for q in range(2 * B):
                if q % 2 == 0:
                    n = q // 2
                    ve.wait_ge(experts_in[n], 96)
                    for j in range(2):
                        last = ve.tensor_scalar(w2_sel[:, 2 * n + j, :, :], w2_sel[:, 2 * n + j, :, :],
                                                weight_all[:, n, j:j + 1], None, ALU.mult)
                    last.then_inc(w2_scaled, 1)
                if q >= 1:
                    ve.wait_ge(res3_done, q)
                for t in range(4):
                    ve.wait_ge(down_mm, 4 * q + t + 1)
                    ve.tensor_tensor(y_new[:, t, :], bank[2 + t % 2][:, 0:C], normed[:, 4 * q + t, :], ALU.add
                                     ).then_inc(y_done, 1)
                    ve.wait_ge(y_done, 4 * q + t + 1)
                    own(ve.bn_stats(stats[:, t, :], y_new[:, t, :]))
                own.wait()
                for t in range(4):
                    own(ve.bn_aggr(mv[:, 4 * q + t, :], stats[:, t, :]))
                own.wait()
                v = mv[:, 4 * q:4 * q + 4, 1]
                ve.tensor_scalar(v, v, LN_EPS, None, ALU.add).then_inc(var3, 1)
                ve.wait_ge(rstd3, q + 1)
                for t in range(4):
                    own(ve.tensor_scalar(y_new[:, t, :], y_new[:, t, :], mv[:, 4 * q + t, 0:1],
                                         rstd[:, 4 * q + t:4 * q + t + 1], ALU.subtract, ALU.mult))
                own.wait()
                to = res[:, 4 * q:4 * q + 4, :]
                own.link(ve.tensor_tensor(y_new[:, :, :], y_new[:, :, :],
                                          bias_all[:, 2:3, :].to_broadcast([P, 4, C]), ALU.mult))
                own(ve.tensor_tensor(to, to, bias_all[:, 3:4, :].to_broadcast([P, 4, C]), ALU.add))
                own.wait()
                ve.tensor_tensor(to, to, y_new[:, :, :], ALU.add).then_inc(res3_done, 1)


_INS = ['x', 'L0_conv_in_w', 'L0_conv_in_b', 'L0_conv_out_w', 'L0_conv_out_b', 'L0_conv_off_w', 'L0_conv_off_b',
        'L0_conv_mask_w', 'L0_conv_mask_b', 'L0_conv_dw_k', 'L0_conv_bn_g', 'L0_conv_bn_b', 'L0_conv_bn_m',
        'L0_conv_bn_v', 'L1_attn_W', 'L1_ffn_Wr', 'L1_ffn_br', 'L1_ffn_W1', 'L1_ffn_b1', 'L1_ffn_W2', 'L1_ffn_b2',
        'L1_ffn_gamma', 'L1_ffn_beta']
_OUTS = [((B, H, W, C), 'float32')]


def kernel(**inputs):
    import numpy as _np
    import concourse.bacc as _bacc
    from concourse import mybir as _mybir
    from concourse.bass_utils import run_bass_kernel_spmd as _run

    nc = _bacc.Bacc("TRN2", target_bir_lowering=False, num_devices=1)
    arrays, args = {}, []
    for name in _INS:
        a = _np.ascontiguousarray(inputs[name])
        arrays[f"in_{name}_dram"] = a
        args.append(nc.dram_tensor(f"in_{name}_dram", a.shape, _mybir.dt.from_np(a.dtype), kind="ExternalInput").ap())
    for i, (shape, dtype) in enumerate(_OUTS):
        dt = _mybir.dt.from_np(_np.dtype(dtype))
        args.append(nc.dram_tensor(f"out_{i}_dram", shape, dt, kind="ExternalOutput").ap())
    hybrid_block_kernel(nc, *args)
    r = _run(nc, [arrays], core_ids=[0])
    got = tuple(r.results[0][f"out_{i}_dram"] for i in range(len(_OUTS)))
    return got[0]
```

```python
from contextlib import ExitStack

import concourse.bass as bass
from concourse import mybir

ALU = mybir.AluOpType
ACT = mybir.ActivationFunctionType
AX = mybir.AxisListType
F32 = mybir.dt.float32
I32 = mybir.dt.int32
U32 = mybir.dt.uint32
BF16 = mybir.dt.bfloat16

B, H, W, C = 4, 32, 32, 128
P = 128
G, PTS = 8, 9
CG = C // G
GP = G * PTS
REACH = 2
TAPS = 2 * REACH + 1
WIN = TAPS + 2
PAD = WIN // 2
HP, WP = H + 2 * PAD, W + 2 * PAD
ROWS = 4
CHUNKS = H // ROWS
CT = ROWS * P
TOK = H * W
TILES = TOK // P
HALF = CHUNKS // 2
SLOTS = ROWS * (HALF - 1) + ROWS + WIN - 1
STENCIL = WIN * WIN
PROD = 7
E = 8
FF = 256
FH = FF // P
CAPACITY = -(-B * TOK * 5 // (4 * E))
GN_EPS = BN_EPS = LN_EPS = 1e-5
GN_C = 4
ROW_UNITS = -(-WIN // 2)
UNITS = WIN * ROW_UNITS
BEGIN = 2
AT_SAMPLES, AT_CONV, AT_FAR, AT_PROJECT = 18, 22, 25, 25
STENCIL_FILL = (0, 1, 1, 0, 1, 1, 0, 1, 1)
RESIDUAL_AT = 3
JOINED_LAST = (8, 10, 12, 14, 16, 18, 20, 22, 24, 25)
OFFS = 3
FLAT_FIRST = 2
ZEROS = 608
XG_PARTS = ((0, ROWS + 1), (ROWS + 1, H))
FAR_COLS = ROWS * GP + ROWS * G + ROWS
PAIRS = B * H // ROWS // 2
LEAD = 6
BIG_SHIFT = 4.0


def first_of(unit):
    return unit // ROW_UNITS * WIN + unit % ROW_UNITS * 2


def joined(chunk):
    return JOINED_LAST if isinstance(chunk, int) and chunk == CHUNKS - 1 else ()


class Own:

    def __init__(self, eng, sem):
        self.eng, self.sem, self.base, self.n, self.alone = eng, sem, 0, 0, None

    def __call__(self, ins):
        ins.then_inc(self.sem, 1)
        self.n += 1
        return ins

    def wait(self):
        self.eng.wait_ge(self.sem, self.base + self.n)
        if self.alone is not None:
            self.eng.sem_inc(self.alone, 1)

    def link(self, ins):
        self(ins)
        self.wait()

    def enter(self, i, per):
        self.saved = self.n
        self.base, self.n, self.per = i * per + self.saved, 0, per

    def leave(self, turns):
        assert self.n == self.per, (self.n, self.per)
        self.base, self.n = 0, self.saved + turns * self.per


def hybrid_block_kernel(nc, x, in_w, in_b, out_w, out_b, off_w, off_b, mask_w, mask_b, dw_k, bn_g, bn_b,
                        bn_m, bn_v, attn_w, wr, br, w1, b1, w2, b2, gamma, beta, out):
    padded = nc.dram_tensor("padded", (B, WP, HP, C), F32, kind="Internal").ap()
    with ExitStack() as ctx:
        def sb(name, shape, dt=F32):
            return ctx.enter_context(nc.sbuf_tensor(name, shape, dt))

        def sem(name):
            return ctx.enter_context(nc.semaphore(name))

        banks = ctx.enter_context(nc.psum_tensor("banks", [P, 4 * 512], F32))
        bank = [banks[:, i * 512:(i + 1) * 512] for i in range(4)]
        pair = [ctx.enter_context(nc.psum_tensor(f"pair{i}", [P, 1024], F32)) for i in range(2)]

        res = sb("res", [P, B * TILES, C])
        stage = sb("stage", [P, H, C])
        shifted = sb("shifted", [P, WIN, SLOTS * G, CG])
        xg = sb("xg", [P, HP - 4, B, W + 2])
        xg_rows = xg[:, :, :, :].rearrange("c y n w -> c (y n) w")

        ident = sb("ident", [P, P])
        ones = sb("ones", [P, P])
        in_w_sb = sb("in_w_sb", [P, C])
        out_w_sb = sb("out_w_sb", [P, C])
        offmask_w = sb("offmask_w", [P, 3 * GP])
        attn_w_sb = sb("attn_w_sb", [P, C])
        wr_sb = sb("wr_sb", [P, E])
        b2_sb = sb("b2_sb", [E, C])
        bias_all = sb("bias_all", [P, 4, C])
        bias_parts = sb("bias_parts", [1, 3, 3 * GP], BF16)
        bias_parts3 = sb("bias_parts3", [3, 3 * GP], BF16)
        ones16 = sb("ones16", [P, P], BF16)
        br_sb = sb("br_sb", [1, E])
        dw_sb = sb("dw_sb", [P, 9])
        bn_sb = sb("bn_sb", [P, 4])
        bn_fold = sb("bn_fold", [P, 4])
        neg_half = sb("neg_half", [P, 32])
        dw_diag = sb("dw_diag", [P, 9, P])
        tap_bias = sb("tap_bias", [P, TAPS + 1])
        zero_col = sb("zero_col", [P, 1])

        gn_stats = sb("gn_stats", [P, B, 2, 6])
        gn_mv = sb("gn_mv", [P, B, 2])
        gn_v = sb("gn_v", [P, 4, B])

        conv = sb("conv", [P, CT])
        conv_bank = pair[1][:, 512:512 + CT]
        gate = sb("gate", [P, CT])
        x1 = gate
        off = sb("off", [P, OFFS, ROWS, 3 * GP])
        off_most = sb("off_most", [P, ROWS * GP])
        far = sb("far", [P, FAR_COLS], BF16)
        far_flags = far[:, 0:ROWS * GP]
        row_max = sb("row_max", [P, ROWS * G])
        row_sum = sb("row_sum", [P, ROWS * G])
        mask = sb("mask", [P, ROWS * G, PTS])
        mask_far = sb("mask_far", [P, 2, ROWS * GP])
        hats = sb("hats", [P, 2, ROWS * GP, TAPS])
        outer = sb("outer", [P, ROWS * G, TAPS, TAPS])
        far_xy = outer[:, :, :, :].rearrange("p g a b -> p (g a b)")[:, 0:ROWS * 2 * GP] \
            .rearrange("p (r o) -> p r o", r=ROWS)
        stencil = sb("stencil", [P, 2, ROWS * G * STENCIL])
        stencil_of = stencil[:, :, :].rearrange("p s (g a b) -> p s g a b", a=WIN, b=WIN)
        prod = sb("prod", [P, PROD, ROWS * G, CG])
        far_counts = sb("far_counts", [1, 2, FAR_COLS], I32)

        outer_flat = outer[:, :, :, :].rearrange("p g a b -> p (g a b)")
        group_mean = outer_flat[:, 0:P]
        offmask_b = outer_flat[0:1, P:P + 3 * GP]
        zero_rows = stencil[:, 1, 0:ZEROS]
        hats_flat = hats[:, :, :, :].rearrange("p a g t -> p (a g t)")
        off_raw = hats_flat[:, 0:2 * GP]
        off_b_raw = hats_flat[0:1, 2 * GP:4 * GP]
        bias_rows = hats_flat[0:1, 4 * GP:4 * GP + 4 * C].rearrange("a (v c) -> a v c", c=C)

        grid = sb("grid", [P, 2, PTS])
        grid_i = sb("grid_i", [P, 2, PTS], I32)
        part_i = sb("part_i", [P, 1], I32)
        cell0 = sb("cell0", [P, G])
        cell0_i = sb("cell0_i", [P, G], I32)
        part_f = sb("part_f", [P, 1])
        pos = sb("pos", [P, 2, PTS])
        low_i = sb("low_i", [P, 2, PTS], I32)
        low = sb("low", [P, 2, PTS])
        over = sb("over", [P, 2, PTS])
        frac = sb("frac", [P, 2, 2, PTS])
        corner = sb("corner", [P, 2, 2, PTS])
        inside = sb("inside", [P, 2, 2, PTS])
        far_m = sb("far_m", [P, PTS])
        cell_f = sb("cell_f", [P, PTS])
        cell_t = sb("cell_t", [P, PTS])
        cells = sb("cells", [P, PTS, 4])
        cell_w = sb("cell_w", [P, PTS, 4])
        cell_now = sb("cell_now", [P, 4], U32)
        w_now = sb("w_now", [P, 4])
        got = sb("got", [P, 4, CG])
        over_stage = stage[:, :, :].rearrange("p y c -> p (y c)")
        fix = over_stage[:, 0:2 * CT].rearrange("p (s g c) -> p s g c", s=2, c=CG)
        samp = over_stage[:, 2 * CT:3 * CT]
        samp_t = over_stage[:, 3 * CT:4 * CT].rearrange("c (n r w) -> c n r w", n=B, r=ROWS)

        over_shifted = shifted[:, :, :, :].rearrange("p d s c -> p (d s c)")
        at_shifted = [0]

        def reuse(n):
            at_shifted[0] += n
            assert at_shifted[0] <= WIN * SLOTS * C
            return over_shifted[:, at_shifted[0] - n:at_shifted[0]]

        normed = reuse(B * TOK).rearrange("p (t c) -> p t c", c=C)
        normed_t = reuse(B * TOK)
        keyed = reuse(B * TOK)
        normed2_t = reuse(B * TOK)
        probs = reuse(2 * TOK).rearrange("p (s t) -> p s t", s=2)
        probs_t = reuse(TOK)
        normed2 = xg[:, :, :, :].rearrange("p y n w -> p (y n w)")[:, 0:B * TOK].rearrange("p (t c) -> p t c", c=C)
        hidden = [h[:, 0:4 * 512].rearrange("p (f t) -> p f t", f=4)
                  for h in (hats_flat, stencil[:, :, :].rearrange("p s g -> p (s g)"))]
        w1_sel = stage[:, 0:16, :].rearrange("p (s f) c -> p s (f c)", s=8)
        w2_sel = stage[:, 16:32, :].rearrange("p (s f) c -> p s f c", s=8)
        b1_sel = sb("b1_sel", [P, 2 * B, FH])
        stats = sb("stats", [P, 8, 6])
        mv = sb("mv", [P, B * TILES, 2])
        rstd = sb("rstd", [P, B * TILES])
        mv_now = sb("mv_now", [P, 4, 2])
        rstd_now = sb("rstd_now", [P, 4])
        neg_max = sb("neg_max", [P, 2])
        den = sb("den", [P, 2])
        rden = sb("rden", [P, 2])
        tok_sum = sb("tok_sum", [P, PAIRS])
        tok_mean = sb("tok_mean", [P, B])
        route = sb("route", [B, 16, E])
        route_s = sb("route_s", [B, 16])
        route_i = sb("route_i", [B, 2], I32)
        rank = sb("rank", [B, E])
        pick_w = sb("pick_w", [B, B, 2])
        weight_all = sb("weight_all", [P, B, 2])
        over_prod = prod[:, :, :, :].rearrange("p s g c -> p s (g c)")
        y_new = over_prod[:, 2:4, :].rearrange("p s (t c) -> p s t c", c=C)
        b2_rows = over_prod[:, 0, :].rearrange("p (n c) -> p n c", n=B)
        dense_t = over_prod[0:E, 1, :].rearrange("e (n t) -> e n t", n=B)
        image_cols = over_prod[0:B, 4, :].rearrange("k (n t) -> k n t", n=B)

        def key_bank(j):
            first = [bank[2], bank[3], pair[0][:, 0:512], pair[0][:, 512:1024], bank[2], bank[3]]
            return first[j] if isinstance(j, int) and j < LEAD else bank[3]

        def flat_rows(q):
            return over_prod[:, q, :] if q < PROD else stencil[:, 1, ZEROS:ZEROS + CT]

        x_in = [sem(f"x_in{n}") for n in range(B)]
        w_in = sem("w_in")
        ident_set = sem("ident_set")
        zeros_set = sem("zeros_set")
        pads_out = sem("pads_out")
        consts = sem("consts")
        dve = sem("dve")
        pool = sem("pool")
        act = sem("act")
        xt_done = sem("xt_done")
        xt_copied = sem("xt_copied")
        gn_mm = sem("gn_mm")
        gn_in = sem("gn_in")
        gn_var = sem("gn_var")
        gn_rstd = sem("gn_rstd")
        xg_ready = sem("xg_ready")
        bias_mm = sem("bias_mm")
        bn_var = sem("bn_var")
        bn_rstd = sem("bn_rstd")
        fold_done = sem("fold_done")
        bias_spread = sem("bias_spread")
        bias_split = sem("bias_split")
        bias_in = sem("bias_in")
        square_done = sem("square_done")
        res_biased = sem("res_biased")
        stencil_clear = sem("stencil_clear")
        flat_done = sem("flat_done")
        proj_mm = sem("proj_mm")
        proj_out = sem("proj_out")
        padded_out = [sem(f"padded_out{q}") for q in range(H // 8)]
        copies_in = sem("copies_in")
        rows_ready = sem("rows_ready")
        conv_done = sem("conv_done")
        gate_done = sem("gate_done")
        x1_done = sem("x1_done")
        off_mm = sem("off_mm")
        off_done = sem("off_done")
        logits_done = sem("logits_done")
        exp_done = sem("exp_done")
        hats_done = sem("hats_done")
        masks_done = sem("masks_done")
        far_mm = sem("far_mm")
        far_done = sem("far_done")
        hats_used = sem("hats_used")
        diag_done = sem("diag_done")
        prod_free = sem("prod_free")
        prod_done = sem("prod_done")
        fix_done = sem("fix_done")
        gathered = sem("gathered")
        waited = sem("waited")
        act_waited = sem("act_waited")
        dve_waited = sem("dve_waited")
        samp_done = sem("samp_done")
        samp_tp = sem("samp_tp")
        samp_t_done = sem("samp_t_done")
        conv_out = sem("conv_out")
        res1_done = sem("res1_done")
        rows_used = sem("rows_used")
        var1 = sem("var1")
        rstd1 = sem("rstd1")
        normed1 = sem("normed1")
        tp1 = sem("tp1")
        normed_t1 = sem("normed_t1")
        key_mm = sem("key_mm")
        keyed_done = sem("keyed_done")
        score_mm = sem("score_mm")
        max_done = sem("max_done")
        prob_done = sem("prob_done")
        probs_tp = sem("probs_tp")
        probs_t_a = sem("probs_t_a")
        probs_t_v = sem("probs_t_v")
        mix_mm = sem("mix_mm")
        res2_done = sem("res2_done")
        var2 = sem("var2")
        rstd2 = sem("rstd2")
        normed2_done = sem("normed2_done")
        tp2 = sem("tp2")
        normed_t2 = sem("normed_t2")
        mean_done = sem("mean_done")
        logit_mm = sem("logit_mm")
        shifted_logits = sem("shifted_logits")
        scaled_logits = sem("scaled_logits")
        gap_done = sem("gap_done")
        routing_done = sem("routing_done")
        r_exp = sem("r_exp")
        load_mm = sem("load_mm")
        beta_added = sem("beta_added")
        b2_mm = sem("b2_mm")
        b2_rows_done = sem("b2_rows_done")
        b2_added = sem("b2_added")
        picked = sem("picked")
        cols_set = sem("cols_set")
        spread_mm = sem("spread_mm")
        spread_done = sem("spread_done")
        experts_in = [sem(f"experts_in{n}") for n in range(B)]
        w2_scaled = sem("w2_scaled")
        up_mm = sem("up_mm")
        gelu_done = sem("gelu_done")
        down_mm = sem("down_mm")
        y_done = sem("y_done")
        var3 = sem("var3")
        rstd3 = sem("rstd3")
        res3_done = sem("res3_done")
        stored = sem("stored")

        N_W = 19
        x_tiles = x.rearrange("n (k r) w c -> n (r w) k c", r=ROWS)
        out_tiles = out.rearrange("n (k r) w c -> n (r w) k c", r=ROWS)
        PIECE = 2 * ROWS
        PCS = H // PIECE
        N_PADS = 4
        FIRST = ROWS + WIN - 1
        PIECES = [(0, FIRST)] + [(FIRST + ROWS * k, FIRST + ROWS * (k + 1)) for k in range(HALF - 1)]

        block = ctx.enter_context(nc.Block())

        @block.sync
        def _(sp):
            for n in range(B):
                sp.dma_start(res[:, n * TILES:(n + 1) * TILES, :], x_tiles[n]).then_inc(x_in[n], 16)
            loads = [(in_w_sb[:, :], in_w), (out_w_sb[:, :], out_w), (off_raw[:, :], off_w),
                     (offmask_w[:, 2 * GP:], mask_w), (attn_w_sb[:, :], attn_w), (wr_sb[:, :], wr),
                     (b2_sb[:, :], b2), (dw_sb[:, :], dw_k.rearrange("c a y x -> c (a y x)")),
                     (off_b_raw[:, :], off_b.rearrange("(a n) -> a n", a=1)),
                     (offmask_b[:, 2 * GP:], mask_b.rearrange("(a n) -> a n", a=1)),
                     (br_sb[:, :], br.rearrange("(a n) -> a n", a=1))]
            for i, v in enumerate((in_b, out_b, gamma, beta)):
                loads.append((bias_rows[:, i, :], v.rearrange("(a n) -> a n", a=1)))
            for i, v in enumerate((bn_g, bn_b, bn_m, bn_v)):
                loads.append((bn_sb[:, i:i + 1], v.rearrange("(n a) -> n a", a=1)))
            for dst, src in loads:
                sp.dma_start(dst, src, allow_slow_non_contiguous=True).then_inc(w_in, 16)
            assert len(loads) == N_W
            sp.wait_ge(zeros_set, 1)
            for w0 in (0, WP - PAD):
                sp.dma_start(padded[:, w0:w0 + PAD, :, :].rearrange("n w y c -> n w (y c)")
                             .rearrange("n w (a b) -> n w a b", b=ZEROS),
                             zero_rows[0:B * PAD * HP * C // ZEROS, :]).then_inc(pads_out, 16)
            for y0 in (0, HP - PAD):
                sp.dma_start(padded[:, PAD:PAD + W, y0:y0 + PAD, :].rearrange("n w y c -> n w (y c)"),
                             zero_rows[:, 0:PAD * C]).then_inc(pads_out, 16)
            for q in range(PCS):
                sp.wait_ge(proj_out, 2 * (q + 1))
                sp.dma_start(padded[:, PAD:PAD + W, PAD + PIECE * q:PAD + PIECE * (q + 1), :]
                             .rearrange("n w y c -> n w (y c)"),
                             stage[:, PIECE * q:PIECE * (q + 1), :].rearrange("p y c -> p (y c)")
                             ).then_inc(padded_out[q], 16)

            def copies(i, r0, r1, s0):
                for d in range(WIN):
                    sp.dma_start(shifted[:, d, s0 * G:(s0 + r1 - r0) * G, :]
                                 .rearrange("p s c -> p (s c)"),
                                 padded[:, d:d + W, r0:r1, :].rearrange("n w y c -> n w (y c)")
                                 ).then_inc(copies_in, 16)
                sp.wait_ge(copies_in, 16 * WIN * (i + 1))

            sp.wait_ge(pads_out, 16 * N_PADS)
            for i, (r0, r1) in enumerate(PIECES):
                for q in range(-(-(r1 - PAD) // PIECE)):
                    sp.wait_ge(padded_out[q], 16)
                copies(i, r0, r1, r0)
                sp.sem_inc(rows_ready, 1)
            for q in range(PCS):
                sp.wait_ge(padded_out[q], 16)
            for k in range(HALF):
                s0, s1 = ROWS * k, (ROWS * (k + 1) if k < HALF - 1 else SLOTS)
                sp.wait_ge(rows_used, k + 1)
                copies(HALF + k, ROWS * HALF + s0, ROWS * HALF + s1, s0)
                if k >= 2:
                    sp.sem_inc(rows_ready, 1 if k == 2 else HALF - 1)

            for n in range(B):
                sp.wait_ge(gap_done, 1)
                for j in range(2):
                    e = sp.value_load(route_i[n:n + 1, j:j + 1], min_val=0, max_val=E - 1)
                    s = 2 * n + j
                    sp.dma_start(w1_sel[:, s, :], w1[bass.ds(e, 1), :, :].rearrange("e d f -> d (e f)")
                                 ).then_inc(experts_in[n], 16)
                    sp.dma_start(w2_sel[:, s, :, :],
                                 w2[bass.ds(e, 1), :, :].rearrange("e (h f) d -> f (e h) d", h=FH)
                                 ).then_inc(experts_in[n], 16)
                    sp.dma_start(b1_sel[:, s, :],
                                 b1[bass.ds(e, 1), :].rearrange("e (h f) -> f (e h)", h=FH),
                                 allow_slow_non_contiguous=True).then_inc(experts_in[n], 16)
            for q in range(2 * B):
                sp.wait_ge(res3_done, q + 1)
                sp.dma_start(out_tiles[q // 2][:, 4 * (q % 2):4 * (q % 2) + 4, :],
                             res[:, 4 * q:4 * q + 4, :]).then_inc(stored, 16)
            sp.wait_ge(stored, 16 * 2 * B)

        @block.scalar
        def _(sc):
            own = Own(sc, act)
            for i in range(2 * B):
                sc.wait_ge(gn_in, i + 1)
                if i == 0:
                    sc.wait_ge(zeros_set, 2)
                n, h = i // 2, i % 2
                sc.activation(xg[:, 1 + 16 * h:17 + 16 * h, n, 1:W + 1],
                              bank[i % 4][:, :].rearrange("c (y w) -> c y w", w=W),
                              ACT.Copy).then_inc(xt_copied, 1)

            sc.wait_ge(w_in, 16 * N_W)
            sc.wait_ge(consts, 1)
            for t in range(9):
                sc.activation(dw_diag[:, t, :], ident[:, :], ACT.Copy, scale=dw_sb[:, t:t + 1]
                              ).then_inc(diag_done, 1)

            sc.wait_ge(bias_split, 3)
            sc.dma_start(bias_parts3[:, :], bias_parts[:, :, :]).then_inc(bias_in, 16)

            def silu(k):
                sc.wait_ge(fold_done, 1)
                sc.wait_ge(conv_done, k + 1)
                sc.wait_ge(off_mm, k + 1)
                sc.activation(gate[:, :], conv_bank, ACT.Tanh, bias=bn_fold[:, 1:2], scale=bn_fold[:, 0:1])
                sc.activation(conv[:, :], conv_bank, ACT.Identity, bias=bn_fold[:, 1:2], scale=bn_fold[:, 0:1]
                              ).then_inc(gate_done, 1)

            for q in range(CHUNKS):
                sc.wait_ge(xg_ready, 1 if q == 0 else 2)
                if q == FLAT_FIRST:
                    silu(0)
                sc.activation(flat_rows(q).rearrange("c (y n w) -> c y n w", y=ROWS, n=B),
                              xg[:, 1 + ROWS * q:1 + ROWS * (q + 1), :, 1:W + 1], ACT.Copy).then_inc(flat_done, 1)

            def prepare(k):
                sc.wait_ge(off_mm, k + 2)
                if not isinstance(k, int) or k > 0:
                    sc.wait_ge(fix_done, k)
                sc.sem_inc(act_waited, 1)
                raw = pair[0][:, :].rearrange("p (r o) -> p r o", r=ROWS)
                sc.activation(off[:, bass.ds(k % OFFS, 1), :, :].rearrange("p s r o -> p (s r) o"),
                              raw[:, :, 0:3 * GP], ACT.Copy).then_inc(off_done, 1)
                sc.wait_ge(hats_used, k + 1)
                sc.activation(far_xy, raw[:, :, 0:2 * GP], ACT.Square).then_inc(square_done, 1)
                sc.wait_ge(off_done, k + 1)
                sc.sem_inc(act_waited, 1)
                for t in range(TAPS):
                    own(sc.activation(
                        hats[:, :, :, t].rearrange("p a (r g) -> p a r g", r=ROWS),
                        off[:, bass.ds(k % OFFS, 1), :, 0:2 * GP].rearrange("p s r (a g) -> p a (s r) g", a=2),
                        ACT.Abs, bias=tap_bias[:, t:t + 1]))
                own.wait()
                hf = hats[:, :, :, :].rearrange("p a g t -> p (a g t)")
                sc.activation(hf, hf, ACT.Relu, bias=tap_bias[:, TAPS:TAPS + 1], scale=-1.0).then_inc(hats_done, 1)
                sc.wait_ge(logits_done, k + 1)
                mf = mask[:, :, :].rearrange("p g q -> p (g q)")
                sc.activation(mf, mf, ACT.Exp).then_inc(exp_done, 1)

            def copy_out(k):
                sc.wait_ge(samp_tp, k + 1)
                sc.activation(samp_t.rearrange("c n r w -> c r n w"),
                              bank[2][:, :].rearrange("c (r n w) -> c r n w", r=ROWS, n=B),
                              ACT.Copy).then_inc(samp_t_done, 1)

            def clear_stencil(k):
                sc.wait_ge(prod_done, (k + 1) * STENCIL)
                sc.sem_inc(act_waited, 1)
                sc.activation(stencil[:, bass.ds(k % 2, 1), :].rearrange("p s g -> p (s g)"),
                              zero_col[:, 0:1].to_broadcast([P, ROWS * G * STENCIL]), ACT.Copy
                              ).then_inc(stencil_clear, 1)

            def count_out(k):
                sc.wait_ge(fix_done, k + 1)
                sc.wait_ge(far_mm, k + 1)
                sc.sem_inc(act_waited, 1)
                sc.activation(far_counts[:, bass.ds(k % 2, 1), :].rearrange("a s o -> a (s o)"),
                              pair[1][0:1, 0:FAR_COLS], ACT.Copy).then_inc(far_done, 1)

            prepare(0)
            count_out(0)
            silu(1)
            prepare(1)
            count_out(1)
            with sc.Fori(0, CHUNKS - 2) as j:
                own.enter(j, TAPS)
                silu(j + 2)
                clear_stencil(j)
                prepare(j + 2)
                copy_out(j)
                count_out(j + 2)
                own.leave(CHUNKS - 2)
            copy_out(CHUNKS - 2)
            copy_out(CHUNKS - 1)

            def copy_normed(j):
                sc.wait_ge(tp1, j + 1)
                sc.sem_inc(act_waited, 1)
                sc.activation(normed_t[:, bass.ds(2 * P * j, 2 * P)], key_bank(j)[:, 0:2 * P], ACT.Copy
                              ).then_inc(normed_t1, 1)

            def copy_keys(j):
                sc.wait_ge(key_mm, j + 1)
                sc.sem_inc(act_waited, 1)
                sc.activation(keyed[:, bass.ds(2 * P * j, 2 * P)], key_bank(j)[:, 0:2 * P], ACT.Copy,
                              scale=float(C) ** -0.5).then_inc(keyed_done, 1)

            def copy_normed2(j):
                sc.wait_ge(tp2, j + 1)
                sc.sem_inc(act_waited, 1)
                sc.activation(normed2_t[:, bass.ds(2 * P * j, 2 * P)], bank[3][:, 2 * P:4 * P], ACT.Copy,
                              accum_out=tok_sum[:, bass.ds(j, 1)]).then_inc(normed_t2, 1)

            def exps(i, s):
                sc.wait_ge(max_done, i + 1)
                sc.activation(probs[:, s, :], pair[s][:, :], ACT.Exp, bias=neg_max[:, s:s + 1],
                              accum_out=den[:, s:s + 1]).then_inc(prob_done, 1)

            def half_probs(i):
                sc.wait_ge(probs_tp, 2 * i + 1)
                sc.activation(probs_t[:, 0:512], bank[0][:, :], ACT.Copy).then_inc(probs_t_a, 1)

            def attend(p, ahead, behind, last=False):
                half_probs(2 * p)
                if behind:
                    copy_normed2(p - 2)
                if not last:
                    exps(2 * p + 2, 0)
                half_probs(2 * p + 1)
                if ahead:
                    copy_normed(p + LEAD)
                if not last:
                    exps(2 * p + 3, 1)
                if ahead:
                    copy_keys(p + LEAD)

            copy_normed(0)
            for j in range(LEAD):
                if j + 1 < LEAD:
                    copy_normed(j + 1)
                copy_keys(j)
                if j == 3:
                    exps(0, 0)
                    exps(1, 1)
            attend(0, True, False)
            attend(1, True, False)
            with sc.Fori(0, PAIRS - LEAD - 2) as j:
                attend(j + 2, True, True)
            with sc.Fori(0, LEAD - 1) as j:
                attend(j + (PAIRS - LEAD), False, True)
            attend(PAIRS - 1, False, True, True)
            copy_normed2(PAIRS - 2)
            copy_normed2(PAIRS - 1)
            sc.wait_ge(shifted_logits, 1)
            sc.activation(route[:, 1, :], route[:, 0, :], ACT.Exp).then_inc(r_exp, 1)
            sc.wait_ge(scaled_logits, 1)
            sc.activation(route[:, 5, :], route[:, 4, :], ACT.Exp).then_inc(r_exp, 1)
            sc.wait_ge(gap_done, 1)
            sc.activation(route_s[:, 9:10], route_s[:, 8:9], ACT.Exp).then_inc(r_exp, 1)
            for q in range(2 * B):
                sc.wait_ge(experts_in[q // 2], 96)
                if q >= 2:
                    sc.wait_ge(down_mm, q - 1)
                for f in range(4):
                    sc.wait_ge(up_mm, 4 * q + f + 1)
                    s = 2 * (q // 2) + f // 2
                    sc.activation(hidden[q % 2][:, f, :], pair[f // 2][:, (f % 2) * 512:(f % 2 + 1) * 512], ACT.Gelu,
                                  bias=b1_sel[:, s, f % 2:f % 2 + 1]).then_inc(gelu_done, 1)

        @block.tensor
        def _(pe):
            pe.wait_ge(ident_set, 1)
            for i in range(2 * B):
                if i % 2 == 0:
                    pe.wait_ge(x_in[i // 2], 16)
                if i >= 4:
                    pe.wait_ge(xt_copied, i - 3)
                    pe.wait_ge(gn_in, i - 3)
                for t in range(4):
                    mm = pe.transpose(bank[i % 4][:, t * P:(t + 1) * P], res[:, 4 * i + t, :], ident[:, :])
                mm.then_inc(xt_done, 1)
            pe.wait_ge(consts, 1)
            pe.wait_ge(gn_in, 2 * B + 1)
            pe.matmul(pair[1][:, 0:B], group_mean[:, :], gn_mv[:, :, 0], start=True, stop=True).then_inc(gn_mm, 1)
            pe.wait_ge(gn_in, 2 * B + 2)
            pe.matmul(pair[1][:, 512:512 + B], group_mean[:, :], gn_v[:, 1, :], start=True, stop=True
                      ).then_inc(gn_mm, 1)
            pe.wait_ge(w_in, 16 * N_W)
            pe.matmul(pair[0][:, 0:4 * C], ones[0:1, :], bias_rows[:, :, :].rearrange("a v c -> a (v c)"),
                      start=True, stop=True).then_inc(bias_mm, 1)

            def offsets(k):
                pe.wait_ge(x1_done, k + 1)
                pe.wait_ge(fold_done, 1)
                if not isinstance(k, int) or k > 0:
                    pe.wait_ge(square_done, k)
                for r in range(ROWS):
                    o = pair[0][:, r * 256:r * 256 + 3 * GP]
                    pe.matmul(o, x1[:, r * P:(r + 1) * P], offmask_w[:, :], start=True, stop=False)
                    mm = pe.matmul(o, ones16[0:3, :], bias_parts3[:, :], start=False, stop=True)
                mm.then_inc(off_mm, 1)

            def convolve(k, t):
                src = xg_rows[:, bass.ds((k * ROWS + t // 3) * B, ROWS * B), t % 3:t % 3 + W]
                mm = pe.matmul(conv_bank.rearrange("c (a w) -> c a w", w=W), dw_diag[:, t, :], src,
                               start=(t == 0), stop=(t == 8))
                if t == 8:
                    mm.then_inc(conv_done, 1)

            pe.wait_ge(xg_ready, 1)
            pe.wait_ge(diag_done, 9)
            pe.sem_inc(off_mm, 1)
            for q in range(CHUNKS):
                if q == 0:
                    for t in range(9):
                        convolve(0, t)
                if q == 2:
                    pe.wait_ge(bias_in, 16)
                    offsets(0)
                pe.wait_ge(flat_done, q + 1)
                if q >= 2:
                    pe.wait_ge(proj_out, q - 1)
                for r in range(ROWS):
                    mm = pe.matmul(bank[q % 2][:, r * P:(r + 1) * P], flat_rows(q)[:, r * P:(r + 1) * P],
                                   in_w_sb[:, :], start=True, stop=True)
                mm.then_inc(proj_mm, 1)
            pe.sem_inc(prod_free, PROD)

            def count_far(k):
                pe.wait_ge(masks_done, k + 1)
                if not isinstance(k, int) or k > 0:
                    pe.wait_ge(far_done, k)
                pe.matmul(pair[1][:, 0:FAR_COLS], ones16[:, :], far[:, :], start=True, stop=True).then_inc(far_mm, 1)

            def add_up(k, first, last):
                for i in range(first, last):
                    c, d = k + i // STENCIL, i % STENCIL
                    acc = banks[:, bass.ds(512 + (c % 2) * 1024, 512)]
                    if d - 1 in [first_of(u) for u in joined(c)]:
                        continue
                    n = 2 if d in [first_of(u) for u in joined(c)] else 1
                    pe.wait_ge(prod_done, c * STENCIL + d + n)
                    pe.matmul(acc, ident[:, :], prod[:, d % PROD, :, :].rearrange("p g c -> p (g c)"),
                              start=(d == 0), stop=(d == STENCIL - 1)).then_inc(prod_free, n)

            def samples_t(k):
                pe.wait_ge(samp_done, k + 2)
                for r in range(ROWS):
                    mm = pe.transpose(bank[2][:, r * P:(r + 1) * P], samp[:, r * P:(r + 1) * P], ident[:, :])
                mm.then_inc(samp_tp, 1)

            def project(k):
                pe.wait_ge(samp_t_done, k + 1)
                pe.wait_ge(res1_done, k + 1)
                for n in range(B):
                    mm = pe.matmul(bank[0][:, n * P:(n + 1) * P], samp_t[:, n, :, :].rearrange("c r w -> c (r w)"),
                                   out_w_sb[:, :], start=True, stop=True)
                mm.then_inc(conv_out, 1)

            pe.wait_ge(gate_done, 1)
            pe.wait_ge(xg_ready, 2)
            for t in range(9):
                convolve(1, t)
            count_far(0)
            add_up(0, 0, first_of(BEGIN))

            def turn(k, first, conv_ahead):
                offsets(k + 1)
                add_up(k, first_of(BEGIN), AT_SAMPLES)
                if not first:
                    samples_t(k - 1)
                add_up(k, AT_SAMPLES, AT_CONV)
                for i in range(AT_CONV, STENCIL):
                    if i == AT_PROJECT and not first:
                        project(k - 1)
                    if conv_ahead and i == AT_CONV:
                        pe.wait_ge(gate_done, k + 2)
                    if conv_ahead and i < AT_CONV + 9:
                        convolve(k + 2, i - AT_CONV)
                    if i == AT_FAR:
                        count_far(k + 1)
                    add_up(k, i, i + 1)
                add_up(k, STENCIL, STENCIL + first_of(BEGIN))

            turn(0, True, True)
            with pe.Fori(0, CHUNKS - 3) as j:
                turn(j + 1, False, True)
            turn(CHUNKS - 2, False, False)
            add_up(CHUNKS - 1, first_of(BEGIN), AT_SAMPLES)
            samples_t(CHUNKS - 2)
            add_up(CHUNKS - 1, AT_SAMPLES, AT_PROJECT)
            project(CHUNKS - 2)
            add_up(CHUNKS - 1, AT_PROJECT, STENCIL)
            samples_t(CHUNKS - 1)
            project(CHUNKS - 1)

            def tokens_t(j, src, dst):
                for t in range(2):
                    mm = pe.transpose(dst[:, t * P:(t + 1) * P],
                                      src[:, bass.ds(2 * j + t, 1), :].rearrange("p t c -> p (t c)"), ident[:, :])
                return mm

            def normed_to_t(j):
                pe.wait_ge(normed1, j + 1)
                if j >= 4:
                    pe.wait_ge(keyed_done, j - 3 if j < LEAD else j)
                if j - LEAD >= 2:
                    pe.wait_ge(normed_t2, j - LEAD - 1)
                tokens_t(j, normed, key_bank(j)).then_inc(tp1, 1)

            def normed2_to_t(j):
                pe.wait_ge(normed2_done, j + 1)
                pe.wait_ge(keyed_done, min(j + LEAD + 2, PAIRS))
                if j > 0:
                    pe.wait_ge(normed_t2, j)
                tokens_t(j, normed2, bank[3][:, 2 * P:4 * P]).then_inc(tp2, 1)

            def keys(j):
                pe.wait_ge(normed_t1, j + 1)
                pe.matmul(key_bank(j)[:, 0:2 * P], attn_w_sb[:, :], normed_t[:, bass.ds(2 * P * j, 2 * P)],
                          start=True, stop=True).then_inc(key_mm, 1)

            def scores(i, s):
                if i >= 2:
                    pe.wait_ge(prob_done, i - 1)
                for h in range(2):
                    mm = pe.matmul(pair[s][:, h * 512:(h + 1) * 512], keyed[:, bass.ds(i * P, P)],
                                   normed_t[:, bass.ds((i // TILES) * TOK + h * 512, 512)], start=True, stop=True)
                mm.then_inc(score_mm, 1)

            def probs_to_t(i, s):
                pe.wait_ge(prob_done, i + 1)
                for h in range(2):
                    if i > 0:
                        pe.wait_ge((probs_t_a, probs_t_v)[h], i)
                    for m in range(4):
                        mm = pe.transpose(bank[h][:, m * P:(m + 1) * P],
                                          probs[:, s, (4 * h + m) * P:(4 * h + m + 1) * P], ident[:, :])
                    mm.then_inc(probs_tp, 1)

            def mix(i):
                pe.wait_ge(probs_t_a, i + 1)
                pe.wait_ge(probs_t_v, i + 1)
                if i > 0:
                    pe.wait_ge(res2_done, i)
                for m in range(TILES):
                    mm = pe.matmul(bank[2][:, 0:C], probs_t[:, m * P:(m + 1) * P],
                                   normed[:, bass.ds((i // TILES) * TILES + m, 1), :].rearrange("p t c -> p (t c)"),
                                   start=(m == 0), stop=(m == TILES - 1))
                mm.then_inc(mix_mm, 1)

            def attend(p, ahead, behind, last=False):
                i = 2 * p
                for s in range(2):
                    probs_to_t(i + s, s)
                    if not last:
                        if s == 0:
                            pe.wait_ge(keyed_done, p + LEAD if ahead else PAIRS)
                        scores(i + s + 2, s)
                    if s == 0 and behind:
                        normed2_to_t(p - 2)
                    if s == 1 and ahead:
                        normed_to_t(p + LEAD)
                    mix(i + s)
                if ahead:
                    keys(p + LEAD)

            normed_to_t(0)
            for j in range(LEAD):
                if j + 1 < LEAD:
                    normed_to_t(j + 1)
                keys(j)
                if j == 3:
                    pe.wait_ge(keyed_done, 4)
                    scores(0, 0)
                    scores(1, 1)
            for p in range(PAIRS):
                attend(p, p < PAIRS - LEAD, p > 1, p == PAIRS - 1)
            normed2_to_t(PAIRS - 2)
            normed2_to_t(PAIRS - 1)

            def up(q):
                n = q // 2
                if q % 2 == 0:
                    pe.wait_ge(experts_in[n], 96)
                for f in range(4):
                    i = 4 * q + f
                    if i >= 4:
                        pe.wait_ge(gelu_done, i - 3)
                    pe.matmul(pair[f // 2][:, (f % 2) * 512:(f % 2 + 1) * 512],
                              w1_sel[:, 2 * n + f // 2, (f % 2) * P:(f % 2 + 1) * P],
                              normed2_t[:, q * 512:(q + 1) * 512], start=True, stop=True).then_inc(up_mm, 1)

            pe.wait_ge(mean_done, 1)
            pe.matmul(bank[2][0:B, 0:E], tok_mean[:, :], wr_sb[:, :], start=True, stop=False)
            pe.matmul(bank[2][0:B, 0:E], ones[0:1, 0:B], br_sb[:, :], start=False, stop=True).then_inc(logit_mm, 1)
            pe.wait_ge(routing_done, 1)
            pe.matmul(bank[2][0:B, 0:E], ones[0:B, 0:B], route[:, 2, :], start=True, stop=True).then_inc(load_mm, 1)
            pe.wait_ge(picked, 1)
            pe.matmul(bank[2][:, 0:2 * B], ones[0:B, :], pick_w[:, :, :].rearrange("k n j -> k (n j)"),
                      start=True, stop=True).then_inc(spread_mm, 1)
            up(0)
            pe.wait_ge(cols_set, 1)
            pe.matmul(bank[3][0:E, :], route[:, 12, :], image_cols[:, :, :].rearrange("k n t -> k (n t)"),
                      start=True, stop=True).then_inc(spread_mm, 1)

            pe.wait_ge(spread_done, 1)
            for n in range(B):
                mm = pe.matmul(bank[1][:, n * C:(n + 1) * C], dense_t[:, n, :], b2_sb[:, :], start=True, stop=True)
            mm.then_inc(b2_mm, 1)

            def down(q):
                n = q // 2
                pe.wait_ge(w2_scaled, n + 1)
                if q == 1:
                    pe.wait_ge(b2_rows_done, 1)
                if q >= 2:
                    pe.wait_ge(y_done, q - 1)
                pe.wait_ge(gelu_done, 4 * (q + 1))
                for t in range(4):
                    for f in range(4):
                        mm = pe.matmul(bank[q % 2][:, t * P:(t + 1) * P], hidden[q % 2][:, f, t * P:(t + 1) * P],
                                       w2_sel[:, 2 * n + f // 2, f % 2, :], start=(f == 0), stop=(f == 3))
                mm.then_inc(down_mm, 1)

            for q in range(1, 2 * B + 1):
                if q < 2 * B:
                    up(q)
                down(q - 1)

        @block.gpsimd
        def _(gp):
            own = Own(gp, pool)
            own.link(gp.memset(ident[:, :], 0.0))
            gp.affine_select(out=ident[:, :], in_=ident[:, :], compare_op=ALU.not_equal, fill=1.0, base=0,
                             pattern=[[-1, P]], channel_multiplier=1).then_inc(ident_set, 1)
            gp.memset(zero_rows, 0.0).then_inc(zeros_set, 1)
            for v in (xg[:, 0, :, :], xg[:, H + 1, :, :], xg[:, 1:H + 1, :, 0]):
                gp.memset(v, 0.0)
            gp.memset(xg[:, 1:H + 1, :, W + 1], 0.0).then_inc(zeros_set, 1)
            own(gp.memset(ones[:, :], 1.0))
            own(gp.memset(ones16[:, :], 1.0))
            own(gp.memset(group_mean[:, :], 1.0 / GN_C))
            own.wait()
            gm = group_mean[:, :].rearrange("p (g j) -> p g j", j=GN_C)
            own.link(gp.affine_select(out=gm, in_=gm, compare_op=ALU.is_ge, fill=0.0, base=0,
                                      pattern=[[-GN_C, P // GN_C], [0, GN_C]], channel_multiplier=1))
            own.link(gp.affine_select(out=gm, in_=gm, compare_op=ALU.is_ge, fill=0.0, base=GN_C - 1,
                                      pattern=[[GN_C, P // GN_C], [0, GN_C]], channel_multiplier=-1))
            for t in range(TAPS):
                gp.memset(tap_bias[:, t:t + 1], float(REACH - t))
            gp.memset(tap_bias[:, TAPS:TAPS + 1], 1.0)
            own(gp.memset(zero_col[:, :], 0.0))
            own.link(gp.memset(neg_half[:, :], -0.5))
            gp.iota(rank[:, :], pattern=[[-1, E]], base=E, channel_multiplier=0,
                    allow_small_or_imprecise_dtypes=True).then_inc(consts, 1)

            for n in range(B):
                rows = slice(32 * n, 32 * n + 32)
                own.link(gp.iota(grid_i[rows, 0, :].rearrange("p (a b) -> p a b", a=3), pattern=[[1, 3], [0, 3]],
                                 base=-1, channel_multiplier=1))
                own.link(gp.iota(part_i[rows, :], pattern=[[0, 1]],
                                 base=(n * WP + PAD) * HP * G + PAD * G, channel_multiplier=0))
            own.link(gp.iota(grid_i[:, 1, :].rearrange("p (a b) -> p a b", a=3), pattern=[[0, 3], [1, 3]],
                             base=-1, channel_multiplier=0))
            own.link(gp.iota(cell0_i[:, :], pattern=[[1, G]], base=0, channel_multiplier=0))
            own.link(gp.tensor_copy(grid[:, :, :], grid_i[:, :, :]))
            own.link(gp.tensor_copy(part_f[:, :], part_i[:, :]))
            own.link(gp.tensor_copy(cell0[:, :], cell0_i[:, :]))
            own.link(gp.tensor_scalar(cell0[:, :], cell0[:, :], part_f[:, 0:1], None, ALU.add))

            gp.wait_ge(gn_var, 1)
            gp.tensor_tensor(gn_v[:, 3, :], gn_v[:, 2, :], neg_half[:, 0:B], ALU.pow).then_inc(gn_rstd, 1)
            gp.wait_ge(bn_var, 1)
            gp.tensor_tensor(bn_fold[:, 3:4], bn_fold[:, 2:3], neg_half[:, 0:1], ALU.pow).then_inc(bn_rstd, 1)

            gp.memset(stencil[:, 0, :], 0.0).then_inc(stencil_clear, 1)
            gp.wait_ge(xt_done, 2 * B)
            gp.wait_ge(bias_spread, 1)
            gp.tensor_tensor(res[:, :, :], res[:, :, :], bias_all[:, 1:2, :].to_broadcast([P, B * TILES, C]), ALU.add
                             ).then_inc(res_biased, 1)

            def wait(what, count):
                gp.wait_ge(what, count)
                gp.sem_inc(waited, 1)

            own.alone = waited
            gp.sem_inc(fix_done, 2)
            GROUP_STEPS, POINT_STEPS = 32, 7
            for q in range(PCS):
                wait(padded_out[q], 16)
            wait(pads_out, 16 * N_PADS)
            gp.memset(stencil[:, 1, :], 0.0).then_inc(stencil_clear, 1)
            own(gp.memset(fix[:, :, :, :], 0.0))
            start = own.n
            per_group = GROUP_STEPS + PTS * POINT_STEPS
            per_row = 1 + G * per_group
            per_chunk = ROWS * per_row + 1
            table = padded.rearrange("n w y (g c) -> (n w y g) c", g=G)

            def far_number(k, at, most):
                return gp.value_load(far_counts[0:1, bass.ds(k % 2, 1), bass.ds(at, 1)].rearrange("a s g -> a (s g)"),
                                     min_val=0, max_val=most)

            def group_corners(k, r, g):
                own(gp.tensor_copy(pos[:, :, :], off[:, bass.ds(k % OFFS, 1), bass.ds(r, 1), 0:2 * GP]
                                   .rearrange("p s r (a o) -> p (s r a) o", a=2)[:, :, bass.ds(g * PTS, PTS)]))
                own(gp.tensor_copy(far_m[:, :], mask_far[:, bass.ds(k % 2, 1), bass.ds((r * G + g) * PTS, PTS)]
                                   .rearrange("p s o -> p (s o)")))
                own.wait()
                own.link(gp.tensor_tensor(pos[:, :, :], pos[:, :, :], grid[:, :, :], ALU.add))
                own.link(gp.tensor_scalar(pos[:, :, :], pos[:, :, :], float(H + 1), -2.0, ALU.min, ALU.max))
                own.link(gp.tensor_copy(low_i[:, :, :], pos[:, :, :]))
                own.link(gp.tensor_copy(low[:, :, :], low_i[:, :, :]))
                own.link(gp.tensor_tensor(over[:, :, :], low[:, :, :], pos[:, :, :], ALU.subtract))
                own.link(gp.tensor_scalar(over[:, :, :], over[:, :, :], 0.0, None, ALU.is_gt))
                own.link(gp.tensor_tensor(low[:, :, :], low[:, :, :], over[:, :, :], ALU.subtract))
                own.link(gp.tensor_tensor(frac[:, 1, :, :], pos[:, :, :], low[:, :, :], ALU.subtract))
                own.link(gp.tensor_scalar(frac[:, 0, :, :], frac[:, 1, :, :], -1.0, 1.0, ALU.mult, ALU.add))
                own.link(gp.tensor_scalar(over[:, :, :], low[:, :, :], 1.0, 1.0, ALU.add, ALU.mult))
                for a in range(2):
                    own(gp.tensor_scalar(corner[:, a, :, :], (low, over)[a][:, :, :], float(W - 1), 0.0,
                                         ALU.min, ALU.max))
                own.wait()
                for a in range(2):
                    own(gp.tensor_tensor(inside[:, a, :, :], corner[:, a, :, :], (low, over)[a][:, :, :],
                                         ALU.subtract))
                own.wait()
                own.link(gp.tensor_scalar(inside[:, :, :, :], inside[:, :, :, :], 0.0, None, ALU.is_equal))
                own.link(gp.tensor_tensor(frac[:, :, :, :], frac[:, :, :, :], inside[:, :, :, :], ALU.mult))
                own(gp.tensor_scalar(corner[:, :, 0, :], corner[:, :, 0, :], float(HP * G), 0.0, ALU.mult, ALU.add))
                own(gp.tensor_scalar(corner[:, :, 1, :], corner[:, :, 1, :], float(G), 0.0, ALU.mult, ALU.add))
                own.wait()
                for a in range(2):
                    own.link(gp.tensor_tensor(cell_f[:, :], corner[:, a, 0, :],
                                              cell0[:, bass.ds(g, 1)].to_broadcast([P, PTS]), ALU.add))
                    own.link(gp.tensor_tensor(cell_t[:, :], far_m[:, :], frac[:, a, 0, :], ALU.mult))
                    for b in range(2):
                        own(gp.tensor_tensor(cells[:, :, 2 * a + b], cell_f[:, :], corner[:, b, 1, :], ALU.add))
                        own(gp.tensor_tensor(cell_w[:, :, 2 * a + b], cell_t[:, :], frac[:, b, 1, :], ALU.mult))
                    own.wait()
                assert own.n == GROUP_STEPS, own.n

            def point_samples(k, r, g, q):
                own(gp.tensor_copy(cell_now[:, :], cells[:, bass.ds(q, 1), :].rearrange("p a b -> p (a b)")))
                own(gp.tensor_copy(w_now[:, :], cell_w[:, bass.ds(q, 1), :].rearrange("p a b -> p (a b)")))
                own.wait()
                for a in range(4):
                    gp.indirect_dma_start(
                        out=got[:, a, :], out_offset=None, in_=table,
                        in_offset=bass.IndirectOffsetOnAxis(ap=cell_now[:, a:a + 1], axis=0)
                    ).then_inc(gathered, 16)
                gp.wait_ge(gathered, 64)
                gp.inc_swdge_sem([gathered], [64], mode="sub")
                own.link(gp.tensor_tensor(got[:, :, :], got[:, :, :],
                                          w_now[:, :].unsqueeze(2).to_broadcast([P, 4, CG]), ALU.mult))
                to = fix[:, bass.ds(k % 2, 1), bass.ds(r * G + g, 1), :].rearrange("p s a c -> p (s a c)")
                for a in range(4):
                    own.link(gp.tensor_tensor(to, to, got[:, a, :], ALU.add))
                assert own.n == POINT_STEPS, own.n

            with gp.Fori(0, CHUNKS) as k:
                wait(off_done, k + 1)
                wait(masks_done, k + 1)
                wait(far_done, k + 1)
                with gp.Fori(0, ROWS) as r:
                    row0 = k * per_chunk + start + r * per_row
                    in_row = far_number(k, r + ROWS * (GP + G), P * GP)
                    with gp.If(in_row > 0):
                        with gp.Fori(0, G) as g:
                            group0 = row0 + g * per_group
                            in_group = far_number(k, r * G + g + ROWS * GP, P * PTS)
                            with gp.If(in_group > 0):
                                own.base, own.n = group0, 0
                                group_corners(k, r, g)
                                with gp.Fori(0, PTS) as q:
                                    at_point = far_number(k, (r * G + g) * PTS + q, P)
                                    own.base, own.n = group0 + (GROUP_STEPS + q * POINT_STEPS), 0
                                    with gp.If(at_point > 0):
                                        point_samples(k, r, g, q)
                                    with gp.Else():
                                        gp.sem_inc(pool, POINT_STEPS)
                                gp.nop()
                            with gp.Else():
                                gp.sem_inc(pool, per_group)
                        gp.nop()
                    with gp.Else():
                        gp.sem_inc(pool, per_row - 1)
                    own.base, own.n = row0 + (per_row - 1), 0
                    own.link(gp.tensor_scalar(grid[:, 1, :], grid[:, 1, :], 1.0, 0.0, ALU.add, ALU.add))
                own.base, own.n = k * per_chunk + (start + ROWS * per_row), 0
                own.wait()
                gp.sem_inc(fix_done, 1)
                wait(samp_done, k + 1)
                own.link(gp.tensor_copy(fix[:, bass.ds((k + 1) % 2, 1), :, :].rearrange("p s g c -> p (s g c)"),
                                        zero_col[:, 0:1].to_broadcast([P, CT])))
            own.base, own.n, own.alone = 0, start + CHUNKS * per_chunk, None

            def roots(j, slot, done, out_sem):
                wait(done, j + 1)
                gp.tensor_tensor(rstd_now[:, slot:slot + 2], mv_now[:, slot:slot + 2, 1], neg_half[:, 0:2], ALU.pow
                                 ).then_inc(out_sem, 1)

            def add_beta(j):
                wait(normed2_done, j + 1)
                to = res[:, bass.ds(2 * j, 2), :]
                gp.tensor_tensor(to, to, bias_all[:, 3:4, :].to_broadcast([P, 2, C]), ALU.add).then_inc(beta_added, 1)

            for j in range(LEAD + 1):
                roots(j, 2 * (j % 2), var1, rstd1)
            with gp.Fori(0, PAIRS - LEAD - 1) as j:
                roots(j + (LEAD + 1), 0, var1, rstd1)
                roots(j, 2, var2, rstd2)
                add_beta(j)
            with gp.Fori(0, LEAD + 1) as j:
                roots(j + (PAIRS - LEAD - 1), 2, var2, rstd2)
                add_beta(j + (PAIRS - LEAD - 1))
            gp.wait_ge(res1_done, CHUNKS + 1)
            own.link(gp.tensor_copy(image_cols[:, :, :], ones[0:B, :].unsqueeze(1).to_broadcast([B, B, P])))
            gp.affine_select(out=image_cols[:, :, :], in_=image_cols[:, :, :], compare_op=ALU.is_equal, fill=0.0,
                             base=0, pattern=[[-1, B], [0, P]], channel_multiplier=1).then_inc(cols_set, 1)
            gp.wait_ge(tp2, PAIRS)
            gp.wait_ge(b2_rows_done, 1)
            for n in range(B):
                to = normed2[:, n * TILES:(n + 1) * TILES, :]
                gp.tensor_tensor(to, to, b2_rows[:, n:n + 1, :].to_broadcast([P, TILES, C]), ALU.add
                                 ).then_inc(b2_added, 1)
            for q in range(2 * B):
                gp.wait_ge(var3, q + 1)
                gp.tensor_tensor(rstd[:, 4 * q:4 * q + 4], mv[:, 4 * q:4 * q + 4, 1], neg_half[:, 0:4], ALU.pow
                                 ).then_inc(rstd3, 1)

        @block.vector
        def _(ve):
            own = Own(ve, dve)
            for i in range(2 * B):
                ve.wait_ge(xt_done, i + 1)
                ve.bn_stats(gn_stats[:, i // 2, i % 2, :], bank[i % 4][:, :]).then_inc(gn_in, 1)
            ve.wait_ge(gn_in, 2 * B)
            for n in range(B):
                last = ve.bn_aggr(gn_mv[:, n, :], gn_stats[:, n, :, :].rearrange("p a b -> p (a b)"))
            last.then_inc(gn_in, 1)
            ve.wait_ge(gn_mm, 1)
            own.link(ve.tensor_copy(gn_v[:, 0, :], pair[1][:, 0:B]))
            own.link(ve.tensor_tensor(gn_v[:, 2, :], gn_mv[:, :, 0], gn_v[:, 0, :], ALU.subtract))
            own.link(ve.tensor_tensor(gn_v[:, 2, :], gn_v[:, 2, :], gn_v[:, 2, :], ALU.mult))
            ve.tensor_tensor(gn_v[:, 1, :], gn_v[:, 2, :], gn_mv[:, :, 1], ALU.add).then_inc(gn_in, 1)
            ve.wait_ge(gn_mm, 2)
            ve.tensor_scalar(gn_v[:, 2, :], pair[1][:, 512:512 + B], GN_EPS, None, ALU.add).then_inc(gn_var, 1)

            def normalise_input(part):
                y0, y1 = XG_PARTS[part]
                for n in range(B):
                    v = xg[:, 1 + y0:1 + y1, n, 1:W + 1]
                    last = ve.tensor_scalar(v, v, gn_v[:, 0, n:n + 1], gn_v[:, 3, n:n + 1],
                                            ALU.subtract, ALU.mult)
                last.then_inc(xg_ready, 1)

            ve.wait_ge(gn_rstd, 1)
            ve.wait_ge(xt_copied, 2 * B)
            normalise_input(0)
            ve.wait_ge(w_in, 16 * N_W)
            ve.tensor_scalar(bn_fold[:, 2:3], bn_sb[:, 3:4], BN_EPS, None, ALU.add).then_inc(bn_var, 1)
            for src, dst in ((off_raw, offmask_w), (off_b_raw, offmask_b)):
                own(ve.tensor_copy(dst[:, 0:2 * GP].rearrange("p (a g) -> p a g", a=2),
                                   src[:, :].rearrange("p (g a) -> p a g", a=2)))
            ve.wait_ge(bias_mm, 1)
            ve.tensor_copy(bias_all[:, :, :].rearrange("p v c -> p (v c)"), pair[0][:, 0:4 * C]
                           ).then_inc(bias_spread, 1)
            own.wait()
            ve.wait_ge(bias_spread, 1)
            ve.sem_inc(hats_used, 1)
            for i in range(3):
                ve.tensor_copy(bias_parts[:, i, :], offmask_b[:, :]).then_inc(bias_split, 1)
                ve.wait_ge(bias_split, i + 1)
                if i < 2:
                    own.link(ve.tensor_tensor(offmask_b[:, :], offmask_b[:, :], bias_parts[:, i, :], ALU.subtract))
            ve.wait_ge(bn_rstd, 1)
            own.link(ve.tensor_tensor(bn_fold[:, 0:1], bn_sb[:, 0:1], bn_fold[:, 3:4], ALU.mult))
            own.link(ve.tensor_tensor(bn_fold[:, 1:2], bn_sb[:, 2:3], bn_fold[:, 0:1], ALU.mult))
            own.link(ve.tensor_tensor(bn_fold[:, 1:2], bn_sb[:, 1:2], bn_fold[:, 1:2], ALU.subtract))
            ve.tensor_scalar(bn_fold[:, 0:2], bn_fold[:, 0:2], 0.5, None, ALU.mult).then_inc(fold_done, 1)
            normalise_input(1)

            def finish_silu(k):
                ve.wait_ge(gate_done, k + 1)
                ve.scalar_tensor_tensor(x1[:, :], gate[:, :], 1.0, conv[:, :],
                                        ALU.add, ALU.mult).then_inc(x1_done, 1)

            for q in range(CHUNKS):
                if q == 2:
                    finish_silu(0)
                ve.wait_ge(proj_mm, q + 1)
                ve.tensor_tensor(stage[:, ROWS * q:ROWS * (q + 1), :],
                                 bank[q % 2][:, :].rearrange("p (r c) -> p r c", r=ROWS),
                                 bias_all[:, 0:1, :].to_broadcast([P, ROWS, C]), ALU.add).then_inc(proj_out, 1)

            def nothing(n):
                pass

            def mask_logits(k, fill):
                ve.wait_ge(off_done, k + 1)
                lg = off[:, bass.ds(k % OFFS, 1), :, 2 * GP:].rearrange("p s r (g q) -> p (s r) g q", g=G)
                own(ve.tensor_reduce(row_max[:, :].rearrange("p (r g) -> p r g", r=ROWS), lg, AX.X, ALU.max))
                fill(1)
                own.wait()
                for r in range(ROWS):
                    last = ve.tensor_tensor(mask[:, r * G:(r + 1) * G, :], lg[:, r],
                                            row_max[:, r * G:(r + 1) * G].unsqueeze(2).to_broadcast([P, G, PTS]),
                                            ALU.subtract)
                last.then_inc(logits_done, 1)
                ve.wait_ge(square_done, k + 1)
                own(ve.tensor_tensor(off_most[:, :].rearrange("p (r g) -> p r g", r=ROWS), far_xy[:, :, 0:GP],
                                     far_xy[:, :, GP:], ALU.max))
                fill(1)
                own.wait()
                own(ve.tensor_scalar(far_flags, off_most[:, :], float(REACH) ** 2, None, ALU.is_gt))
                fill(1)
                own.wait()
                with nc.allow_low_precision(reason="whole numbers up to 72 are exact in bfloat16"):
                    own.link(ve.tensor_reduce(far[:, ROWS * GP:ROWS * (GP + G)],
                                              far_flags.rearrange("p (g q) -> p g q", q=PTS), AX.X, ALU.add))
                    own(ve.tensor_reduce(far[:, ROWS * (GP + G):],
                                         far[:, ROWS * GP:ROWS * (GP + G)].rearrange("p (r g) -> p r g", r=ROWS),
                                         AX.X, ALU.add))

            def masks(k, fill):
                mf = mask[:, :, :].rearrange("p g q -> p (g q)")
                ve.wait_ge(exp_done, k + 1)
                own(ve.tensor_reduce(row_sum[:, :], mask[:, :, :], AX.X, ALU.add))
                fill(1)
                own.wait()
                own.link(ve.reciprocal(row_sum[:, :], row_sum[:, :]))
                own(ve.tensor_tensor(mask[:, :, :], mask[:, :, :],
                                     row_sum[:, :].unsqueeze(2).to_broadcast([P, ROWS * G, PTS]), ALU.mult))
                fill(1)
                own.wait()
                far_part = mask_far[:, bass.ds(k % 2, 1), :].rearrange("p s o -> p (s o)")
                own.link(ve.tensor_tensor(far_part, far_flags, mf, ALU.mult))
                own.link(ve.tensor_tensor(mf, mf, far_part, ALU.subtract))
                ve.sem_inc(masks_done, 1)
                ve.wait_ge(hats_done, k + 1)
                own(ve.tensor_tensor(hats[:, 1, :, :], hats[:, 1, :, :],
                                     mf.unsqueeze(2).to_broadcast([P, ROWS * GP, TAPS]), ALU.mult))

            def stencils(k, fill, residual_at=0):
                ve.wait_ge(stencil_clear, k + 1)
                hx = hats[:, 0, :, :].rearrange("p (g q) t -> p g q t", q=PTS)
                hy = hats[:, 1, :, :].rearrange("p (g q) t -> p g q t", q=PTS)
                now = stencil_of[:, bass.ds(k % 2, 1), :, :, :].rearrange("p s g a b -> p (s g) a b")
                full = [P, ROWS * G, TAPS, TAPS]
                for q in range(PTS):
                    kx, ky = q // 3, q % 3
                    to = now[:, :, ky:ky + TAPS, kx:kx + TAPS]
                    own.wait()
                    if q == residual_at > 0:
                        residual(k - 2)
                    own(ve.tensor_tensor(to if q == 0 else outer[:, :, :, :],
                                         hy[:, :, q, :].unsqueeze(3).to_broadcast(full),
                                         hx[:, :, q, :].unsqueeze(2).to_broadcast(full), ALU.mult))
                    fill(1)
                    if q > 0:
                        own.wait()
                        own(ve.tensor_tensor(to, to, outer[:, :, :, :], ALU.add))
                        fill(STENCIL_FILL[q])
                own.wait()
                ve.sem_inc(hats_used, 1)

            def products(k, first, last):
                for i in range(first, last):
                    c, u = k + i // UNITS, i % UNITS
                    d = first_of(u)
                    dy, dx = divmod(d, WIN)
                    n = min(2, WIN - dx)
                    full = [P, n, ROWS * G, CG]
                    if u == 0:
                        ve.wait_ge(rows_ready, c + 1)
                    ve.wait_ge(prod_free, c * STENCIL + d + n)
                    ins = ve.tensor_tensor(
                        prod[:, dx:dx + n, :, :],
                        shifted[:, dx:dx + n, bass.ds(((c % HALF) * ROWS + dy) * G, ROWS * G), :],
                        stencil_of[:, bass.ds(c % 2, 1), :, dy, dx:dx + n].rearrange("p s g b -> p b (s g)")
                        .unsqueeze(3).to_broadcast(full), ALU.mult)
                    if u in joined(c):
                        own.link(ins)
                        ins = ve.tensor_tensor(prod[:, dx, :, :], prod[:, dx, :, :], prod[:, dx + 1, :, :], ALU.add)
                    ins.then_inc(prod_done, n)

            def collect(k):
                ve.wait_ge(prod_free, k * STENCIL + STENCIL + PROD)
                ve.sem_inc(rows_used, 1)
                ve.wait_ge(fix_done, k + 3)
                ve.tensor_tensor(samp, banks[:, bass.ds(512 + (k % 2) * 1024, 512)],
                                 fix[:, bass.ds(k % 2, 1), :, :].rearrange("p s g c -> p (s g c)"), ALU.add
                                 ).then_inc(samp_done, 1)

            def residual(k):
                ve.wait_ge(conv_out, k + 1)
                to = res[:, :, :].rearrange("p (n k) c -> p n k c", n=B)[:, :, bass.ds(k, 1), :] \
                    .rearrange("p n k c -> p n (k c)")
                ve.tensor_tensor(to, bank[0][:, :].rearrange("p (n c) -> p n c", n=B), to, ALU.add
                                 ).then_inc(res1_done, 1)

            ve.sem_inc(res1_done, 1)
            n0 = own.n
            ve.sem_inc(samp_done, 1)
            mask_logits(0, nothing)
            masks(0, nothing)
            stencils(0, nothing)
            per = own.n - n0
            products(0, 0, BEGIN)
            ve.wait_ge(res_biased, 1)
            for q in range(PCS):
                ve.wait_ge(padded_out[q], 16)

            def turn(k, first):
                place = [BEGIN]

                def fill(n):
                    products(k, place[0], place[0] + n)
                    place[0] += n

                finish_silu(k + 1)
                fill(5)
                mask_logits(k + 1, fill)
                if not first:
                    collect(k - 1)
                fill(1)
                masks(k + 1, fill)
                stencils(k + 1, fill, 0 if first else RESIDUAL_AT)
                assert place[0] <= UNITS, place
                fill(UNITS + BEGIN - place[0])

            turn(0, True)
            with ve.Fori(0, CHUNKS - 2) as j:
                own.enter(j, per)
                turn(j + 1, False)
                own.leave(CHUNKS - 2)
            products(CHUNKS - 1, BEGIN, BEGIN + 4)
            collect(CHUNKS - 2)
            products(CHUNKS - 1, BEGIN + 4, UNITS - 4)
            residual(CHUNKS - 2)
            products(CHUNKS - 1, UNITS - 4, UNITS)
            collect(CHUNKS - 1)
            residual(CHUNKS - 1)
            ve.wait_ge(res1_done, CHUNKS + 1)

            def token_stats(j, slot, done):
                for t in range(2):
                    own(ve.bn_stats(stats[:, slot + t, :],
                                    res[:, bass.ds(2 * j + t, 1), :].rearrange("p t c -> p (t c)")))
                own.wait()
                ve.sem_inc(dve_waited, 1)
                for t in range(2):
                    own(ve.bn_aggr(mv_now[:, slot + t, :], stats[:, slot + t, :]))
                own.wait()
                v = mv_now[:, slot:slot + 2, 1]
                ve.tensor_scalar(v, v, LN_EPS, None, ALU.add).then_inc(done, 1)

            def normalise(j, slot, dst, rstd_sem, normed_sem):
                ve.wait_ge(rstd_sem, j + 1)
                for t in range(2):
                    now = bass.ds(2 * j + t, 1)
                    last = ve.tensor_scalar(dst[:, now, :].rearrange("p t c -> p (t c)"),
                                            res[:, now, :].rearrange("p t c -> p (t c)"),
                                            mv_now[:, slot + t, 0:1], rstd_now[:, slot + t:slot + t + 1],
                                            ALU.subtract, ALU.mult)
                last.then_inc(normed_sem, 1)

            def maxima(i, s):
                ve.wait_ge(score_mm, i + 1)
                ve.tensor_reduce(neg_max[:, s:s + 1], pair[s][:, :], AX.X, ALU.max, negate=True).then_inc(max_done, 1)

            def half_probs(i, s):
                ve.wait_ge(probs_tp, 2 * i + 2)
                ve.tensor_copy(probs_t[:, 512:1024], bank[1][:, :]).then_inc(probs_t_v, 1)
                own.link(ve.reciprocal(rden[:, s:s + 1], den[:, s:s + 1]))

            def add_mix(i, s):
                ve.wait_ge(mix_mm, i + 1)
                to = res[:, bass.ds(i, 1), :].rearrange("p a c -> p (a c)")
                ve.scalar_tensor_tensor(to, bank[2][:, 0:C], rden[:, s:s + 1], to, ALU.mult, ALU.add
                                        ).then_inc(res2_done, 1)

            def attend(p, ahead, behind, last=False):
                half_probs(2 * p, 0)
                if not last:
                    maxima(2 * p + 2, 0)
                if ahead:
                    token_stats(p + LEAD, 0, var1)
                if behind:
                    ve.wait_ge(res2_done, 2 * p)
                    token_stats(p - 1, 2, var2)
                add_mix(2 * p, 0)
                if ahead:
                    normalise(p + LEAD, 0, normed, rstd1, normed1)
                half_probs(2 * p + 1, 1)
                if not last:
                    maxima(2 * p + 3, 1)
                if behind:
                    normalise(p - 1, 2, normed2, rstd2, normed2_done)
                add_mix(2 * p + 1, 1)

            def attend_all(turns, first, ahead):
                steps = 2 + 4 * ahead + 4
                with ve.Fori(0, turns) as j:
                    own.enter(j, steps)
                    attend(j + first, ahead, True)
                    own.leave(turns)

            token_stats(0, 0, var1)
            for j in range(LEAD):
                if j < LEAD - 1:
                    token_stats(j + 1, 2 * ((j + 1) % 2), var1)
                normalise(j, 2 * (j % 2), normed, rstd1, normed1)
            maxima(0, 0)
            maxima(1, 1)
            attend(0, True, False)
            attend_all(PAIRS - LEAD - 1, 1, True)
            attend_all(LEAD - 1, PAIRS - LEAD, False)
            attend(PAIRS - 1, False, True, True)
            ve.wait_ge(res2_done, B * TILES)
            token_stats(PAIRS - 1, 2, var2)
            normalise(PAIRS - 1, 2, normed2, rstd2, normed2_done)

            ve.wait_ge(normed_t2, PAIRS)
            own.link(ve.tensor_reduce(tok_mean[:, :], tok_sum[:, :].rearrange("p (n h) -> p n h", n=B), AX.X, ALU.add))
            ve.tensor_scalar(tok_mean[:, :], tok_mean[:, :], 1.0 / TOK, None, ALU.mult).then_inc(mean_done, 1)
            ve.wait_ge(logit_mm, 1)
            own.link(ve.tensor_copy(route[:, 3, :], bank[2][0:B, 0:E]))
            own.link(ve.tensor_reduce(route_s[:, 0:1], route[:, 3, :], AX.X, ALU.max))
            ve.tensor_scalar(route[:, 0, :], route[:, 3, :], route_s[:, 0:1], None, ALU.subtract
                             ).then_inc(shifted_logits, 1)
            ve.wait_ge(r_exp, 1)
            own.link(ve.tensor_reduce(route_s[:, 1:2], route[:, 1, :], AX.X, ALU.add))
            own.link(ve.reciprocal(route_s[:, 2:3], route_s[:, 1:2]))
            ve.tensor_scalar(route[:, 2, :], route[:, 1, :], route_s[:, 2:3], None, ALU.mult).then_inc(routing_done, 1)
            ve.wait_ge(load_mm, 1)
            own.link(ve.tensor_scalar(route[:, 6, :], bank[2][0:B, 0:E], float(TOK), float(CAPACITY),
                                      ALU.mult, ALU.max))
            own.link(ve.reciprocal(route[:, 7, :], route[:, 6, :]))
            own.link(ve.scalar_tensor_tensor(route[:, 8, :], route[:, 7, :], float(CAPACITY), route[:, 2, :],
                                             ALU.mult, ALU.mult))
            own.link(ve.tensor_reduce(route_s[:, 3:4], route[:, 8, :], AX.X, ALU.max))
            ve.tensor_scalar(route[:, 4, :], route[:, 8, :], route_s[:, 3:4], None, ALU.subtract
                             ).then_inc(scaled_logits, 1)
            ve.wait_ge(r_exp, 2)
            own.link(ve.tensor_reduce(route_s[:, 4:5], route[:, 5, :], AX.X, ALU.add))
            own.link(ve.reciprocal(route_s[:, 5:6], route_s[:, 4:5]))
            own.link(ve.tensor_scalar(route[:, 9, :], route[:, 5, :], route_s[:, 5:6], None, ALU.mult))
            for j in range(2):
                w = route[:, 9, :]
                own.link(ve.tensor_reduce(route_s[:, 6 + j:7 + j], w, AX.X, ALU.max))
                own.link(ve.scalar_tensor_tensor(route[:, 13, :], w, route_s[:, 6 + j:7 + j], rank[:, :],
                                                 ALU.is_equal, ALU.mult))
                own.link(ve.tensor_reduce(route_s[:, 12 + j:13 + j], route[:, 13, :], AX.X, ALU.max))
                own.link(ve.tensor_scalar(route[:, 10 + j, :], rank[:, :], route_s[:, 12 + j:13 + j], None,
                                          ALU.is_equal))
                own.link(ve.tensor_scalar(route_i[:, j:j + 1], route_s[:, 12 + j:13 + j], -1.0, float(E),
                                          ALU.mult, ALU.add))
                if j == 0:
                    own.link(ve.scalar_tensor_tensor(w, route[:, 10, :], -BIG_SHIFT, w, ALU.mult, ALU.add))
            ve.tensor_tensor(route_s[:, 8:9], route_s[:, 7:8], route_s[:, 6:7], ALU.subtract).then_inc(gap_done, 1)
            ve.wait_ge(r_exp, 3)
            own.link(ve.tensor_scalar(route_s[:, 10:11], route_s[:, 9:10], 1.0, None, ALU.add))
            own.link(ve.reciprocal(route_s[:, 10:11], route_s[:, 10:11]))
            own.link(ve.tensor_tensor(route_s[:, 11:12], route_s[:, 9:10], route_s[:, 10:11], ALU.mult))
            own.link(ve.tensor_scalar(route[:, 14, :], route[:, 11, :], route_s[:, 11:12], None, ALU.mult))
            own.link(ve.scalar_tensor_tensor(route[:, 12, :], route[:, 10, :], route_s[:, 10:11], route[:, 14, :],
                                             ALU.mult, ALU.add))
            own.link(ve.tensor_copy(pick_w[:, :, :], route_s[:, 10:12].unsqueeze(1).to_broadcast([B, B, 2])))
            ve.tensor_tensor(pick_w[:, :, :], pick_w[:, :, :], ident[0:B, 0:B].unsqueeze(2).to_broadcast([B, B, 2]),
                             ALU.mult).then_inc(picked, 1)
            ve.wait_ge(spread_mm, 2)
            own.link(ve.tensor_copy(weight_all[:, :, :].rearrange("p n j -> p (n j)"), bank[2][:, 0:2 * B]))
            ve.tensor_copy(dense_t[:, :, :].rearrange("e n t -> e (n t)"), bank[3][0:E, :]).then_inc(spread_done, 1)

            ve.wait_ge(b2_mm, 1)
            ve.tensor_copy(b2_rows.rearrange("p n c -> p (n c)"), bank[1][:, :]).then_inc(b2_rows_done, 1)

            def outputs(q):
                ve.wait_ge(b2_added, q // 2 + 1)
                if q >= 2:
                    ve.wait_ge(res3_done, q - 1)
                ve.wait_ge(down_mm, q + 1)
                y = y_new[:, q % 2, :, :]
                ve.tensor_tensor(y, bank[q % 2][:, :].rearrange("p (t c) -> p t c", c=C),
                                 normed2[:, 4 * q:4 * q + 4, :], ALU.add).then_inc(y_done, 1)
                ve.wait_ge(y_done, q + 1)
                for t in range(4):
                    own(ve.bn_stats(stats[:, 4 * (q % 2) + t, :], y[:, t, :]))
                own.wait()
                for t in range(4):
                    own(ve.bn_aggr(mv[:, 4 * q + t, :], stats[:, 4 * (q % 2) + t, :]))
                own.wait()
                v = mv[:, 4 * q:4 * q + 4, 1]
                ve.tensor_scalar(v, v, LN_EPS, None, ALU.add).then_inc(var3, 1)

            def finish(q):
                y = y_new[:, q % 2, :, :]
                for t in range(4):
                    own(ve.scalar_tensor_tensor(y[:, t, :], y[:, t, :], mv[:, 4 * q + t, 0:1], bias_all[:, 2, :],
                                                ALU.subtract, ALU.mult))
                own.wait()
                ve.wait_ge(rstd3, q + 1)
                for t in range(4):
                    to = res[:, 4 * q + t, :]
                    last = ve.scalar_tensor_tensor(to, y[:, t, :], rstd[:, 4 * q + t:4 * q + t + 1], to,
                                                   ALU.mult, ALU.add)
                last.then_inc(res3_done, 1)

            def scale_w2(n):
                ve.wait_ge(experts_in[n], 96)
                for j in range(2):
                    last = ve.tensor_scalar(w2_sel[:, 2 * n + j, :, :], w2_sel[:, 2 * n + j, :, :],
                                            weight_all[:, n, j:j + 1], None, ALU.mult)
                last.then_inc(w2_scaled, 1)

            ve.wait_ge(beta_added, PAIRS)
            scale_w2(0)
            for q in range(2 * B + 1):
                if q < 2 * B:
                    if q % 2 == 1 and q // 2 + 1 < B:
                        scale_w2(q // 2 + 1)
                    outputs(q)
                if q >= 1:
                    finish(q - 1)


_INS = ['x', 'L0_conv_in_w', 'L0_conv_in_b', 'L0_conv_out_w', 'L0_conv_out_b', 'L0_conv_off_w', 'L0_conv_off_b',
        'L0_conv_mask_w', 'L0_conv_mask_b', 'L0_conv_dw_k', 'L0_conv_bn_g', 'L0_conv_bn_b', 'L0_conv_bn_m',
        'L0_conv_bn_v', 'L1_attn_W', 'L1_ffn_Wr', 'L1_ffn_br', 'L1_ffn_W1', 'L1_ffn_b1', 'L1_ffn_W2', 'L1_ffn_b2',
        'L1_ffn_gamma', 'L1_ffn_beta']
_OUTS = [((B, H, W, C), 'float32')]


def kernel(**inputs):
    import numpy as _np
    import concourse.bacc as _bacc
    from concourse import mybir as _mybir
    from concourse.bass_utils import run_bass_kernel_spmd as _run

    nc = _bacc.Bacc("TRN2", target_bir_lowering=False, num_devices=1)
    arrays, args = {}, []
    for name in _INS:
        a = _np.ascontiguousarray(inputs[name])
        arrays[f"in_{name}_dram"] = a
        args.append(nc.dram_tensor(f"in_{name}_dram", a.shape, _mybir.dt.from_np(a.dtype), kind="ExternalInput").ap())
    for i, (shape, dtype) in enumerate(_OUTS):
        dt = _mybir.dt.from_np(_np.dtype(dtype))
        args.append(nc.dram_tensor(f"out_{i}_dram", shape, dt, kind="ExternalOutput").ap())
    hybrid_block_kernel(nc, *args)
    r = _run(nc, [arrays], core_ids=[0])
    got = tuple(r.results[0][f"out_{i}_dram"] for i in range(len(_OUTS)))
    return got[0]
```
